# Optimizing a Trainium2 kernel written in Bass

```python
import numpy as np
import jax
import jax.numpy as jnp

def _softmax(x, axis=-1):
    return jax.nn.softmax(x, axis=axis)

def _gelu(x):
    return jax.nn.gelu(x, approximate=True)

def _silu(x):
    return jax.nn.silu(x)

def _sigmoid(x):
    return jax.nn.sigmoid(x)

def _layernorm(x, axis=-1, eps=1e-05):
    m = jnp.mean(x, axis=axis, keepdims=True)
    v = jnp.var(x, axis=axis, keepdims=True)
    return (x - m) / jnp.sqrt(v + eps)

def _scatter_add(tgt, idx, src, axis=0):
    return tgt.at[idx].add(src)

def _segment_sum(src, seg, n):
    return jax.ops.segment_sum(src, seg, n)
kernel_name = 'mk_xattn_ffn_d1_seqx_r4_01846d'

def setup_inputs(seed: int=0):
    np.random.seed(seed)
    _w = jnp.asarray

    def _rec_inputs():
        import jax
        import jax.numpy as jnp
        _rk = jax.random.key(seed)
        x = -0.0002928 + 1 * jax.random.normal(jax.random.fold_in(_rk, 1), (8, 512, 256), jnp.float32)
        _lenS = 512 - jax.random.randint(jax.random.fold_in(_rk, 7), (8,), 0, max(1, 512 // 4) + 1, jnp.int32)
        _lenS2 = 512 - jax.random.randint(jax.random.fold_in(_rk, 8), (8,), 0, max(1, 512 // 4) + 1, jnp.int32)
        _ctx_1024P = jax.random.normal(jax.random.fold_in(_rk, 11), (8, 16, 256), jnp.float32)
        _ctx_1024c = jax.random.dirichlet(jax.random.fold_in(_rk, 511), 0.3 * jnp.ones((16,), jnp.float32), (8, 512))
        _ctx_1024t = jnp.einsum('bsk,bkd->bsd', _ctx_1024c, _ctx_1024P)
        _ctx_1024t = _ctx_1024t * jax.lax.rsqrt(jnp.mean(jnp.square(_ctx_1024t)) + 1e-12) * 0.953939
        ctx_1024 = -1.39393e-06 + 0.999914 * (_ctx_1024t + 0.3 * jax.random.normal(jax.random.fold_in(_rk, 611), (8, 512, 256), jnp.float32))
        return (x, ctx_1024)
    x, ctx_1024 = _rec_inputs()

    def _L0_xattn_setup():
        import jax, jax.numpy as jnp
        import numpy as np
        B, S, D, NH = (2, 512, 256, 8)
        DH = D // NH
        EPS = 1e-06
        LN_EPS = 1e-05

        def _mlstm_cell(q, k, v, igate_w, igate_b, fgate_w, fgate_b, ln_scale):
            Slen = q.shape[0]
            ifg = jnp.concatenate([q, k, v], axis=-1)
            ig = (ifg @ igate_w.T + igate_b).T
            fg = (ifg @ fgate_w.T + fgate_b).T
            qh = q.reshape(Slen, NH, DH).transpose(1, 0, 2)
            kh = k.reshape(Slen, NH, DH).transpose(1, 0, 2)
            vh = v.reshape(Slen, NH, DH).transpose(1, 0, 2)
            log_f = jax.nn.log_sigmoid(fg)
            cs = jnp.cumsum(log_f, axis=1)
            fg_mat = cs[:, :, None] - cs[:, None, :]
            mask = jnp.tril(jnp.ones((Slen, Slen), dtype=bool))
            log_fg_mat = jnp.where(mask, fg_mat, -jnp.inf)
            log_D = log_fg_mat + ig[:, None, :]
            max_log_D = jnp.max(log_D, axis=-1, keepdims=True)
            D_mat = jnp.exp(log_D - max_log_D)
            qk = jnp.einsum('hsd,htd->hst', qh, kh) / np.sqrt(DH)
            C = qk * D_mat
            normalizer = jnp.maximum(jnp.abs(C.sum(axis=-1, keepdims=True)), jnp.exp(-max_log_D))
            h = jnp.einsum('hst,htd->hsd', C / (normalizer + EPS), vh)
            h = h.transpose(1, 0, 2).reshape(Slen, D)
            mu = h.mean(axis=-1, keepdims=True)
            var = h.var(axis=-1, keepdims=True)
            return (h - mu) / jnp.sqrt(var + LN_EPS) * ln_scale
        key = jax.random.key(seed)
        ks = jax.random.split(key, 8)
        rnd = lambda k, sh, s=1.0: jax.random.normal(k, sh, dtype=jnp.float32) * s
        return {'q': rnd(ks[0], (B, S, D)), 'k': rnd(ks[1], (B, S, D)), 'v': rnd(ks[2], (B, S, D)), 'igate_w': rnd(ks[3], (NH, 3 * D), 0.02), 'igate_b': jnp.linspace(3.0, 6.0, NH, dtype=jnp.float32), 'fgate_w': rnd(ks[4], (NH, 3 * D), 0.02), 'fgate_b': rnd(ks[5], (NH,), 0.3162278), 'ln_scale': jnp.ones((D,), dtype=jnp.float32)}
    _L0_xattn_all = _L0_xattn_setup()
    _L0_xattn_in = {k: v for k, v in _L0_xattn_all.items() if k in ('igate_w', 'igate_b', 'fgate_w', 'fgate_b', 'ln_scale')}
    del _L0_xattn_all

    def _L0_ffn_setup():
        import jax, jax.numpy as jnp
        import numpy as np
        B, T, C = (2, 256, 256)
        H = 1024
        E_R, E_S, K = (8, 2, 2)

        def _rmsnorm(x, g):
            eps = jnp.finfo(x.dtype).eps
            return x * jax.lax.rsqrt(jnp.mean(x * x, axis=-1, keepdims=True) + eps) * g

        def _experts_mlp(x, g, W1, b1, W2, b2):
            xn = _rmsnorm(x, g)
            h = jnp.einsum('btc,ech->bteh', xn, W1) + b1
            h = jax.nn.gelu(h, approximate=False)
            return jnp.einsum('bteh,ehc->btec', h, W2) + b2
        key = jax.random.key(seed)
        ks = jax.random.split(key, 12)
        s = 0.02
        return {'u': jax.random.normal(ks[0], (B, T, C), dtype=jnp.float32), 'g_shared': jnp.ones((C,), jnp.float32), 'W1_s': jax.random.normal(ks[1], (E_S, C, H), jnp.float32) * s, 'b1_s': jax.random.normal(ks[2], (E_S, H), jnp.float32) * s, 'W2_s': jax.random.normal(ks[3], (E_S, H, C), jnp.float32) * s, 'b2_s': jax.random.normal(ks[4], (E_S, C), jnp.float32) * s, 'g_routed': jnp.ones((C,), jnp.float32), 'W1_r': jax.random.normal(ks[5], (E_R, C, H), jnp.float32) * s, 'b1_r': jax.random.normal(ks[6], (E_R, H), jnp.float32) * s, 'W2_r': jax.random.normal(ks[7], (E_R, H, C), jnp.float32) * s, 'b2_r': jax.random.normal(ks[8], (E_R, C), jnp.float32) * s, 'centroids': jax.random.normal(ks[9], (C, E_R), jnp.float32) * s}
    _L0_ffn_all = _L0_ffn_setup()
    _L0_ffn_in = {k: v for k, v in _L0_ffn_all.items() if k in ('g_shared', 'W1_s', 'b1_s', 'W2_s', 'b2_s', 'g_routed', 'W1_r', 'b1_r', 'W2_r', 'b2_r', 'centroids')}
    del _L0_ffn_all
    return {'x': x, 'ctx_1024': ctx_1024, 'L0_xattn_igate_w': _L0_xattn_in['igate_w'], 'L0_xattn_igate_b': _L0_xattn_in['igate_b'], 'L0_xattn_fgate_w': _L0_xattn_in['fgate_w'], 'L0_xattn_fgate_b': _L0_xattn_in['fgate_b'], 'L0_xattn_ln_scale': _L0_xattn_in['ln_scale'], 'L0_ffn_g_shared': _L0_ffn_in['g_shared'], 'L0_ffn_W1_s': _L0_ffn_in['W1_s'], 'L0_ffn_b1_s': _L0_ffn_in['b1_s'], 'L0_ffn_W2_s': _L0_ffn_in['W2_s'], 'L0_ffn_b2_s': _L0_ffn_in['b2_s'], 'L0_ffn_g_routed': _L0_ffn_in['g_routed'], 'L0_ffn_W1_r': _L0_ffn_in['W1_r'], 'L0_ffn_b1_r': _L0_ffn_in['b1_r'], 'L0_ffn_W2_r': _L0_ffn_in['W2_r'], 'L0_ffn_b2_r': _L0_ffn_in['b2_r'], 'L0_ffn_centroids': _L0_ffn_in['centroids']}

def reference(x, ctx_1024, L0_xattn_igate_w, L0_xattn_igate_b, L0_xattn_fgate_w, L0_xattn_fgate_b, L0_xattn_ln_scale, L0_ffn_g_shared, L0_ffn_W1_s, L0_ffn_b1_s, L0_ffn_W2_s, L0_ffn_b2_s, L0_ffn_g_routed, L0_ffn_W1_r, L0_ffn_b1_r, L0_ffn_W2_r, L0_ffn_b2_r, L0_ffn_centroids):
    import jax
    import jax.numpy as jnp

    def _L0_xattn_ref(q, k, v, igate_w, igate_b, fgate_w, fgate_b, ln_scale):
        import jax, jax.numpy as jnp
        import numpy as np
        B, S, D, NH = (2, 512, 256, 8)
        DH = D // NH
        EPS = 1e-06
        LN_EPS = 1e-05

        def _mlstm_cell(q, k, v, igate_w, igate_b, fgate_w, fgate_b, ln_scale):
            Slen = q.shape[0]
            ifg = jnp.concatenate([q, k, v], axis=-1)
            ig = (ifg @ igate_w.T + igate_b).T
            fg = (ifg @ fgate_w.T + fgate_b).T
            qh = q.reshape(Slen, NH, DH).transpose(1, 0, 2)
            kh = k.reshape(Slen, NH, DH).transpose(1, 0, 2)
            vh = v.reshape(Slen, NH, DH).transpose(1, 0, 2)
            log_f = jax.nn.log_sigmoid(fg)
            cs = jnp.cumsum(log_f, axis=1)
            fg_mat = cs[:, :, None] - cs[:, None, :]
            mask = jnp.tril(jnp.ones((Slen, Slen), dtype=bool))
            log_fg_mat = jnp.where(mask, fg_mat, -jnp.inf)
            log_D = log_fg_mat + ig[:, None, :]
            max_log_D = jnp.max(log_D, axis=-1, keepdims=True)
            D_mat = jnp.exp(log_D - max_log_D)
            qk = jnp.einsum('hsd,htd->hst', qh, kh) / np.sqrt(DH)
            C = qk * D_mat
            normalizer = jnp.maximum(jnp.abs(C.sum(axis=-1, keepdims=True)), jnp.exp(-max_log_D))
            h = jnp.einsum('hst,htd->hsd', C / (normalizer + EPS), vh)
            h = h.transpose(1, 0, 2).reshape(Slen, D)
            mu = h.mean(axis=-1, keepdims=True)
            var = h.var(axis=-1, keepdims=True)
            return (h - mu) / jnp.sqrt(var + LN_EPS) * ln_scale
        return jax.vmap(lambda qq, kk, vv: _mlstm_cell(qq, kk, vv, igate_w, igate_b, fgate_w, fgate_b, ln_scale))(q, k, v)

    def _L0_ffn_ref(u, g_shared, W1_s, b1_s, W2_s, b2_s, g_routed, W1_r, b1_r, W2_r, b2_r, centroids):
        import jax, jax.numpy as jnp
        import numpy as np
        B, T, C = (2, 256, 256)
        H = 1024
        E_R, E_S, K = (8, 2, 2)

        def _rmsnorm(x, g):
            eps = jnp.finfo(x.dtype).eps
            return x * jax.lax.rsqrt(jnp.mean(x * x, axis=-1, keepdims=True) + eps) * g

        def _experts_mlp(x, g, W1, b1, W2, b2):
            xn = _rmsnorm(x, g)
            h = jnp.einsum('btc,ech->bteh', xn, W1) + b1
            h = jax.nn.gelu(h, approximate=False)
            return jnp.einsum('bteh,ehc->btec', h, W2) + b2
        h_s = _experts_mlp(u, g_shared, W1_s, b1_s, W2_s, b2_s).sum(axis=-2)
        scores = jax.nn.sigmoid(u @ centroids)
        gpk, i_topk = jax.lax.top_k(scores, K)
        gk = gpk / scores.sum(axis=-1, keepdims=True)
        routed_all = _experts_mlp(u, g_routed, W1_r, b1_r, W2_r, b2_r)
        routed_topk = jnp.take_along_axis(routed_all, i_topk[..., None], axis=2)
        h_r = (gk[..., None] * routed_topk).sum(axis=-2)
        return u + h_s + h_r
    x = x + _L0_xattn_ref(_layernorm(x, axis=-1), ctx_1024, ctx_1024, L0_xattn_igate_w, L0_xattn_igate_b, L0_xattn_fgate_w, L0_xattn_fgate_b, L0_xattn_ln_scale)
    x = x + _L0_ffn_ref(_layernorm(x, axis=-1), L0_ffn_g_shared, L0_ffn_W1_s, L0_ffn_b1_s, L0_ffn_W2_s, L0_ffn_b2_s, L0_ffn_g_routed, L0_ffn_W1_r, L0_ffn_b1_r, L0_ffn_W2_r, L0_ffn_b2_r, L0_ffn_centroids)
    return x

_drawn_inputs = setup_inputs


def setup_inputs(seed=0):
    import zlib

    import numpy as np

    out = dict(_drawn_inputs(seed))
    spreads = {'L0_xattn_ln_scale': (1.0, 0.2),
     'L0_ffn_g_shared': (1.0, 0.6),
     'L0_ffn_g_routed': (1.0, 0.6)}
    factors = {'L0_ffn_b1_s': 8.0,
     'L0_ffn_b2_s': 5.764,
     'L0_ffn_W1_r': 6.353,
     'L0_ffn_b1_r': 8.0,
     'L0_ffn_W2_r': 6.178,
     'L0_ffn_b2_r': 30.548,
     'L0_ffn_centroids': 7.017}
    for name, (base, spread) in spreads.items():
        noise = np.random.default_rng([zlib.crc32(name.encode()), seed]).standard_normal(out[name].shape)
        drawn = base * np.exp(spread * noise) if base else spread * noise
        out[name] = jnp.asarray(drawn.astype(out[name].dtype))
    for name, factor in factors.items():
        out[name] = (out[name] * factor).astype(out[name].dtype)
    return out
```

```python
import concourse.bass as bass
from concourse import mybir
from contextlib import ExitStack

fp32 = mybir.dt.float32
bf16 = mybir.dt.bfloat16
i32 = mybir.dt.int32
ALU = mybir.AluOpType
ACT = mybir.ActivationFunctionType
AX = mybir.AxisListType

P = 128
LN_EPS = 1e-5
RMS_EPS = 1.1920928955078125e-07
NORM_EPS = 1e-6
MASKED = -1.0e30


def xattn_moe_kernel(nc, x, ctxt, ig_w, ig_b, fg_w, fg_b, ln_scale, g_s, W1_s, b1_s, W2_s, b2_s,
                     g_r, W1_r, b1_r, W2_r, b2_r, centroids, out):
    B, S, D = x.shape
    NH = ig_w.shape[0]
    DH = D // NH
    J = S // P
    KD = D // P
    HG = NH // KD
    NS, _, HID = W1_s.shape
    NE = W1_r.shape[0]
    M = HID // P
    VW = DH + 1
    HW = HG * VW
    PW = 3 * VW
    VPAD = 2
    C = B * J
    T = 512
    TJ = T // P
    TOPK = 2
    NT = (B * S * TOPK + NE * (T - 1)) // T
    NL = B * S // T
    SCALE = float(DH) ** -0.5
    IG, FG, TR = 0, 32, 64

    xs_dram = nc.dram_tensor("sorted_tokens", [NT * T, D], fp32).ap()
    ys_dram = nc.dram_tensor("sorted_outputs", [NT * T, D], fp32).ap()
    un_dram = nc.dram_tensor("normed_tokens", [B * S, D], fp32).ap()
    base_dram = nc.dram_tensor("residual_and_shared", [B * S, D], fp32).ap()

    x_v = x.rearrange("b (j p) d -> b p j d", p=P)
    c_v = ctxt.rearrange("b (j p) d -> b p j d", p=P)
    un_v = un_dram.rearrange("(b j p) d -> b p j d", p=P, j=J)
    base_v = base_dram.rearrange("(b j p) d -> b p j d", p=P, j=J)
    un_c = un_dram.rearrange("(c p) d -> c p d", p=P)
    base_c = base_dram.rearrange("(c p) d -> c p d", p=P)
    out_c = out.rearrange("b (j p) d -> (b j) p d", p=P)
    xs_v = xs_dram.rearrange("(n j p) d -> n p j d", p=P, j=TJ)
    ys_v = ys_dram.rearrange("(n j p) d -> n p j d", p=P, j=TJ)

    whole = ExitStack()
    with whole:
        def sb(stack, name, shape, dt=fp32):
            return stack.enter_context(nc.sbuf_tensor(name, shape, dt))

        def sem(name):
            return whole.enter_context(nc.semaphore(name))

        psum = [whole.enter_context(nc.psum_tensor(f"bank{i}", [P, 512], fp32)) for i in range(8)]

        ident = sb(whole, "ident", [P, P])
        logits = sb(whole, "logits", [P, C, NE])
        slots = sb(whole, "slots", [P, TOPK, C], i32)
        gates = sb(whole, "gates", [P, TOPK, C])
        tile_expert = sb(whole, "tile_expert", [P, NT], i32)
        zeros = sb(whole, "zeros", [P, D])

        stage_a = ExitStack()
        A = lambda name, shape, dt=fp32: sb(stage_a, name, shape, dt)
        identb = A("identb", [P, P], bf16)
        causal = A("causal", [P, P], bf16)
        gate_w = A("gate_w", [P, 2 * KD, 40])
        ig_bias = A("ig_bias", [NH, 1])
        fg_bias = A("fg_bias", [40, 1])
        negsel = A("negsel", [NH, NH])
        headmask = A("headmask", [P, HG])
        blockmask = A("blockmask", [P, HG, VW])
        lnsc = A("lnsc", [P, D])
        gs_col = A("gs_col", [P, KD])
        cent = A("cent", [P, KD, NE])
        w1s = A("w1s", [P, NS, KD, HID])
        w2s = A("w2s", [P, NS, M, D])
        b1s = A("b1s", [P, NS, M])
        b2s2 = A("b2s2", [P, NS, D])
        b2s = A("b2s", [P, D])
        eps = A("eps", [P, 2])
        exp_rhs = A("exp_rhs", [40, J, NH, P])
        exp_lhs = A("exp_lhs", [40, S])
        rows = A("rows", [72, S])
        frow = A("frow", [40, 5, S])
        cs = A("cs", [NH, S])
        zrow = A("zrow", [40, S])
        vaug = A("vaug", [P, J, NH + VPAD, VW])
        xb = A("xb", [P, J, D])
        cb = A("cb", [P, J, D])
        qn = A("qn", [P, J, D])
        qcT = A("qcT", [P, 2 * KD, S])
        qmask = A("qmask", [P, KD, HG, S])
        bn6 = A("bn6", [P, J, 6])
        mv = A("mv", [P, J, 2])
        nw = A("nw", [P, 5, J])
        cols = A("cols", [P, 3 * P])
        earg = A("earg", [P, P])
        eexp = A("eexp", [P, P])
        NPAIR = J * (J - 1) // 2
        wv = A("wv", [P, NPAIR, NH, VW])
        state = A("state", [P, KD, J - 1, HW])
        decay = A("decay", [P, NH, P])
        ct = A("ct", [P, NH, P])
        hn = A("hn", [P, J, NH, VW])
        rnorm = A("rnorm", [P, 3, J * NH])
        hh = A("hh", [P, J, D])
        x1 = A("x1", [P, J, D])
        un = A("un", [P, J, D])
        base = A("base", [P, J, D])
        junk = A("junk", [P, D])
        unT = A("unT", [P, KD, S])
        xs = A("xs", [P, KD, S])
        hT = A("hT", [P, 2, M, S])

        gw_nat = hT[0:40, 0, 0:2, :].rearrange("p a s -> p (a s)")[:, 0:3 * D]

        s_load = sem("s_load")
        s_const = sem("s_const")
        s_cpre = sem("s_cpre")
        s_gwT = sem("s_gwT")

        with nc.Block() as block:
            @block.sync
            def _(sp):
                sp.wait_ge(s_cpre, 1)
                loads = [
                    (gw_nat[IG:IG + NH, :], ig_w), (gw_nat[FG:FG + NH, :], fg_w),
                    (ig_bias[:, :], ig_b.rearrange("(h o) -> h o", o=1)),
                    (fg_bias[FG:FG + NH, :], fg_b.rearrange("(h o) -> h o", o=1)),
                    (lnsc[:, :], ln_scale.rearrange("(o d) -> o d", o=1).to_broadcast([P, D])),
                    (cent[:, :, :], centroids.rearrange("(k p) e -> p k e", p=P)),
                    (w1s[:, :, :, :], W1_s.rearrange("e (k p) h -> p e k h", p=P)),
                    (w2s[:, :, :, :], W2_s.rearrange("e (m p) d -> p e m d", p=P)),
                    (b2s2[:, :, :], b2_s.rearrange("(o e) d -> o e d", o=1).to_broadcast([P, NS, D])),
                ]
                with nc.allow_non_contiguous_dma(reason="small transposed vectors"):
                    for n, (dst, src) in enumerate(loads):
                        sp.dma_start(dst, src).then_inc(s_load, 16)
                    sp.dma_start(gs_col[:, :], g_s.rearrange("(k p) -> p k", p=P)).then_inc(s_load, 16)
                    for e in range(NS):
                        sp.dma_start(b1s[:, e, :], b1_s[e, :].rearrange("(m p) -> p m", p=P)).then_inc(s_load, 16)
                sp.wait_ge(s_load, 16 * (len(loads) + 1 + NS))

            @block.gpsimd
            def _(pool):
                nc.gpsimd.memset(ident[:, :], 0.0)
                nc.gpsimd.memset(negsel[:, :], 0.0)
                nc.gpsimd.memset(causal[:, :], 0.0)
                nc.gpsimd.memset(headmask[:, :], 1.0)
                nc.gpsimd.memset(exp_lhs[:, :], 0.0)
                nc.gpsimd.memset(rows[:, :], 0.0)
                nc.gpsimd.memset(blockmask[:, :, :], SCALE)
                nc.gpsimd.memset(exp_rhs[:, :, :, :], 0.0)
                nc.gpsimd.memset(vaug[:, :, :, :], 1.0)
                nc.gpsimd.memset(zrow[:, :], 0.0)
                nc.gpsimd.memset(eps[:, 0:1], LN_EPS)
                nc.gpsimd.memset(eps[:, 1:2], RMS_EPS).then_inc(s_const, 1)
                pool.wait_ge(s_const, 1)
                nc.gpsimd.affine_select(out=ident[:, :], in_=ident[:, :], compare_op=ALU.not_equal, fill=1.0,
                                        base=0, pattern=[[-1, P]], channel_multiplier=1)
                nc.gpsimd.affine_select(out=negsel[:, :], in_=negsel[:, :], compare_op=ALU.not_equal, fill=-1.0,
                                        base=0, pattern=[[-1, NH]], channel_multiplier=1)
                nc.gpsimd.affine_select(out=causal[:, :], in_=causal[:, :], compare_op=ALU.is_ge, fill=MASKED,
                                        base=0, pattern=[[1, P]], channel_multiplier=-1)
                nc.gpsimd.affine_select(out=headmask[:, :], in_=headmask[:, :], compare_op=ALU.is_ge, fill=0.0,
                                        base=0, pattern=[[-DH, HG]], channel_multiplier=1)
                nc.gpsimd.affine_select(out=blockmask[:, :, :], in_=blockmask[:, :, :], compare_op=ALU.is_ge,
                                        fill=0.0, base=0, pattern=[[-DH, HG], [0, VW]], channel_multiplier=1)
                nc.gpsimd.memset(exp_lhs[0:NH, :], 1.0).then_inc(s_const, 1)
                pool.wait_ge(s_const, 2)
                nc.gpsimd.affine_select(out=headmask[:, :], in_=headmask[:, :], compare_op=ALU.is_ge, fill=0.0,
                                        base=DH - 1, pattern=[[DH, HG]], channel_multiplier=-1)
                nc.gpsimd.affine_select(out=blockmask[:, :, :], in_=blockmask[:, :, :], compare_op=ALU.is_ge,
                                        fill=0.0, base=DH - 1, pattern=[[DH, HG], [0, VW]], channel_multiplier=-1)
                for j in range(J):
                    nc.gpsimd.affine_select(out=exp_rhs[:, j, :, :], in_=exp_rhs[:, j, :, :],
                                            compare_op=ALU.not_equal, fill=1.0, base=FG,
                                            pattern=[[1, NH], [0, P]], channel_multiplier=-1)
                nc.gpsimd.tensor_copy(identb[:, :], ident[:, :]).then_inc(s_const, 1)

            @block.vector
            def _(dve):
                nc.vector.memset(gw_nat, 0.0).then_inc(s_cpre, 1)
                nc.vector.memset(zeros[:, :], 0.0)
                dve.wait_ge(s_load, 16 * 12)
                nc.vector.tensor_tensor(b2s[:, :], b2s2[:, 0, :], b2s2[:, 1, :], ALU.add)
                dve.wait_ge(s_gwT, 1)
                pv = psum[0][:, 0:6 * 40].rearrange("p (n g) -> p n g", g=40)
                nc.vector.tensor_copy(gate_w[:, :, :], pv[:, 0:2 * KD, :]).then_inc(s_cpre, 1)
                dve.wait_ge(s_cpre, 2)
                nc.vector.tensor_tensor(gate_w[:, KD:2 * KD, :], gate_w[:, KD:2 * KD, :], pv[:, 2 * KD:3 * KD, :],
                                        ALU.add).then_inc(s_cpre, 1)

            @block.tensor
            def _(pe):
                pe.wait_ge(s_load, 16 * 12)
                pe.wait_ge(s_const, 3)
                for n in range(3 * KD):
                    last = nc.tensor.transpose(psum[0][:, n * 40:(n + 1) * 40], gw_nat[:, n * P:(n + 1) * P],
                                               ident[0:40, 0:40])
                last.then_inc(s_gwT, 1)

        s_x, s_c = sem("s_x"), sem("s_c")
        s_un_out, s_base_out = sem("s_un_out"), sem("s_base_out")
        xc_free = sem("xc_free")
        stats = sem("stats")
        rsq = sem("rsq")
        act = sem("act")
        chain = sem("chain")
        q_ready, tr_done, qcT_ready, qmask_ready = sem("q_ready"), sem("tr_done"), sem("qcT_ready"), sem("qmask_ready")
        gates_done, logsig_ready, rows_ready, lhs_ready = sem("gates_done"), sem("logsig_ready"), sem("rows_ready"), sem("lhs_ready")
        rhs_ready, cols_done, earg_ready, eexp_ready = sem("rhs_ready"), sem("cols_done"), sem("earg_ready"), sem("eexp_ready")
        vaug_ready, wv_ready, state_done, state_ready = sem("vaug_ready"), sem("wv_ready"), sem("state_done"), sem("state_ready")
        exp_done, score_done, decay_ready, ct_ready = sem("exp_done"), sem("score_done"), sem("decay_ready"), sem("ct_ready")
        inter_done, pv_done, hn_ready = sem("inter_done"), sem("pv_done"), sem("hn_ready")
        x1_ready, u_ready, un_ready = sem("x1_ready"), sem("u_ready"), sem("un_ready")
        unT_done, unT_ready, xs_ready, logit_done = sem("unT_done"), sem("unT_ready"), sem("xs_ready"), sem("logit_done")
        logit_read = sem("logit_read")
        up_done, gelu_done, down_done, base_ready = sem("up_done"), sem("gelu_done"), sem("down_done"), sem("base_ready")

        passed = sem("passed")

        def wait_apart(engine, semaphore, value):
            engine.wait_ge(semaphore, value)
            engine.sem_inc(passed, 1)

        class Steps:
            def __init__(self, engine, semaphore, i, n):
                self.engine, self.semaphore, self.first, self.n, self.k = engine, semaphore, i * n, n, 0

            def done(self, instruction, alone=False):
                self.k += 1
                instruction.then_inc(self.semaphore, 1)
                (wait_apart if alone else type(self.engine).wait_ge)(self.engine, self.semaphore, self.first + self.k)

            def end(self):
                assert self.k == self.n, self.k

        with nc.Block() as block:
            @block.sync
            def _(sp):
                with sp.Fori(0, B) as b:
                    wait_apart(sp, xc_free, b + 1)
                    sp.dma_start(xb[:, :, :], x_v[bass.ds(b, 1)].rearrange("b p j d -> (b p) j d")).then_inc(s_x, 16)
                    sp.dma_start(cb[:, :, :], c_v[bass.ds(b, 1)].rearrange("b p j d -> (b p) j d")).then_inc(s_c, 16)
                    wait_apart(sp, un_ready, b + 1)
                    sp.dma_start(un_v[bass.ds(b, 1)].rearrange("b p j d -> (b p) j d"), un[:, :, :]).then_inc(s_un_out, 16)
                    wait_apart(sp, base_ready, b + 1)
                    sp.dma_start(base_v[bass.ds(b, 1)].rearrange("b p j d -> (b p) j d"), base[:, :, :]).then_inc(s_base_out, 16)
                    sp.wait_ge(s_un_out, 16 * b + 16)
                    wait_apart(sp, s_base_out, 16 * b + 16)

            @block.gpsimd
            def _(pool):
                with pool.Fori(0, B) as b:
                    pool.wait_ge(s_c, 16 * b + 16)
                    wait_apart(pool, xc_free, b + 1)
                    nc.gpsimd.tensor_copy(vaug[:, :, 0:NH, 0:DH], cb[:, :, :].rearrange("p j (h e) -> p j h e", e=DH)
                                          ).then_inc(vaug_ready, 1)
                    wait_apart(pool, qcT_ready, J * b + J)
                    for g in range(KD):
                        for r in range(HG):
                            last = nc.gpsimd.tensor_scalar(qmask[:, g, r, :], qcT[:, g, :], headmask[:, r:r + 1], None,
                                                           ALU.mult)
                    last.then_inc(qmask_ready, 1)
                    pool.wait_ge(rows_ready, b + 1)
                    for j in range(J):
                        last = nc.gpsimd.tensor_tensor(
                            exp_rhs[0:NH, j, :, :], negsel[:, :].unsqueeze(2).to_broadcast([NH, NH, P]),
                            rows[0:NH, j * P:(j + 1) * P].unsqueeze(1).to_broadcast([NH, NH, P]), ALU.mult)
                    last.then_inc(rhs_ready, 1)
                    pool.wait_ge(eexp_ready, b + 1)
                    n = 0
                    for j in range(J - 1):
                        for i in range(j + 1):
                            w = eexp[:, (i * (J - 1) + j) * NH:(i * (J - 1) + j + 1) * NH]
                            last = nc.gpsimd.tensor_tensor(wv[:, n, :, :], vaug[:, i, 0:NH, :],
                                                           w.unsqueeze(2).to_broadcast([P, NH, VW]), ALU.mult)
                            n += 1
                    last.then_inc(wv_ready, 1)

            @block.scalar
            def _(sc):
                with sc.Fori(0, B) as b:
                    own = Steps(sc, act, b, 12)

                    def rsqrt(k, src, col, scale):
                        sc.wait_ge(stats, 3 * b + k + 1)
                        own.done(nc.scalar.activation(nw[:, 1, :], src, ACT.Ln, bias=eps[:, col:col + 1], scale=scale))
                        nc.scalar.activation(nw[:, 0, :], nw[:, 1, :], ACT.Exp, scale=-0.5).then_inc(rsq, 1)

                    rsqrt(0, mv[:, :, 1], 0, 1.0)
                    for j in range(J):
                        sc.wait_ge(tr_done, J * b + j + 1)
                        nc.scalar.copy(qcT[:, :, j * P:(j + 1) * P],
                                       psum[2 + j][:, :].rearrange("p (k s) -> p k s", s=P)).then_inc(qcT_ready, 1)
                    sc.wait_ge(gates_done, b + 1)
                    own.done(nc.scalar.activation(frow[FG:FG + NH, 0, :], psum[6][FG:FG + NH, :], ACT.Abs,
                                                  bias=fg_bias[FG:FG + NH, :]))
                    own.done(nc.scalar.activation(frow[FG:FG + NH, 1, :], frow[FG:FG + NH, 0, :], ACT.Exp, scale=-1.0))
                    nc.scalar.activation(frow[FG:FG + NH, 2, :], frow[FG:FG + NH, 1, :], ACT.Ln, bias=1.0
                                         ).then_inc(logsig_ready, 1)
                    sc.wait_ge(rows_ready, b + 1)
                    nc.scalar.copy(exp_lhs[FG:FG + NH, :], rows[FG:FG + NH, :]).then_inc(lhs_ready, 1)
                    sc.wait_ge(earg_ready, b + 1)
                    nc.scalar.activation(eexp[:, :], earg[:, :], ACT.Exp).then_inc(eexp_ready, 1)
                    for j in range(J):
                        sc.wait_ge(exp_done, J * b + j + 1)
                        if j > 0:
                            sc.wait_ge(ct_ready, J * b + j)
                        for g in range(KD):
                            last = nc.scalar.activation(
                                decay[:, g * HG:(g + 1) * HG, :], psum[g][:, :].rearrange("p (h s) -> p h s", s=P),
                                ACT.Exp)
                        last.then_inc(decay_ready, 1)
                    rsqrt(1, mv[:, :, 1], 0, 1.0)
                    rsqrt(2, mv[:, :, 1], 0, 1.0)
                    sc.wait_ge(u_ready, b + 1)
                    for j in range(J):
                        own.done(nc.scalar.activation(junk[:, :], hh[:, j, :], ACT.Square, accum_out=nw[:, 4, j:j + 1]))
                    rsqrt3 = nc.scalar.activation(nw[:, 1, :], nw[:, 4, :], ACT.Ln, bias=eps[:, 1:2], scale=1.0 / D)
                    own.done(rsqrt3)
                    nc.scalar.activation(nw[:, 0, :], nw[:, 1, :], ACT.Exp, scale=-0.5).then_inc(rsq, 1)
                    sc.wait_ge(unT_done, b + 1)
                    for k in range(KD):
                        own_last = nc.scalar.copy(unT[:, k, :], psum[2 + k][:, :])
                        if k == KD - 1:
                            own_last.then_inc(unT_ready, 1)
                    own.done(nc.scalar.copy(junk[:, 0:1], eps[:, 0:1]))
                    own.done(nc.scalar.copy(junk[:, 0:1], eps[:, 0:1]))
                    for e in range(NS):
                        for m in range(M):
                            n = e * M + m
                            sc.wait_ge(up_done, NS * M * b + n + 1)
                            nc.scalar.activation(hT[:, e % 2, m, :], psum[n % 2][:, :], ACT.Gelu,
                                                 bias=b1s[:, e, m:m + 1]).then_inc(gelu_done, 1)
                    own.end()

            @block.vector
            def _(dve):
                nc.vector.memset(junk[:, 0:1], 0.0).then_inc(xc_free, 1)
                with dve.Fori(0, B) as b:
                    own = Steps(dve, chain, b, 39)
                    ts, tt, stt = nc.vector.tensor_scalar, nc.vector.tensor_tensor, nc.vector.scalar_tensor_tensor

                    def moments(src, k):
                        for j in range(J):
                            last = nc.vector.bn_stats(bn6[:, j, :], src[:, j, :])
                        own.done(last, alone=True)
                        for j in range(J):
                            last = nc.vector.bn_aggr(mv[:, j, :], bn6[:, j, :])
                        last.then_inc(stats, 1)
                        dve.wait_ge(stats, 3 * b + k + 1)

                    def refine(k, v, e, scale):
                        own.done(ts(nw[:, 2, :], v, scale, e, ALU.mult, ALU.add))
                        dve.wait_ge(rsq, 4 * b + k + 1)
                        own.done(tt(nw[:, 3, :], nw[:, 0, :], nw[:, 0, :], ALU.mult))
                        own.done(stt(nw[:, 2, :], nw[:, 3, :], -0.5, nw[:, 2, :], ALU.mult, ALU.mult))
                        own.done(stt(nw[:, 3, :], nw[:, 2, :], 1.5, nw[:, 0, :], ALU.add, ALU.mult))

                    def normed(dst, src):
                        for j in range(J):
                            last = ts(dst[:, j, :], src[:, j, :], mv[:, j, 0:1], nw[:, 3, j:j + 1],
                                      ALU.subtract, ALU.mult)
                        return last

                    dve.wait_ge(s_x, 16 * b + 16)
                    moments(xb, 0)
                    refine(0, mv[:, :, 1], LN_EPS, 1.0)
                    normed(qn, xb).then_inc(q_ready, 1)

                    dve.wait_ge(gates_done, b + 1)
                    dve.wait_ge(logsig_ready, b + 1)
                    own.done(ts(frow[FG:FG + NH, 3, :], psum[6][FG:FG + NH, :], fg_bias[FG:FG + NH, :], 0.0,
                                ALU.add, ALU.min))
                    own.done(tt(frow[FG:FG + NH, 4, :], frow[FG:FG + NH, 3, :], frow[FG:FG + NH, 2, :], ALU.subtract))
                    own.done(nc.vector.tensor_tensor_scan(cs[:, :], zrow[FG:FG + NH, :], frow[FG:FG + NH, 4, :], 0.0,
                                                          ALU.add, ALU.add))
                    own.done(stt(rows[FG:FG + NH, :], psum[6][IG:IG + NH, :], ig_bias[:, :], cs[:, :],
                                 ALU.add, ALU.subtract))
                    own.done(nc.vector.tensor_tensor_scan(rows[0:NH, :], rows[FG:FG + NH, :], rows[FG:FG + NH, :],
                                                          -3.0e38, ALU.max, ALU.max))
                    tt(rows[TR:TR + NH, :], cs[:, :], rows[0:NH, :], ALU.add).then_inc(rows_ready, 1)

                    dve.wait_ge(cols_done, b + 1)
                    own.done(nc.vector.tensor_copy(cols[:, 0:J * 72 + (J - 1) * NH], psum[7][:, 0:J * 72 + (J - 1) * NH]))
                    cv = cols[:, 0:J * 72].rearrange("p (j r) -> p j r", r=72)
                    nm = cols[:, J * 72:J * 72 + (J - 1) * NH].rearrange("p (j h) -> p j h", h=NH)
                    NW = (J - 1) * (J - 1) * NH
                    for i in range(J - 1):
                        ev = earg[:, i * (J - 1) * NH:(i + 1) * (J - 1) * NH].rearrange("p (j h) -> p j h", h=NH)
                        last = tt(ev, nm, cv[:, i:i + 1, FG:FG + NH].to_broadcast([P, J - 1, NH]), ALU.add)
                    rv = earg[:, NW:NW + (J - 1) * NH].rearrange("p (j h) -> p j h", h=NH)
                    stt(rv, cv[:, 1:J, 0:NH], -1.0, nm, ALU.mult, ALU.subtract)
                    mvw = earg[:, NW + (J - 1) * NH:NW + (2 * J - 1) * NH].rearrange("p (j h) -> p j h", h=NH)
                    own.done(ts(mvw, cv[:, :, TR:TR + NH], -1.0, None, ALU.mult))
                    ts(earg[:, 0:NW], earg[:, 0:NW], 0.0, None, ALU.min).then_inc(earg_ready, 1)

                    dve.wait_ge(state_done, b + 1)
                    bm = blockmask[:, :, :].rearrange("p h e -> p (h e)").unsqueeze(1).to_broadcast([P, J - 1, HW])
                    for g in range(KD):
                        last = tt(state[:, g, :, :], psum[g][:, 0:(J - 1) * HW].rearrange("p (j c) -> p j c", c=HW), bm,
                                  ALU.mult)
                    last.then_inc(state_ready, 1)
                    dve.wait_ge(eexp_ready, b + 1)
                    for j in range(J):
                        dve.wait_ge(score_done, J * b + j + 1)
                        dve.wait_ge(decay_ready, J * b + j + 1)
                        for g in range(KD):
                            last = stt(ct[:, g * HG:(g + 1) * HG, :],
                                       psum[2 + g][:, :].rearrange("p (h s) -> p h s", s=P), SCALE,
                                       decay[:, g * HG:(g + 1) * HG, :], ALU.mult, ALU.mult)
                        last.then_inc(ct_ready, 1)
                        dve.wait_ge(pv_done, J * b + j + 1)
                        if j > 0:
                            rr = eexp[:, NW + (j - 1) * NH:NW + j * NH].unsqueeze(2).to_broadcast([P, NH, VW])
                            own.done(tt(hn[:, j, :, :], psum[4][:, 0:NH * VW].rearrange("p (h e) -> p h e", e=VW), rr,
                                        ALU.mult))
                        for g in range(KD):
                            pvv = psum[5 + g][:, 0:HG * PW].rearrange("p (h e) -> p h e", e=PW)[:, :, 0:VW]
                            dst = hn[:, j, g * HG:(g + 1) * HG, :]
                            if j > 0:
                                last = tt(dst, dst, pvv, ALU.add)
                            else:
                                last = nc.vector.tensor_copy(dst, pvv)
                        last.then_inc(hn_ready, 1)
                    dve.wait_ge(hn_ready, J * b + J)
                    hv = hn[:, :, :, :].rearrange("p j h e -> p (j h) e")
                    own.done(stt(rnorm[:, 0, :], hv[:, :, DH], -1.0, hv[:, :, DH], ALU.mult, ALU.max))
                    own.done(tt(rnorm[:, 1, :], rnorm[:, 0, :], eexp[:, NW + (J - 1) * NH:NW + (2 * J - 1) * NH], ALU.max))
                    own.done(ts(rnorm[:, 0, :], rnorm[:, 1, :], NORM_EPS, None, ALU.add))
                    own.done(nc.vector.reciprocal(rnorm[:, 2, :], rnorm[:, 0, :]))
                    own.done(tt(hh[:, :, :].rearrange("p j (h e) -> p (j h) e", e=DH), hv[:, :, 0:DH],
                                rnorm[:, 2, :].unsqueeze(2).to_broadcast([P, J * NH, DH]), ALU.mult))
                    moments(hh, 1)
                    refine(1, mv[:, :, 1], LN_EPS, 1.0)
                    own.done(normed(qn, hh))
                    own.done(tt(qn[:, :, :], qn[:, :, :], lnsc[:, :].unsqueeze(1).to_broadcast([P, J, D]), ALU.mult))
                    tt(x1[:, :, :], qn[:, :, :], xb[:, :, :], ALU.add).then_inc(x1_ready, 1)
                    dve.wait_ge(x1_ready, b + 1)
                    nc.vector.memset(junk[:, 0:1], 0.0).then_inc(xc_free, 1)
                    moments(x1, 2)
                    refine(2, mv[:, :, 1], LN_EPS, 1.0)
                    normed(hh, x1).then_inc(u_ready, 1)
                    dve.wait_ge(u_ready, b + 1)
                    own.done(tt(base[:, :, :], x1[:, :, :], hh[:, :, :], ALU.add))
                    dve.wait_ge(rsq, 4 * b + 4)
                    refine(3, nw[:, 4, :], RMS_EPS, 1.0 / D)
                    for j in range(J):
                        last = ts(un[:, j, :], hh[:, j, :], nw[:, 3, j:j + 1], None, ALU.mult)
                    last.then_inc(un_ready, 1)
                    own.done(nc.vector.reciprocal(nw[:, 2, :], nw[:, 3, :]))
                    own.done(tt(base[:, :, :], base[:, :, :], b2s[:, :].unsqueeze(1).to_broadcast([P, J, D]), ALU.add))
                    dve.wait_ge(unT_ready, b + 1)
                    for k in range(KD):
                        last = ts(xs[:, k, :], unT[:, k, :], gs_col[:, k:k + 1], None, ALU.mult)
                    last.then_inc(xs_ready, 1)
                    dve.wait_ge(logit_done, b + 1)
                    tt(logits[:, bass.ds(b * J, J), :], psum[4][:, 0:J * NE].rearrange("p (j e) -> p j e", e=NE),
                       nw[:, 2, :].unsqueeze(2).to_broadcast([P, J, NE]), ALU.mult).then_inc(logit_read, 1)
                    dve.wait_ge(down_done, b + 1)
                    for h in range(2):
                        last = tt(base[:, 2 * h:2 * h + 2, :], base[:, 2 * h:2 * h + 2, :],
                                  psum[6 + h][:, :].rearrange("p (j d) -> p j d", d=D), ALU.add)
                    last.then_inc(base_ready, 1)
                    dve.wait_ge(s_base_out, 16 * b + 16)
                    dve.wait_ge(s_un_out, 16 * b + 16)
                    own.end()

            @block.tensor
            def _(pe):
                with pe.Fori(0, B) as b:
                    mm, tr = nc.tensor.matmul, nc.tensor.transpose
                    pe.wait_ge(q_ready, b + 1)
                    pe.wait_ge(s_c, 16 * b + 16)
                    for j in range(J):
                        for k in range(KD):
                            tr(psum[2 + j][:, k * P:(k + 1) * P], qn[:, j, k * P:(k + 1) * P], ident[:, :])
                        for k in range(KD):
                            last = tr(psum[2 + j][:, (KD + k) * P:(KD + k + 1) * P], cb[:, j, k * P:(k + 1) * P], ident[:, :])
                        last.then_inc(tr_done, 1)
                    pe.wait_ge(qcT_ready, J * b + J)
                    for k in range(2 * KD):
                        last = mm(psum[6][0:40, :], gate_w[:, k, :], qcT[:, k, :], start=k == 0, stop=k == 2 * KD - 1)
                    last.then_inc(gates_done, 1)
                    pe.wait_ge(rows_ready, b + 1)
                    for j in range(J):
                        tr(psum[7][:, j * 72:(j + 1) * 72], rows[:, j * P:(j + 1) * P], ident[0:72, 0:72])
                    pe.wait_ge(rhs_ready, b + 1)
                    mm(psum[7][:, J * 72:J * 72 + (J - 1) * NH], exp_lhs[0:NH, 0:P], exp_rhs[0:NH, 0:J - 1, :, P - 1],
                       start=True, stop=True).then_inc(cols_done, 1)
                    pe.wait_ge(wv_ready, b + 1)
                    for g in range(KD):
                        for j in range(J - 1):
                            for i in range(j + 1):
                                last = mm(psum[g][:, j * HW:(j + 1) * HW], cb[:, i, g * P:(g + 1) * P],
                                          wv[:, j * (j + 1) // 2 + i, g * HG:(g + 1) * HG, :].rearrange("p h e -> p (h e)"),
                                          start=i == 0, stop=i == j)
                    last.then_inc(state_done, 1)
                    pe.wait_ge(state_ready, b + 1)
                    pe.wait_ge(qmask_ready, b + 1)
                    pe.wait_ge(lhs_ready, b + 1)
                    for j in range(J):
                        cj = slice(j * P, (j + 1) * P)
                        if j > 0:
                            pe.wait_ge(decay_ready, J * b + j)
                            pe.wait_ge(hn_ready, J * b + j)
                        for g in range(KD):
                            mm(psum[g][:, :], identb[:, :], causal[:, :].unsqueeze(1).to_broadcast([P, HG, P]),
                               start=True, stop=False)
                            last = mm(psum[g][:, :], exp_lhs[:, cj],
                                      exp_rhs[:, j, g * HG:(g + 1) * HG, :].rearrange("p h s -> p (h s)"),
                                      start=False, stop=True)
                        last.then_inc(exp_done, 1)
                        for g in range(KD):
                            last = mm(psum[2 + g][:, :], qcT[:, KD + g, cj], qmask[:, g, :, cj], start=True, stop=True)
                        last.then_inc(score_done, 1)
                        if j > 0:
                            for g in range(KD):
                                mm(psum[4][:, g * HW:(g + 1) * HW], qcT[:, g, cj], state[:, g, j - 1, :],
                                   start=True, stop=True)
                        pe.wait_ge(ct_ready, J * b + j + 1)
                        vflat = vaug[:, j, :, :].rearrange("p h e -> p (h e)")
                        for h in range(NH):
                            last = mm(psum[5 + h // HG][:, (h % HG) * PW:(h % HG + 1) * PW], ct[:, h, :],
                                      vflat[:, h * VW:h * VW + PW], start=True, stop=True)
                        last.then_inc(pv_done, 1)
                    pe.wait_ge(un_ready, b + 1)
                    for k in range(KD):
                        for j in range(J):
                            last = tr(psum[2 + k][:, j * P:(j + 1) * P], un[:, j, k * P:(k + 1) * P], ident[:, :])
                    last.then_inc(unT_done, 1)
                    pe.wait_ge(unT_ready, b + 1)
                    for j in range(J):
                        for k in range(KD):
                            last = mm(psum[4][:, j * NE:(j + 1) * NE], unT[:, k, j * P:(j + 1) * P], cent[:, k, :],
                                      start=k == 0, stop=k == KD - 1)
                    last.then_inc(logit_done, 1)
                    pe.wait_ge(xs_ready, b + 1)
                    for e in range(NS):
                        for m in range(M):
                            n = e * M + m
                            if n >= 2:
                                pe.wait_ge(gelu_done, NS * M * b + n - 1)
                            for k in range(KD):
                                last = mm(psum[n % 2][:, :], w1s[:, e, k, m * P:(m + 1) * P], xs[:, k, :],
                                          start=k == 0, stop=k == KD - 1)
                            last.then_inc(up_done, 1)
                    pe.wait_ge(gelu_done, NS * M * (b + 1))
                    for j in range(J):
                        for e in range(NS):
                            for m in range(M):
                                last = mm(psum[6 + j // 2][:, (j % 2) * D:(j % 2 + 1) * D],
                                          hT[:, e, m, j * P:(j + 1) * P], w2s[:, e, m, :],
                                          start=e == 0 and m == 0, stop=e == NS - 1 and m == M - 1)
                    last.then_inc(down_done, 1)
                    pe.wait_ge(base_ready, b + 1)
                    pe.wait_ge(logit_read, b + 1)

        stage_a.close()

        stage_r = ExitStack()
        R = lambda name, shape, dt=fp32: sb(stage_r, name, shape, dt)
        prob = R("prob", [P, C, NE])
        cmp_a = R("cmp_a", [P, C * NE, NE])
        cmp_b = R("cmp_b", [P, C * NE, NE])
        earlier = R("earlier", [P, NE, NE])
        rank = R("rank", [P, C, NE])
        pick = R("pick", [P, TOPK, C, NE])
        sel = R("sel", [P, NE, C])
        total = R("total", [P, NE * C])
        upto = R("upto", [P, NE * C])
        pos = R("pos", [P, NE, C])
        tri = R("tri", [P, P])
        ones = R("ones", [P, P])
        tmp = R("tmp", [P, C, NE])
        tmp2 = R("tmp2", [P, C])
        count = R("count", [P, NE])
        first = R("first", [P, NE])
        ntile = R("ntile", [P, NE])
        ends = R("ends", [P, NE])
        delta = R("delta", [P, NE])
        limits = R("limits", [P, NL])
        numbers = R("numbers", [P, NT])
        over = R("over", [P, NE, NL])
        owner = R("owner", [P, NT, NE])
        ownerf = R("ownerf", [P, NT])
        zc = R("zc", [P, NE * C])
        slotf = R("slotf", [P, TOPK, C])
        NX = 4
        xrow = R("xrow", [P, NX, D])

        s_fill = sem("s_fill")
        r_const = sem("r_const")
        r_exp = sem("r_exp")
        r_chain = sem("r_chain")
        r_sel = sem("r_sel")
        r_cnt = sem("r_cnt")
        r_slots = sem("r_slots")
        s_row = [sem(f"s_row{i}") for i in range(NX)]
        s_scat = [sem(f"s_scat{i}") for i in range(NX)]
        ROWS_FILL = NT * T // P

        with nc.Block() as block:
            @block.sync
            def _(sp):
                sp.dma_start(xs_dram.rearrange("(p n) d -> p n d", p=P),
                             zeros[:, :].unsqueeze(1).to_broadcast([P, ROWS_FILL, D])).then_inc(s_fill, 16)
                for c in range(C):
                    if c >= NX:
                        sp.wait_ge(s_scat[c % NX], 32 * (c // NX))
                    sp.dma_start(xrow[:, c % NX, :], un_c[c]).then_inc(s_row[c % NX], 16)

            @block.gpsimd
            def _(pool):
                nc.gpsimd.memset(ones[:, :], 1.0)
                nc.gpsimd.memset(tri[:, :], 1.0)
                nc.gpsimd.memset(zc[:, :], 0.0)
                nc.gpsimd.memset(earlier[:, :, :], 1.0)
                nc.gpsimd.iota(limits[:, :], pattern=[[T, NL]], base=0, channel_multiplier=0,
                               allow_small_or_imprecise_dtypes=True)
                nc.gpsimd.iota(numbers[:, :], pattern=[[1, NT]], base=0, channel_multiplier=0,
                               allow_small_or_imprecise_dtypes=True).then_inc(r_const, 1)
                pool.wait_ge(r_const, 1)
                nc.gpsimd.affine_select(out=tri[:, :], in_=tri[:, :], compare_op=ALU.is_gt, fill=0.0, base=0,
                                        pattern=[[1, P]], channel_multiplier=-1)
                nc.gpsimd.affine_select(out=earlier[:, :, :], in_=earlier[:, :, :], compare_op=ALU.is_gt, fill=0.0,
                                        base=0, pattern=[[1, NE], [-1, NE]], channel_multiplier=0).then_inc(r_const, 1)
                pool.wait_ge(r_slots, 1)
                pool.wait_ge(s_fill, 16)
                for c in range(C):
                    pool.wait_ge(s_row[c % NX], 16 * (c // NX + 1))
                    for k in range(TOPK):
                        nc.gpsimd.indirect_dma_start(
                            out=xs_dram, out_offset=bass.IndirectOffsetOnAxis(ap=slots[:, k, c:c + 1], axis=0),
                            in_=xrow[:, c % NX, :], in_offset=None).then_inc(s_scat[c % NX], 16)
                for i in range(NX):
                    pool.wait_ge(s_scat[i], 32 * (C // NX))

            @block.scalar
            def _(sc):
                nc.scalar.activation(tmp[:, :, :], logits[:, :, :], ACT.Exp, scale=-1.0).then_inc(r_exp, 1)

            @block.tensor
            def _(pe):
                pe.wait_ge(r_const, 2)
                pe.wait_ge(r_sel, 1)
                nc.tensor.matmul(psum[0][:, 0:NE * C], tri[:, :], sel[:, :, :].rearrange("p e c -> p (e c)"),
                                 start=True, stop=True)
                nc.tensor.matmul(psum[1][:, 0:NE * C], ones[:, :], sel[:, :, :].rearrange("p e c -> p (e c)"),
                                 start=True, stop=True).then_inc(r_cnt, 1)

            @block.vector
            def _(dve):
                own = Steps(dve, r_chain, 0, 37)
                ts, tt, stt = nc.vector.tensor_scalar, nc.vector.tensor_tensor, nc.vector.scalar_tensor_tensor
                dve.wait_ge(r_exp, 1)
                own.done(ts(tmp[:, :, :], tmp[:, :, :], 1.0, None, ALU.add))
                own.done(nc.vector.reciprocal(prob[:, :, :], tmp[:, :, :]))
                dve.wait_ge(r_const, 2)
                pf = prob[:, :, :].unsqueeze(2).to_broadcast([P, C, NE, NE])
                pe_ = prob[:, :, :].unsqueeze(3).to_broadcast([P, C, NE, NE])
                ca = cmp_a[:, :, :].rearrange("p (c e) f -> p c e f", e=NE)
                cbv = cmp_b[:, :, :].rearrange("p (c e) f -> p c e f", e=NE)
                own.done(tt(ca, pf, pe_, ALU.is_gt))
                own.done(tt(cbv, pf, pe_, ALU.is_equal))
                own.done(tt(cbv, cbv, earlier[:, :, :].unsqueeze(1).to_broadcast([P, C, NE, NE]), ALU.mult))
                own.done(tt(cmp_a[:, :, :], cmp_a[:, :, :], cmp_b[:, :, :], ALU.add))
                own.done(nc.vector.tensor_reduce(rank[:, :, :].rearrange("p c e -> p (c e)"), cmp_a[:, :, :], AX.X, ALU.add))
                for k in range(TOPK):
                    own.done(ts(pick[:, k, :, :], rank[:, :, :], float(k), None, ALU.is_equal))
                tt(sel[:, :, :].rearrange("p e c -> p c e"), pick[:, 0, :, :], pick[:, 1, :, :], ALU.add).then_inc(r_sel, 1)
                own.done(nc.vector.tensor_reduce(tmp2[:, :], prob[:, :, :], AX.X, ALU.add))
                own.done(nc.vector.reciprocal(tmp2[:, :], tmp2[:, :]))
                for k in range(TOPK):
                    own.done(tt(tmp[:, :, :], pick[:, k, :, :], prob[:, :, :], ALU.mult))
                    own.done(nc.vector.tensor_reduce(gates[:, k, :], tmp[:, :, :], AX.X, ALU.add))
                    own.done(tt(gates[:, k, :], gates[:, k, :], tmp2[:, :], ALU.mult))
                dve.wait_ge(r_cnt, 1)
                own.done(nc.vector.tensor_copy(total[:, :], psum[1][:, 0:NE * C]))
                own.done(nc.vector.tensor_tensor_scan(upto[:, :], zc[:, :], total[:, :], 0.0, ALU.add, ALU.add))
                own.done(tt(total[:, :], upto[:, :], total[:, :], ALU.subtract))
                own.done(tt(pos[:, :, :].rearrange("p e c -> p (e c)"), total[:, :], psum[0][:, 0:NE * C], ALU.add))
                tv = total[:, :].rearrange("p (e c) -> p e c", c=C)
                uv = upto[:, :].rearrange("p (e c) -> p e c", c=C)
                own.done(nc.vector.tensor_copy(first[:, :], tv[:, :, 0]))
                own.done(tt(count[:, :], uv[:, :, C - 1], first[:, :], ALU.subtract))
                own.done(tt(over[:, :, :], count[:, :].unsqueeze(2).to_broadcast([P, NE, NL]),
                            limits[:, :].unsqueeze(1).to_broadcast([P, NE, NL]), ALU.is_gt))
                own.done(nc.vector.tensor_reduce(ntile[:, :], over[:, :, :], AX.X, ALU.add))
                own.done(nc.vector.tensor_tensor_scan(ends[:, :], zc[:, 0:NE], ntile[:, :], 0.0, ALU.add, ALU.add))
                own.done(tt(delta[:, :], ends[:, :], ntile[:, :], ALU.subtract))
                own.done(stt(delta[:, :], delta[:, :], float(T), first[:, :], ALU.mult, ALU.subtract))
                own.done(tt(pos[:, :, :], pos[:, :, :], delta[:, :].unsqueeze(2).to_broadcast([P, NE, C]), ALU.add))
                for k in range(TOPK):
                    own.done(tt(tmp[:, :, :], pick[:, k, :, :], pos[:, :, :].rearrange("p e c -> p c e"), ALU.mult))
                    own.done(nc.vector.tensor_reduce(slotf[:, k, :], tmp[:, :, :], AX.X, ALU.add))
                own.done(tt(owner[:, :, :], numbers[:, :].unsqueeze(2).to_broadcast([P, NT, NE]),
                            ends[:, :].unsqueeze(1).to_broadcast([P, NT, NE]), ALU.is_ge))
                own.done(nc.vector.tensor_reduce(ownerf[:, :], owner[:, :, :], AX.X, ALU.add))
                own.done(ts(ownerf[:, :], ownerf[:, :], float(NE - 1), None, ALU.min))
                own.done(nc.vector.tensor_copy(tile_expert[:, :], ownerf[:, :]))
                nc.vector.tensor_copy(slots[:, :, :], slotf[:, :, :]).then_inc(r_slots, 1)
                own.end()

        stage_r.close()

        stage_c = ExitStack()
        Cc = lambda name, shape, dt=fp32: sb(stage_c, name, shape, dt)
        gr_col = Cc("gr_col", [P, KD])
        w1 = [Cc(f"w1_{i}", [P, KD, HID]) for i in range(2)]
        w2 = [Cc(f"w2_{i}", [P, M, D]) for i in range(2)]
        b1 = [Cc(f"b1_{i}", [P, M]) for i in range(2)]
        b2 = [Cc(f"b2_{i}", [P, D]) for i in range(2)]
        xt = [Cc(f"xt_{i}", [P, TJ, D]) for i in range(2)]
        xT = [Cc(f"xT_{i}", [P, KD, T]) for i in range(2)]
        hid = [Cc(f"hid_{i}", [P, M, T]) for i in range(2)]
        yt = [Cc(f"yt_{i}", [P, TJ, D]) for i in range(2)]
        s_gr = sem("s_gr")
        t_load = [[sem(f"t_load{i}_{n}") for n in range(5)] for i in range(2)]
        t_tr, t_xT, t_up, t_gelu, t_down, t_y = (sem(n) for n in ("t_tr", "t_xT", "t_up", "t_gelu", "t_down", "t_y"))
        t_out = [sem(f"t_out{i}") for i in range(2)]
        w1_v = W1_r.rearrange("e (k p) h -> e p k h", p=P)
        w2_v = W2_r.rearrange("e (m p) d -> e p m d", p=P)
        b1_v = b1_r.rearrange("e (m p) -> e p m", p=P)

        PAIRS = NT // 2

        def tiles(engine, body):
            for i in range(2):
                body(i, i, 0)
            with engine.Fori(1, PAIRS) as r:
                for i in range(2):
                    body(2 * r + i, i, r)
            if NT % 2:
                body(NT - 1, 0, PAIRS)

        with nc.Block() as block:
            @block.sync
            def _(sp):
                with nc.allow_non_contiguous_dma(reason="a column per half"):
                    sp.dma_start(gr_col[:, :], g_r.rearrange("(k p) -> p k", p=P)).then_inc(s_gr, 16)

                def body(n, i, half):
                    e = sp.value_load(tile_expert[0:1, bass.ds(n, 1)], min_val=0, max_val=NE - 1)
                    if not (isinstance(half, int) and half == 0):
                        wait_apart(sp, t_y, n - 1)
                    sp.dma_start(xt[i][:, :, :], xs_v[bass.ds(n, 1)].rearrange("n p j d -> (n p) j d")).then_inc(t_load[i][0], 16)
                    sp.dma_start(w1[i][:, :, :], w1_v[bass.ds(e, 1)].rearrange("e p k h -> (e p) k h")).then_inc(t_load[i][1], 16)
                    with nc.allow_non_contiguous_dma(reason="a bias column per hidden chunk"):
                        sp.dma_start(b1[i][:, :], b1_v[bass.ds(e, 1)].rearrange("e p m -> (e p) m")).then_inc(t_load[i][2], 16)
                    sp.dma_start(w2[i][:, :, :], w2_v[bass.ds(e, 1)].rearrange("e p m d -> (e p) m d")).then_inc(t_load[i][3], 16)
                    sp.dma_start(b2[i][:, :], b2_r[bass.ds(e, 1), :].to_broadcast([P, D])).then_inc(t_load[i][4], 16)
                tiles(sp, body)

            @block.tensor
            def _(pe):
                def body(n, i, half):
                    pe.wait_ge(t_load[i][0], 16 * half + 16)
                    for k in range(KD):
                        for j in range(TJ):
                            last = nc.tensor.transpose(psum[4 + k][:, j * P:(j + 1) * P], xt[i][:, j, k * P:(k + 1) * P],
                                                       ident[:, :])
                    last.then_inc(t_tr, 1)
                    pe.wait_ge(t_xT, n + 1)
                    pe.wait_ge(t_load[i][1], 16 * half + 16)
                    for m in range(M):
                        if m >= 2:
                            pe.wait_ge(t_gelu, M * n + m - 1)
                        for k in range(KD):
                            last = nc.tensor.matmul(psum[m % 2][:, :], w1[i][:, k, m * P:(m + 1) * P], xT[i][:, k, :],
                                                    start=k == 0, stop=k == KD - 1)
                        last.then_inc(t_up, 1)
                    pe.wait_ge(t_load[i][3], 16 * half + 16)
                    pe.wait_ge(t_gelu, M * n + M)
                    for j in range(TJ):
                        for m in range(M):
                            last = nc.tensor.matmul(psum[6 + j // 2][:, (j % 2) * D:(j % 2 + 1) * D],
                                                    hid[i][:, m, j * P:(j + 1) * P], w2[i][:, m, :],
                                                    start=m == 0, stop=m == M - 1)
                    last.then_inc(t_down, 1)
                    pe.wait_ge(t_y, n + 1)
                tiles(pe, body)

            @block.scalar
            def _(sc):
                def body(n, i, half):
                    sc.wait_ge(t_load[i][2], 16 * half + 16)
                    for m in range(M):
                        sc.wait_ge(t_up, M * n + m + 1)
                        nc.scalar.activation(hid[i][:, m, :], psum[m % 2][:, :], ACT.Gelu, bias=b1[i][:, m:m + 1]
                                             ).then_inc(t_gelu, 1)
                    sc.wait_ge(t_y, n + 1)
                    sc.dma_start(ys_v[bass.ds(n, 1)].rearrange("n p j d -> (n p) j d"), yt[i][:, :, :]).then_inc(t_out[i], 16)
                tiles(sc, body)
                sc.wait_ge(t_out[0], 16 * (NT - PAIRS))
                sc.wait_ge(t_out[1], 16 * PAIRS)

            @block.vector
            def _(dve):
                dve.wait_ge(s_gr, 16)

                def body(n, i, half):
                    dve.wait_ge(t_tr, n + 1)
                    for k in range(KD):
                        last = nc.vector.tensor_scalar(xT[i][:, k, :], psum[4 + k][:, :], gr_col[:, k:k + 1], None, ALU.mult)
                    last.then_inc(t_xT, 1)
                    dve.wait_ge(t_down, n + 1)
                    dve.wait_ge(t_load[i][4], 16 * half + 16)
                    if not (isinstance(half, int) and half == 0):
                        dve.wait_ge(t_out[i], 16 * half)
                    for h in range(2):
                        last = nc.vector.tensor_tensor(
                            yt[i][:, 2 * h:2 * h + 2, :], psum[6 + h][:, :].rearrange("p (j d) -> p j d", d=D),
                            b2[i][:, :].unsqueeze(1).to_broadcast([P, 2, D]), ALU.add)
                    last.then_inc(t_y, 1)
                tiles(dve, body)

        stage_c.close()

        stage_d = ExitStack()
        NB = 4
        bs = sb(stage_d, "bs", [P, NB, D])
        ya = sb(stage_d, "ya", [P, TOPK, NB, D])
        yo = sb(stage_d, "yo", [P, NB, D])
        d_base = [sem(f"d_base{i}") for i in range(NB)]
        d_y = [sem(f"d_y{i}") for i in range(NB)]
        d_sum, d_res = sem("d_sum"), sem("d_res")
        d_out = [sem(f"d_out{i}") for i in range(NB)]
        with nc.Block() as block:
            @block.sync
            def _(sp):
                for c in range(C):
                    if c >= NB:
                        sp.wait_ge(d_res, c - NB + 1)
                    sp.dma_start(bs[:, c % NB, :], base_c[c]).then_inc(d_base[c % NB], 16)

            @block.gpsimd
            def _(pool):
                for c in range(C):
                    if c >= NB:
                        pool.wait_ge(d_res, c - NB + 1)
                    for k in range(TOPK):
                        nc.gpsimd.indirect_dma_start(
                            out=ya[:, k, c % NB, :], out_offset=None, in_=ys_dram,
                            in_offset=bass.IndirectOffsetOnAxis(ap=slots[:, k, c:c + 1], axis=0)).then_inc(d_y[c % NB], 16)

            @block.vector
            def _(dve):
                for c in range(C):
                    i = c % NB
                    dve.wait_ge(d_base[i], 16 * (c // NB + 1))
                    dve.wait_ge(d_y[i], 32 * (c // NB + 1))
                    nc.vector.scalar_tensor_tensor(bs[:, i, :], ya[:, 0, i, :], gates[:, 0, c:c + 1], bs[:, i, :],
                                                   ALU.mult, ALU.add).then_inc(d_sum, 1)
                    dve.wait_ge(d_sum, c + 1)
                    if c >= NB:
                        dve.wait_ge(d_out[i], 16 * (c // NB))
                    nc.vector.scalar_tensor_tensor(yo[:, i, :], ya[:, 1, i, :], gates[:, 1, c:c + 1], bs[:, i, :],
                                                   ALU.mult, ALU.add).then_inc(d_res, 1)

            @block.scalar
            def _(sc):
                for c in range(C):
                    sc.wait_ge(d_res, c + 1)
                    sc.dma_start(out_c[c], yo[:, c % NB, :]).then_inc(d_out[c % NB], 16)
                for i in range(NB):
                    sc.wait_ge(d_out[i], 16 * (C // NB))
        stage_d.close()


_INS = ['x', 'ctx_1024', 'L0_xattn_igate_w', 'L0_xattn_igate_b', 'L0_xattn_fgate_w', 'L0_xattn_fgate_b',
        'L0_xattn_ln_scale', 'L0_ffn_g_shared', 'L0_ffn_W1_s', 'L0_ffn_b1_s', 'L0_ffn_W2_s', 'L0_ffn_b2_s',
        'L0_ffn_g_routed', 'L0_ffn_W1_r', 'L0_ffn_b1_r', 'L0_ffn_W2_r', 'L0_ffn_b2_r', 'L0_ffn_centroids']


def kernel(**inputs):
    import numpy as _np
    import concourse.bacc as _bacc
    from concourse import mybir as _mybir
    from concourse.bass_utils import run_bass_kernel_spmd as _run

    nc = _bacc.Bacc("TRN2", target_bir_lowering=False, num_devices=1)
    arrays, args = {}, []
    for name in _INS:
        a = _np.ascontiguousarray(inputs[name])
        arrays[f"in_{name}_dram"] = a
        args.append(nc.dram_tensor(f"in_{name}_dram", a.shape, _mybir.dt.from_np(a.dtype), kind="ExternalInput").ap())
    o = nc.dram_tensor("out_0_dram", inputs['x'].shape, _mybir.dt.float32, kind="ExternalOutput").ap()
    xattn_moe_kernel(nc, *args, o)
    r = _run(nc, [arrays], core_ids=[0])
    return r.results[0]["out_0_dram"]
```

```python
import concourse.bass as bass
from concourse import mybir
from contextlib import ExitStack

fp32 = mybir.dt.float32
fp32r = mybir.dt.float32r
bf16 = mybir.dt.bfloat16
i32 = mybir.dt.int32
ALU = mybir.AluOpType
ACT = mybir.ActivationFunctionType
AX = mybir.AxisListType

P = 128
LN_EPS = 1e-5
RMS_EPS = 1.1920928955078125e-07
NORM_EPS = 1e-6
MASKED = -1.0e30


def xattn_moe_kernel(nc, x, ctxt, ig_w, ig_b, fg_w, fg_b, ln_scale, g_s, W1_s, b1_s, W2_s, b2_s,
                     g_r, W1_r, b1_r, W2_r, b2_r, centroids, out):
    B, S, D = x.shape
    NH = ig_w.shape[0]
    DH = D // NH
    J = S // P
    KD = D // P
    HG = NH // KD
    NS, _, HID = W1_s.shape
    NE = W1_r.shape[0]
    M = HID // P
    VW = DH + 1
    HW = HG * VW
    PW = 3 * VW
    VPAD = 2
    C = B * J
    T = 256
    TJ = T // P
    TOPK = 2
    NT = (B * S * TOPK + NE * (T - 1)) // T
    NL = B * S // T
    SCALE = float(DH) ** -0.5
    IG, FG, TR = 0, 32, 64

    xs_dram = nc.dram_tensor("sorted_tokens", [NT * T, D], fp32).ap()
    ys_dram = nc.dram_tensor("sorted_outputs", [NT * T, D], fp32).ap()
    un_dram = nc.dram_tensor("normed_tokens", [B * S, D], fp32).ap()
    base_dram = nc.dram_tensor("residual_and_shared", [B * S, D], fp32).ap()

    x_v = x.rearrange("b (j p) d -> b p j d", p=P)
    c_v = ctxt.rearrange("b (j p) d -> b p j d", p=P)
    un_v = un_dram.rearrange("(b j p) d -> b p j d", p=P, j=J)
    base_v = base_dram.rearrange("(b j p) d -> b p j d", p=P, j=J)
    un_c = un_dram.rearrange("(c p) d -> c p d", p=P)
    base_c = base_dram.rearrange("(c p) d -> c p d", p=P)
    out_c = out.rearrange("b (j p) d -> (b j) p d", p=P)
    xs_v = xs_dram.rearrange("(n j p) d -> n p j d", p=P, j=TJ)
    ys_v = ys_dram.rearrange("(n j p) d -> n p j d", p=P, j=TJ)

    whole = ExitStack()
    with whole:
        def sb(stack, name, shape, dt=fp32):
            return stack.enter_context(nc.sbuf_tensor(name, shape, dt))

        def sem(name):
            return whole.enter_context(nc.semaphore(name))

        psum = [whole.enter_context(nc.psum_tensor(f"bank{i}", [P, 512], fp32)) for i in range(8)]

        ident = sb(whole, "ident", [P, P])
        logits = sb(whole, "logits", [P, C, NE])
        slots = sb(whole, "slots", [P, TOPK, C], i32)
        gates = sb(whole, "gates", [P, TOPK, C])
        tile_expert = sb(whole, "tile_expert", [P, NT], i32)
        zeros = sb(whole, "zeros", [P, D])

        stage_a = ExitStack()
        A = lambda name, shape, dt=fp32: sb(stage_a, name, shape, dt)
        identb = A("identb", [P, P], bf16)
        causal = A("causal", [P, P], bf16)
        gate_w = A("gate_w", [P, 2 * KD, 40])
        ig_bias = A("ig_bias", [NH, 1])
        fg_bias = A("fg_bias", [40, 1])
        negsel = A("negsel", [NH, NH])
        headmask = A("headmask", [P, HG])
        blockmask = A("blockmask", [P, HG, VW])
        lnsc = A("lnsc", [P, D])
        gs_col = A("gs_col", [P, KD])
        cent = A("cent", [P, KD, NE])
        w1s = A("w1s", [P, NS, KD, HID])
        w2s = A("w2s", [P, NS, M, D])
        b1s = A("b1s", [P, NS, M])
        b2s2 = A("b2s2", [P, NS, D])
        b2s = A("b2s", [P, D])
        eps = A("eps", [P, 2])
        exp_rhs = A("exp_rhs", [40, J, NH, P])
        exp_lhs = A("exp_lhs", [40, S])
        rows = A("rows", [72, S])
        frow = A("frow", [40, 5, S])
        cs = A("cs", [NH, S])
        zrow = A("zrow", [40, S])
        vaug = A("vaug", [P, J, NH + VPAD, VW])
        xb = A("xb", [P, J, D])
        cb = A("cb", [P, J, D])
        qn = A("qn", [P, J, D])
        qcT = A("qcT", [P, 2 * KD, S])
        qmask = A("qmask", [P, KD, HG, S])
        bn6 = A("bn6", [P, J, 6])
        mv = A("mv", [P, J, 2])
        nw = A("nw", [P, 5, J])
        cols = A("cols", [P, 3 * P])
        earg = A("earg", [P, P])
        eexp = A("eexp", [P, P])
        NPAIR = J * (J - 1) // 2
        wv = A("wv", [P, NPAIR, NH, VW])
        state = A("state", [P, KD, J - 1, HW])
        decay = A("decay", [P, NH, P])
        ct = A("ct", [P, NH, P])
        hn = A("hn", [P, J, NH, VW])
        rnorm = A("rnorm", [P, 3, J * NH])
        hh = A("hh", [P, J, D])
        x1 = A("x1", [P, J, D])
        un = A("un", [P, J, D])
        base = A("base", [P, J, D])
        junk = A("junk", [P, D])
        unT = A("unT", [P, KD, S])
        xs = A("xs", [P, KD, S])
        hT = A("hT", [P, 2, M, S])

        gw_nat = hT[0:40, 0, 0:2, :].rearrange("p a s -> p (a s)")[:, 0:3 * D]

        s_load = sem("s_load")
        s_const = sem("s_const")
        s_cpre = sem("s_cpre")
        s_gwT = sem("s_gwT")

        with nc.Block() as block:
            @block.sync
            def _(sp):
                sp.wait_ge(s_cpre, 1)
                loads = [
                    (gw_nat[IG:IG + NH, :], ig_w), (gw_nat[FG:FG + NH, :], fg_w),
                    (ig_bias[:, :], ig_b.rearrange("(h o) -> h o", o=1)),
                    (fg_bias[FG:FG + NH, :], fg_b.rearrange("(h o) -> h o", o=1)),
                    (lnsc[:, :], ln_scale.rearrange("(o d) -> o d", o=1).to_broadcast([P, D])),
                    (cent[:, :, :], centroids.rearrange("(k p) e -> p k e", p=P)),
                    (w1s[:, :, :, :], W1_s.rearrange("e (k p) h -> p e k h", p=P)),
                    (w2s[:, :, :, :], W2_s.rearrange("e (m p) d -> p e m d", p=P)),
                    (b2s2[:, :, :], b2_s.rearrange("(o e) d -> o e d", o=1).to_broadcast([P, NS, D])),
                ]
                with nc.allow_non_contiguous_dma(reason="small transposed vectors"):
                    for n, (dst, src) in enumerate(loads):
                        sp.dma_start(dst, src).then_inc(s_load, 16)
                    sp.dma_start(gs_col[:, :], g_s.rearrange("(k p) -> p k", p=P)).then_inc(s_load, 16)
                    for e in range(NS):
                        sp.dma_start(b1s[:, e, :], b1_s[e, :].rearrange("(m p) -> p m", p=P)).then_inc(s_load, 16)
                sp.wait_ge(s_load, 16 * (len(loads) + 1 + NS))

            @block.gpsimd
            def _(pool):
                nc.gpsimd.memset(ident[:, :], 0.0)
                nc.gpsimd.memset(negsel[:, :], 0.0)
                nc.gpsimd.memset(causal[:, :], 0.0)
                nc.gpsimd.memset(headmask[:, :], 1.0)
                nc.gpsimd.memset(exp_lhs[:, :], 0.0)
                nc.gpsimd.memset(rows[:, :], 0.0)
                nc.gpsimd.memset(blockmask[:, :, :], SCALE)
                nc.gpsimd.memset(exp_rhs[:, :, :, :], 0.0)
                nc.gpsimd.memset(vaug[:, :, :, :], 1.0)
                nc.gpsimd.memset(zrow[:, :], 0.0)
                nc.gpsimd.memset(eps[:, 0:1], LN_EPS)
                nc.gpsimd.memset(eps[:, 1:2], RMS_EPS).then_inc(s_const, 1)
                pool.wait_ge(s_const, 1)
                nc.gpsimd.affine_select(out=ident[:, :], in_=ident[:, :], compare_op=ALU.not_equal, fill=1.0,
                                        base=0, pattern=[[-1, P]], channel_multiplier=1)
                nc.gpsimd.affine_select(out=negsel[:, :], in_=negsel[:, :], compare_op=ALU.not_equal, fill=-1.0,
                                        base=0, pattern=[[-1, NH]], channel_multiplier=1)
                nc.gpsimd.affine_select(out=causal[:, :], in_=causal[:, :], compare_op=ALU.is_ge, fill=MASKED,
                                        base=0, pattern=[[1, P]], channel_multiplier=-1)
                nc.gpsimd.affine_select(out=headmask[:, :], in_=headmask[:, :], compare_op=ALU.is_ge, fill=0.0,
                                        base=0, pattern=[[-DH, HG]], channel_multiplier=1)
                nc.gpsimd.affine_select(out=blockmask[:, :, :], in_=blockmask[:, :, :], compare_op=ALU.is_ge,
                                        fill=0.0, base=0, pattern=[[-DH, HG], [0, VW]], channel_multiplier=1)
                nc.gpsimd.memset(exp_lhs[0:NH, :], 1.0).then_inc(s_const, 1)
                pool.wait_ge(s_const, 2)
                nc.gpsimd.affine_select(out=headmask[:, :], in_=headmask[:, :], compare_op=ALU.is_ge, fill=0.0,
                                        base=DH - 1, pattern=[[DH, HG]], channel_multiplier=-1)
                nc.gpsimd.affine_select(out=blockmask[:, :, :], in_=blockmask[:, :, :], compare_op=ALU.is_ge,
                                        fill=0.0, base=DH - 1, pattern=[[DH, HG], [0, VW]], channel_multiplier=-1)
                for j in range(J):
                    nc.gpsimd.affine_select(out=exp_rhs[:, j, :, :], in_=exp_rhs[:, j, :, :],
                                            compare_op=ALU.not_equal, fill=1.0, base=FG,
                                            pattern=[[1, NH], [0, P]], channel_multiplier=-1)
                nc.gpsimd.tensor_copy(identb[:, :], ident[:, :]).then_inc(s_const, 1)

            @block.vector
            def _(dve):
                nc.vector.memset(gw_nat, 0.0).then_inc(s_cpre, 1)
                nc.vector.memset(zeros[:, :], 0.0)
                dve.wait_ge(s_load, 16 * 12)
                nc.vector.tensor_tensor(b2s[:, :], b2s2[:, 0, :], b2s2[:, 1, :], ALU.add)
                dve.wait_ge(s_gwT, 1)
                pv = psum[0][:, 0:6 * 40].rearrange("p (n g) -> p n g", g=40)
                nc.vector.tensor_copy(gate_w[:, :, :], pv[:, 0:2 * KD, :]).then_inc(s_cpre, 1)
                dve.wait_ge(s_cpre, 2)
                nc.vector.tensor_tensor(gate_w[:, KD:2 * KD, :], gate_w[:, KD:2 * KD, :], pv[:, 2 * KD:3 * KD, :],
                                        ALU.add).then_inc(s_cpre, 1)

            @block.tensor
            def _(pe):
                pe.wait_ge(s_load, 16 * 12)
                pe.wait_ge(s_const, 3)
                for n in range(3 * KD):
                    last = nc.tensor.transpose(psum[0][:, n * 40:(n + 1) * 40], gw_nat[:, n * P:(n + 1) * P],
                                               ident[0:40, 0:40])
                last.then_inc(s_gwT, 1)

        s_x, s_c = sem("s_x"), sem("s_c")
        s_un_out, s_base_out = sem("s_un_out"), sem("s_base_out")
        xc_free = sem("xc_free")
        stats = sem("stats")
        rsq = sem("rsq")
        act = sem("act")
        chain = sem("chain")
        q_ready, tr_done, qcT_ready, qmask_ready = sem("q_ready"), sem("tr_done"), sem("qcT_ready"), sem("qmask_ready")
        gates_done, logsig_ready, rows_ready, lhs_ready = sem("gates_done"), sem("logsig_ready"), sem("rows_ready"), sem("lhs_ready")
        rhs_ready, cols_done, earg_ready, eexp_ready = sem("rhs_ready"), sem("cols_done"), sem("earg_ready"), sem("eexp_ready")
        vaug_ready, wv_ready, state_done, state_ready = sem("vaug_ready"), sem("wv_ready"), sem("state_done"), sem("state_ready")
        exp_done, score_done, decay_ready, ct_ready = sem("exp_done"), sem("score_done"), sem("decay_ready"), sem("ct_ready")
        inter_done, pv_done, hn_ready = sem("inter_done"), sem("pv_done"), sem("hn_ready")
        x1_ready, u_ready, un_ready = sem("x1_ready"), sem("u_ready"), sem("un_ready")
        unT_done, unT_ready, xs_ready, logit_done = sem("unT_done"), sem("unT_ready"), sem("xs_ready"), sem("logit_done")
        logit_read = sem("logit_read")
        up_done, gelu_done, down_done, base_ready = sem("up_done"), sem("gelu_done"), sem("down_done"), sem("base_ready")

        passed = sem("passed")

        def wait_apart(engine, semaphore, value):
            engine.wait_ge(semaphore, value)
            engine.sem_inc(passed, 1)

        class Steps:
            def __init__(self, engine, semaphore, i, n):
                self.engine, self.semaphore, self.first, self.n, self.k = engine, semaphore, i * n, n, 0

            def done(self, instruction, alone=False):
                self.k += 1
                instruction.then_inc(self.semaphore, 1)
                (wait_apart if alone else type(self.engine).wait_ge)(self.engine, self.semaphore, self.first + self.k)

            def end(self):
                assert self.k == self.n, self.k

        with nc.Block() as block:
            @block.sync
            def _(sp):
                with sp.Fori(0, B) as b:
                    wait_apart(sp, xc_free, b + 1)
                    sp.dma_start(xb[:, :, :], x_v[bass.ds(b, 1)].rearrange("b p j d -> (b p) j d")).then_inc(s_x, 16)
                    sp.dma_start(cb[:, :, :], c_v[bass.ds(b, 1)].rearrange("b p j d -> (b p) j d")).then_inc(s_c, 16)
                    wait_apart(sp, un_ready, b + 1)
                    sp.dma_start(un_v[bass.ds(b, 1)].rearrange("b p j d -> (b p) j d"), un[:, :, :]).then_inc(s_un_out, 16)
                    wait_apart(sp, base_ready, b + 1)
                    sp.dma_start(base_v[bass.ds(b, 1)].rearrange("b p j d -> (b p) j d"), base[:, :, :]).then_inc(s_base_out, 16)
                    sp.wait_ge(s_un_out, 16 * b + 16)
                    wait_apart(sp, s_base_out, 16 * b + 16)

            @block.gpsimd
            def _(pool):
                with pool.Fori(0, B) as b:
                    pool.wait_ge(s_c, 16 * b + 16)
                    wait_apart(pool, xc_free, b + 1)
                    nc.gpsimd.tensor_copy(vaug[:, :, 0:NH, 0:DH], cb[:, :, :].rearrange("p j (h e) -> p j h e", e=DH)
                                          ).then_inc(vaug_ready, 1)
                    wait_apart(pool, qcT_ready, J * b + J)
                    for g in range(KD):
                        for r in range(HG):
                            last = nc.gpsimd.tensor_scalar(qmask[:, g, r, :], qcT[:, g, :], headmask[:, r:r + 1], None,
                                                           ALU.mult)
                    last.then_inc(qmask_ready, 1)
                    pool.wait_ge(rows_ready, b + 1)
                    for j in range(J):
                        last = nc.gpsimd.tensor_tensor(
                            exp_rhs[0:NH, j, :, :], negsel[:, :].unsqueeze(2).to_broadcast([NH, NH, P]),
                            rows[0:NH, j * P:(j + 1) * P].unsqueeze(1).to_broadcast([NH, NH, P]), ALU.mult)
                    last.then_inc(rhs_ready, 1)
                    pool.wait_ge(eexp_ready, b + 1)
                    n = 0
                    for j in range(J - 1):
                        for i in range(j + 1):
                            w = eexp[:, (i * (J - 1) + j) * NH:(i * (J - 1) + j + 1) * NH]
                            last = nc.gpsimd.tensor_tensor(wv[:, n, :, :], vaug[:, i, 0:NH, :],
                                                           w.unsqueeze(2).to_broadcast([P, NH, VW]), ALU.mult)
                            n += 1
                    last.then_inc(wv_ready, 1)

            @block.scalar
            def _(sc):
                with sc.Fori(0, B) as b:
                    own = Steps(sc, act, b, 12)

                    def rsqrt(k, src, col, scale):
                        sc.wait_ge(stats, 3 * b + k + 1)
                        own.done(nc.scalar.activation(nw[:, 1, :], src, ACT.Ln, bias=eps[:, col:col + 1], scale=scale))
                        nc.scalar.activation(nw[:, 0, :], nw[:, 1, :], ACT.Exp, scale=-0.5).then_inc(rsq, 1)

                    rsqrt(0, mv[:, :, 1], 0, 1.0)
                    for j in range(J):
                        sc.wait_ge(tr_done, J * b + j + 1)
                        nc.scalar.copy(qcT[:, :, j * P:(j + 1) * P],
                                       psum[2 + j][:, :].rearrange("p (k s) -> p k s", s=P)).then_inc(qcT_ready, 1)
                    sc.wait_ge(gates_done, b + 1)
                    own.done(nc.scalar.activation(frow[FG:FG + NH, 0, :], psum[6][FG:FG + NH, :], ACT.Abs,
                                                  bias=fg_bias[FG:FG + NH, :]))
                    own.done(nc.scalar.activation(frow[FG:FG + NH, 1, :], frow[FG:FG + NH, 0, :], ACT.Exp, scale=-1.0))
                    nc.scalar.activation(frow[FG:FG + NH, 2, :], frow[FG:FG + NH, 1, :], ACT.Ln, bias=1.0
                                         ).then_inc(logsig_ready, 1)
                    sc.wait_ge(rows_ready, b + 1)
                    nc.scalar.copy(exp_lhs[FG:FG + NH, :], rows[FG:FG + NH, :]).then_inc(lhs_ready, 1)
                    sc.wait_ge(earg_ready, b + 1)
                    nc.scalar.activation(eexp[:, :], earg[:, :], ACT.Exp).then_inc(eexp_ready, 1)
                    for j in range(J):
                        sc.wait_ge(exp_done, J * b + j + 1)
                        if j > 0:
                            sc.wait_ge(ct_ready, J * b + j)
                        for g in range(KD):
                            last = nc.scalar.activation(
                                decay[:, g * HG:(g + 1) * HG, :], psum[g][:, :].rearrange("p (h s) -> p h s", s=P),
                                ACT.Exp)
                        last.then_inc(decay_ready, 1)
                    rsqrt(1, mv[:, :, 1], 0, 1.0)
                    rsqrt(2, mv[:, :, 1], 0, 1.0)
                    sc.wait_ge(u_ready, b + 1)
                    for j in range(J):
                        own.done(nc.scalar.activation(junk[:, :], hh[:, j, :], ACT.Square, accum_out=nw[:, 4, j:j + 1]))
                    rsqrt3 = nc.scalar.activation(nw[:, 1, :], nw[:, 4, :], ACT.Ln, bias=eps[:, 1:2], scale=1.0 / D)
                    own.done(rsqrt3)
                    nc.scalar.activation(nw[:, 0, :], nw[:, 1, :], ACT.Exp, scale=-0.5).then_inc(rsq, 1)
                    sc.wait_ge(unT_done, b + 1)
                    for k in range(KD):
                        own_last = nc.scalar.copy(unT[:, k, :], psum[2 + k][:, :])
                        if k == KD - 1:
                            own_last.then_inc(unT_ready, 1)
                    own.done(nc.scalar.copy(junk[:, 0:1], eps[:, 0:1]))
                    own.done(nc.scalar.copy(junk[:, 0:1], eps[:, 0:1]))
                    for e in range(NS):
                        for m in range(M):
                            n = e * M + m
                            sc.wait_ge(up_done, NS * M * b + n + 1)
                            nc.scalar.activation(hT[:, e % 2, m, :], psum[n % 2][:, :], ACT.Gelu,
                                                 bias=b1s[:, e, m:m + 1]).then_inc(gelu_done, 1)
                    own.end()

            @block.vector
            def _(dve):
                nc.vector.memset(junk[:, 0:1], 0.0).then_inc(xc_free, 1)
                with dve.Fori(0, B) as b:
                    own = Steps(dve, chain, b, 39)
                    ts, tt, stt = nc.vector.tensor_scalar, nc.vector.tensor_tensor, nc.vector.scalar_tensor_tensor

                    def moments(src, k):
                        for j in range(J):
                            last = nc.vector.bn_stats(bn6[:, j, :], src[:, j, :])
                        own.done(last, alone=True)
                        for j in range(J):
                            last = nc.vector.bn_aggr(mv[:, j, :], bn6[:, j, :])
                        last.then_inc(stats, 1)
                        dve.wait_ge(stats, 3 * b + k + 1)

                    def refine(k, v, e, scale):
                        own.done(ts(nw[:, 2, :], v, scale, e, ALU.mult, ALU.add))
                        dve.wait_ge(rsq, 4 * b + k + 1)
                        own.done(tt(nw[:, 3, :], nw[:, 0, :], nw[:, 0, :], ALU.mult))
                        own.done(stt(nw[:, 2, :], nw[:, 3, :], -0.5, nw[:, 2, :], ALU.mult, ALU.mult))
                        own.done(stt(nw[:, 3, :], nw[:, 2, :], 1.5, nw[:, 0, :], ALU.add, ALU.mult))

                    def normed(dst, src):
                        for j in range(J):
                            last = ts(dst[:, j, :], src[:, j, :], mv[:, j, 0:1], nw[:, 3, j:j + 1],
                                      ALU.subtract, ALU.mult)
                        return last

                    dve.wait_ge(s_x, 16 * b + 16)
                    moments(xb, 0)
                    refine(0, mv[:, :, 1], LN_EPS, 1.0)
                    normed(qn, xb).then_inc(q_ready, 1)

                    dve.wait_ge(gates_done, b + 1)
                    dve.wait_ge(logsig_ready, b + 1)
                    own.done(ts(frow[FG:FG + NH, 3, :], psum[6][FG:FG + NH, :], fg_bias[FG:FG + NH, :], 0.0,
                                ALU.add, ALU.min))
                    own.done(tt(frow[FG:FG + NH, 4, :], frow[FG:FG + NH, 3, :], frow[FG:FG + NH, 2, :], ALU.subtract))
                    own.done(nc.vector.tensor_tensor_scan(cs[:, :], zrow[FG:FG + NH, :], frow[FG:FG + NH, 4, :], 0.0,
                                                          ALU.add, ALU.add))
                    own.done(stt(rows[FG:FG + NH, :], psum[6][IG:IG + NH, :], ig_bias[:, :], cs[:, :],
                                 ALU.add, ALU.subtract))
                    own.done(nc.vector.tensor_tensor_scan(rows[0:NH, :], rows[FG:FG + NH, :], rows[FG:FG + NH, :],
                                                          -3.0e38, ALU.max, ALU.max))
                    tt(rows[TR:TR + NH, :], cs[:, :], rows[0:NH, :], ALU.add).then_inc(rows_ready, 1)

                    dve.wait_ge(cols_done, b + 1)
                    own.done(nc.vector.tensor_copy(cols[:, 0:J * 72 + (J - 1) * NH], psum[7][:, 0:J * 72 + (J - 1) * NH]))
                    cv = cols[:, 0:J * 72].rearrange("p (j r) -> p j r", r=72)
                    nm = cols[:, J * 72:J * 72 + (J - 1) * NH].rearrange("p (j h) -> p j h", h=NH)
                    NW = (J - 1) * (J - 1) * NH
                    for i in range(J - 1):
                        ev = earg[:, i * (J - 1) * NH:(i + 1) * (J - 1) * NH].rearrange("p (j h) -> p j h", h=NH)
                        last = tt(ev, nm, cv[:, i:i + 1, FG:FG + NH].to_broadcast([P, J - 1, NH]), ALU.add)
                    rv = earg[:, NW:NW + (J - 1) * NH].rearrange("p (j h) -> p j h", h=NH)
                    stt(rv, cv[:, 1:J, 0:NH], -1.0, nm, ALU.mult, ALU.subtract)
                    mvw = earg[:, NW + (J - 1) * NH:NW + (2 * J - 1) * NH].rearrange("p (j h) -> p j h", h=NH)
                    own.done(ts(mvw, cv[:, :, TR:TR + NH], -1.0, None, ALU.mult))
                    ts(earg[:, 0:NW], earg[:, 0:NW], 0.0, None, ALU.min).then_inc(earg_ready, 1)

                    dve.wait_ge(state_done, b + 1)
                    bm = blockmask[:, :, :].rearrange("p h e -> p (h e)").unsqueeze(1).to_broadcast([P, J - 1, HW])
                    for g in range(KD):
                        last = tt(state[:, g, :, :], psum[g][:, 0:(J - 1) * HW].rearrange("p (j c) -> p j c", c=HW), bm,
                                  ALU.mult)
                    last.then_inc(state_ready, 1)
                    dve.wait_ge(eexp_ready, b + 1)
                    for j in range(J):
                        dve.wait_ge(score_done, J * b + j + 1)
                        dve.wait_ge(decay_ready, J * b + j + 1)
                        for g in range(KD):
                            last = stt(ct[:, g * HG:(g + 1) * HG, :],
                                       psum[2 + g][:, :].rearrange("p (h s) -> p h s", s=P), SCALE,
                                       decay[:, g * HG:(g + 1) * HG, :], ALU.mult, ALU.mult)
                        last.then_inc(ct_ready, 1)
                        dve.wait_ge(pv_done, J * b + j + 1)
                        if j > 0:
                            rr = eexp[:, NW + (j - 1) * NH:NW + j * NH].unsqueeze(2).to_broadcast([P, NH, VW])
                            own.done(tt(hn[:, j, :, :], psum[4][:, 0:NH * VW].rearrange("p (h e) -> p h e", e=VW), rr,
                                        ALU.mult))
                        for g in range(KD):
                            pvv = psum[5 + g][:, 0:HG * PW].rearrange("p (h e) -> p h e", e=PW)[:, :, 0:VW]
                            dst = hn[:, j, g * HG:(g + 1) * HG, :]
                            if j > 0:
                                last = tt(dst, dst, pvv, ALU.add)
                            else:
                                last = nc.vector.tensor_copy(dst, pvv)
                        last.then_inc(hn_ready, 1)
                    dve.wait_ge(hn_ready, J * b + J)
                    hv = hn[:, :, :, :].rearrange("p j h e -> p (j h) e")
                    own.done(stt(rnorm[:, 0, :], hv[:, :, DH], -1.0, hv[:, :, DH], ALU.mult, ALU.max))
                    own.done(tt(rnorm[:, 1, :], rnorm[:, 0, :], eexp[:, NW + (J - 1) * NH:NW + (2 * J - 1) * NH], ALU.max))
                    own.done(ts(rnorm[:, 0, :], rnorm[:, 1, :], NORM_EPS, None, ALU.add))
                    own.done(nc.vector.reciprocal(rnorm[:, 2, :], rnorm[:, 0, :]))
                    own.done(tt(hh[:, :, :].rearrange("p j (h e) -> p (j h) e", e=DH), hv[:, :, 0:DH],
                                rnorm[:, 2, :].unsqueeze(2).to_broadcast([P, J * NH, DH]), ALU.mult))
                    moments(hh, 1)
                    refine(1, mv[:, :, 1], LN_EPS, 1.0)
                    own.done(normed(qn, hh))
                    own.done(tt(qn[:, :, :], qn[:, :, :], lnsc[:, :].unsqueeze(1).to_broadcast([P, J, D]), ALU.mult))
                    tt(x1[:, :, :], qn[:, :, :], xb[:, :, :], ALU.add).then_inc(x1_ready, 1)
                    dve.wait_ge(x1_ready, b + 1)
                    nc.vector.memset(junk[:, 0:1], 0.0).then_inc(xc_free, 1)
                    moments(x1, 2)
                    refine(2, mv[:, :, 1], LN_EPS, 1.0)
                    normed(hh, x1).then_inc(u_ready, 1)
                    dve.wait_ge(u_ready, b + 1)
                    own.done(tt(base[:, :, :], x1[:, :, :], hh[:, :, :], ALU.add))
                    dve.wait_ge(rsq, 4 * b + 4)
                    refine(3, nw[:, 4, :], RMS_EPS, 1.0 / D)
                    for j in range(J):
                        last = ts(un[:, j, :], hh[:, j, :], nw[:, 3, j:j + 1], None, ALU.mult)
                    last.then_inc(un_ready, 1)
                    own.done(nc.vector.reciprocal(nw[:, 2, :], nw[:, 3, :]))
                    own.done(tt(base[:, :, :], base[:, :, :], b2s[:, :].unsqueeze(1).to_broadcast([P, J, D]), ALU.add))
                    dve.wait_ge(unT_ready, b + 1)
                    for k in range(KD):
                        last = ts(xs[:, k, :], unT[:, k, :], gs_col[:, k:k + 1], None, ALU.mult)
                    last.then_inc(xs_ready, 1)
                    dve.wait_ge(logit_done, b + 1)
                    tt(logits[:, bass.ds(b * J, J), :], psum[4][:, 0:J * NE].rearrange("p (j e) -> p j e", e=NE),
                       nw[:, 2, :].unsqueeze(2).to_broadcast([P, J, NE]), ALU.mult).then_inc(logit_read, 1)
                    dve.wait_ge(down_done, b + 1)
                    for h in range(2):
                        last = tt(base[:, 2 * h:2 * h + 2, :], base[:, 2 * h:2 * h + 2, :],
                                  psum[6 + h][:, :].rearrange("p (j d) -> p j d", d=D), ALU.add)
                    last.then_inc(base_ready, 1)
                    dve.wait_ge(s_base_out, 16 * b + 16)
                    dve.wait_ge(s_un_out, 16 * b + 16)
                    own.end()

            @block.tensor
            def _(pe):
                with pe.Fori(0, B) as b:
                    mm, tr = nc.tensor.matmul, nc.tensor.transpose
                    pe.wait_ge(q_ready, b + 1)
                    pe.wait_ge(s_c, 16 * b + 16)
                    for j in range(J):
                        for k in range(KD):
                            tr(psum[2 + j][:, k * P:(k + 1) * P], qn[:, j, k * P:(k + 1) * P], ident[:, :])
                        for k in range(KD):
                            last = tr(psum[2 + j][:, (KD + k) * P:(KD + k + 1) * P], cb[:, j, k * P:(k + 1) * P], ident[:, :])
                        last.then_inc(tr_done, 1)
                    pe.wait_ge(qcT_ready, J * b + J)
                    for k in range(2 * KD):
                        last = mm(psum[6][0:40, :], gate_w[:, k, :], qcT[:, k, :], start=k == 0, stop=k == 2 * KD - 1)
                    last.then_inc(gates_done, 1)
                    pe.wait_ge(rows_ready, b + 1)
                    for j in range(J):
                        tr(psum[7][:, j * 72:(j + 1) * 72], rows[:, j * P:(j + 1) * P], ident[0:72, 0:72])
                    pe.wait_ge(rhs_ready, b + 1)
                    mm(psum[7][:, J * 72:J * 72 + (J - 1) * NH], exp_lhs[0:NH, 0:P], exp_rhs[0:NH, 0:J - 1, :, P - 1],
                       start=True, stop=True).then_inc(cols_done, 1)
                    pe.wait_ge(wv_ready, b + 1)
                    for g in range(KD):
                        for j in range(J - 1):
                            for i in range(j + 1):
                                last = mm(psum[g][:, j * HW:(j + 1) * HW], cb[:, i, g * P:(g + 1) * P],
                                          wv[:, j * (j + 1) // 2 + i, g * HG:(g + 1) * HG, :].rearrange("p h e -> p (h e)"),
                                          start=i == 0, stop=i == j)
                    last.then_inc(state_done, 1)
                    pe.wait_ge(state_ready, b + 1)
                    pe.wait_ge(qmask_ready, b + 1)
                    pe.wait_ge(lhs_ready, b + 1)
                    for j in range(J):
                        cj = slice(j * P, (j + 1) * P)
                        if j > 0:
                            pe.wait_ge(decay_ready, J * b + j)
                            pe.wait_ge(hn_ready, J * b + j)
                        for g in range(KD):
                            mm(psum[g][:, :], identb[:, :], causal[:, :].unsqueeze(1).to_broadcast([P, HG, P]),
                               start=True, stop=False)
                            last = mm(psum[g][:, :], exp_lhs[:, cj],
                                      exp_rhs[:, j, g * HG:(g + 1) * HG, :].rearrange("p h s -> p (h s)"),
                                      start=False, stop=True)
                        last.then_inc(exp_done, 1)
                        for g in range(KD):
                            last = mm(psum[2 + g][:, :], qcT[:, KD + g, cj], qmask[:, g, :, cj], start=True, stop=True)
                        last.then_inc(score_done, 1)
                        if j > 0:
                            for g in range(KD):
                                mm(psum[4][:, g * HW:(g + 1) * HW], qcT[:, g, cj], state[:, g, j - 1, :],
                                   start=True, stop=True)
                        pe.wait_ge(ct_ready, J * b + j + 1)
                        vflat = vaug[:, j, :, :].rearrange("p h e -> p (h e)")
                        for h in range(NH):
                            last = mm(psum[5 + h // HG][:, (h % HG) * PW:(h % HG + 1) * PW], ct[:, h, :],
                                      vflat[:, h * VW:h * VW + PW], start=True, stop=True)
                        last.then_inc(pv_done, 1)
                    pe.wait_ge(un_ready, b + 1)
                    for k in range(KD):
                        for j in range(J):
                            last = tr(psum[2 + k][:, j * P:(j + 1) * P], un[:, j, k * P:(k + 1) * P], ident[:, :])
                    last.then_inc(unT_done, 1)
                    pe.wait_ge(unT_ready, b + 1)
                    for j in range(J):
                        for k in range(KD):
                            last = mm(psum[4][:, j * NE:(j + 1) * NE], unT[:, k, j * P:(j + 1) * P], cent[:, k, :],
                                      start=k == 0, stop=k == KD - 1)
                    last.then_inc(logit_done, 1)
                    pe.wait_ge(xs_ready, b + 1)
                    for e in range(NS):
                        for m in range(M):
                            n = e * M + m
                            if n >= 2:
                                pe.wait_ge(gelu_done, NS * M * b + n - 1)
                            for k in range(KD):
                                last = mm(psum[n % 2][:, :], w1s[:, e, k, m * P:(m + 1) * P], xs[:, k, :],
                                          start=k == 0, stop=k == KD - 1)
                            last.then_inc(up_done, 1)
                    pe.wait_ge(gelu_done, NS * M * (b + 1))
                    for j in range(J):
                        for e in range(NS):
                            for m in range(M):
                                last = mm(psum[6 + j // 2][:, (j % 2) * D:(j % 2 + 1) * D],
                                          hT[:, e, m, j * P:(j + 1) * P], w2s[:, e, m, :],
                                          start=e == 0 and m == 0, stop=e == NS - 1 and m == M - 1)
                    last.then_inc(down_done, 1)
                    pe.wait_ge(base_ready, b + 1)
                    pe.wait_ge(logit_read, b + 1)

        stage_a.close()

        stage_r = ExitStack()
        R = lambda name, shape, dt=fp32: sb(stage_r, name, shape, dt)
        prob = R("prob", [P, C, NE])
        cmp_a = R("cmp_a", [P, C * NE, NE])
        cmp_b = R("cmp_b", [P, C * NE, NE])
        earlier = R("earlier", [P, NE, NE])
        rank = R("rank", [P, C, NE])
        pick = R("pick", [P, TOPK, C, NE])
        sel = R("sel", [P, NE, C])
        total = R("total", [P, NE * C])
        upto = R("upto", [P, NE * C])
        pos = R("pos", [P, NE, C])
        tri = R("tri", [P, P])
        ones = R("ones", [P, P])
        tmp = R("tmp", [P, C, NE])
        tmp2 = R("tmp2", [P, C])
        count = R("count", [P, NE])
        first = R("first", [P, NE])
        ntile = R("ntile", [P, NE])
        ends = R("ends", [P, NE])
        delta = R("delta", [P, NE])
        limits = R("limits", [P, NL])
        numbers = R("numbers", [P, NT])
        over = R("over", [P, NE, NL])
        owner = R("owner", [P, NT, NE])
        ownerf = R("ownerf", [P, NT])
        zc = R("zc", [P, NE * C])
        slotf = R("slotf", [P, TOPK, C])
        NX = 4
        xrow = R("xrow", [P, NX, D])

        s_fill = sem("s_fill")
        r_const = sem("r_const")
        r_exp = sem("r_exp")
        r_chain = sem("r_chain")
        r_sel = sem("r_sel")
        r_cnt = sem("r_cnt")
        r_slots = sem("r_slots")
        s_row = [sem(f"s_row{i}") for i in range(NX)]
        s_scat = [sem(f"s_scat{i}") for i in range(NX)]
        ROWS_FILL = NT * T // P

        with nc.Block() as block:
            @block.sync
            def _(sp):
                sp.dma_start(xs_dram.rearrange("(p n) d -> p n d", p=P),
                             zeros[:, :].unsqueeze(1).to_broadcast([P, ROWS_FILL, D])).then_inc(s_fill, 16)
                for c in range(C):
                    if c >= NX:
                        sp.wait_ge(s_scat[c % NX], 32 * (c // NX))
                    sp.dma_start(xrow[:, c % NX, :], un_c[c]).then_inc(s_row[c % NX], 16)

            @block.gpsimd
            def _(pool):
                nc.gpsimd.memset(ones[:, :], 1.0)
                nc.gpsimd.memset(tri[:, :], 1.0)
                nc.gpsimd.memset(zc[:, :], 0.0)
                nc.gpsimd.memset(earlier[:, :, :], 1.0)
                nc.gpsimd.iota(limits[:, :], pattern=[[T, NL]], base=0, channel_multiplier=0,
                               allow_small_or_imprecise_dtypes=True)
                nc.gpsimd.iota(numbers[:, :], pattern=[[1, NT]], base=0, channel_multiplier=0,
                               allow_small_or_imprecise_dtypes=True).then_inc(r_const, 1)
                pool.wait_ge(r_const, 1)
                nc.gpsimd.affine_select(out=tri[:, :], in_=tri[:, :], compare_op=ALU.is_gt, fill=0.0, base=0,
                                        pattern=[[1, P]], channel_multiplier=-1)
                nc.gpsimd.affine_select(out=earlier[:, :, :], in_=earlier[:, :, :], compare_op=ALU.is_gt, fill=0.0,
                                        base=0, pattern=[[1, NE], [-1, NE]], channel_multiplier=0).then_inc(r_const, 1)
                pool.wait_ge(r_slots, 1)
                pool.wait_ge(s_fill, 16)
                for c in range(C):
                    pool.wait_ge(s_row[c % NX], 16 * (c // NX + 1))
                    for k in range(TOPK):
                        nc.gpsimd.indirect_dma_start(
                            out=xs_dram, out_offset=bass.IndirectOffsetOnAxis(ap=slots[:, k, c:c + 1], axis=0),
                            in_=xrow[:, c % NX, :], in_offset=None).then_inc(s_scat[c % NX], 16)
                for i in range(NX):
                    pool.wait_ge(s_scat[i], 32 * (C // NX))

            @block.scalar
            def _(sc):
                nc.scalar.activation(tmp[:, :, :], logits[:, :, :], ACT.Exp, scale=-1.0).then_inc(r_exp, 1)

            @block.tensor
            def _(pe):
                pe.wait_ge(r_const, 2)
                pe.wait_ge(r_sel, 1)
                nc.tensor.matmul(psum[0][:, 0:NE * C], tri[:, :], sel[:, :, :].rearrange("p e c -> p (e c)"),
                                 start=True, stop=True)
                nc.tensor.matmul(psum[1][:, 0:NE * C], ones[:, :], sel[:, :, :].rearrange("p e c -> p (e c)"),
                                 start=True, stop=True).then_inc(r_cnt, 1)

            @block.vector
            def _(dve):
                own = Steps(dve, r_chain, 0, 37)
                ts, tt, stt = nc.vector.tensor_scalar, nc.vector.tensor_tensor, nc.vector.scalar_tensor_tensor
                dve.wait_ge(r_exp, 1)
                own.done(ts(tmp[:, :, :], tmp[:, :, :], 1.0, None, ALU.add))
                own.done(nc.vector.reciprocal(prob[:, :, :], tmp[:, :, :]))
                dve.wait_ge(r_const, 2)
                pf = prob[:, :, :].unsqueeze(2).to_broadcast([P, C, NE, NE])
                pe_ = prob[:, :, :].unsqueeze(3).to_broadcast([P, C, NE, NE])
                ca = cmp_a[:, :, :].rearrange("p (c e) f -> p c e f", e=NE)
                cbv = cmp_b[:, :, :].rearrange("p (c e) f -> p c e f", e=NE)
                own.done(tt(ca, pf, pe_, ALU.is_gt))
                own.done(tt(cbv, pf, pe_, ALU.is_equal))
                own.done(tt(cbv, cbv, earlier[:, :, :].unsqueeze(1).to_broadcast([P, C, NE, NE]), ALU.mult))
                own.done(tt(cmp_a[:, :, :], cmp_a[:, :, :], cmp_b[:, :, :], ALU.add))
                own.done(nc.vector.tensor_reduce(rank[:, :, :].rearrange("p c e -> p (c e)"), cmp_a[:, :, :], AX.X, ALU.add))
                for k in range(TOPK):
                    own.done(ts(pick[:, k, :, :], rank[:, :, :], float(k), None, ALU.is_equal))
                tt(sel[:, :, :].rearrange("p e c -> p c e"), pick[:, 0, :, :], pick[:, 1, :, :], ALU.add).then_inc(r_sel, 1)
                own.done(nc.vector.tensor_reduce(tmp2[:, :], prob[:, :, :], AX.X, ALU.add))
                own.done(nc.vector.reciprocal(tmp2[:, :], tmp2[:, :]))
                for k in range(TOPK):
                    own.done(tt(tmp[:, :, :], pick[:, k, :, :], prob[:, :, :], ALU.mult))
                    own.done(nc.vector.tensor_reduce(gates[:, k, :], tmp[:, :, :], AX.X, ALU.add))
                    own.done(tt(gates[:, k, :], gates[:, k, :], tmp2[:, :], ALU.mult))
                dve.wait_ge(r_cnt, 1)
                own.done(nc.vector.tensor_copy(total[:, :], psum[1][:, 0:NE * C]))
                own.done(nc.vector.tensor_tensor_scan(upto[:, :], zc[:, :], total[:, :], 0.0, ALU.add, ALU.add))
                own.done(tt(total[:, :], upto[:, :], total[:, :], ALU.subtract))
                own.done(tt(pos[:, :, :].rearrange("p e c -> p (e c)"), total[:, :], psum[0][:, 0:NE * C], ALU.add))
                tv = total[:, :].rearrange("p (e c) -> p e c", c=C)
                uv = upto[:, :].rearrange("p (e c) -> p e c", c=C)
                own.done(nc.vector.tensor_copy(first[:, :], tv[:, :, 0]))
                own.done(tt(count[:, :], uv[:, :, C - 1], first[:, :], ALU.subtract))
                own.done(tt(over[:, :, :], count[:, :].unsqueeze(2).to_broadcast([P, NE, NL]),
                            limits[:, :].unsqueeze(1).to_broadcast([P, NE, NL]), ALU.is_gt))
                own.done(nc.vector.tensor_reduce(ntile[:, :], over[:, :, :], AX.X, ALU.add))
                own.done(nc.vector.tensor_tensor_scan(ends[:, :], zc[:, 0:NE], ntile[:, :], 0.0, ALU.add, ALU.add))
                own.done(tt(delta[:, :], ends[:, :], ntile[:, :], ALU.subtract))
                own.done(stt(delta[:, :], delta[:, :], float(T), first[:, :], ALU.mult, ALU.subtract))
                own.done(tt(pos[:, :, :], pos[:, :, :], delta[:, :].unsqueeze(2).to_broadcast([P, NE, C]), ALU.add))
                for k in range(TOPK):
                    own.done(tt(tmp[:, :, :], pick[:, k, :, :], pos[:, :, :].rearrange("p e c -> p c e"), ALU.mult))
                    own.done(nc.vector.tensor_reduce(slotf[:, k, :], tmp[:, :, :], AX.X, ALU.add))
                own.done(tt(owner[:, :, :], numbers[:, :].unsqueeze(2).to_broadcast([P, NT, NE]),
                            ends[:, :].unsqueeze(1).to_broadcast([P, NT, NE]), ALU.is_ge))
                own.done(nc.vector.tensor_reduce(ownerf[:, :], owner[:, :, :], AX.X, ALU.add))
                own.done(ts(ownerf[:, :], ownerf[:, :], float(NE - 1), None, ALU.min))
                own.done(nc.vector.tensor_copy(tile_expert[:, :], ownerf[:, :]))
                nc.vector.tensor_copy(slots[:, :, :], slotf[:, :, :]).then_inc(r_slots, 1)
                own.end()

        stage_r.close()

        stage_c = ExitStack()
        Cc = lambda name, shape, dt=fp32: sb(stage_c, name, shape, dt)
        WN = KD * HID
        PIECE = 2 * WN // M
        NP1 = WN // PIECE
        gr_col = Cc("gr_col", [P, KD])
        raw = [Cc(f"raw_{i}", [P, 2 * WN]) for i in range(2)]
        whi = [Cc(f"whi_{i}", [P, 2 * WN], fp32r) for i in range(2)]
        wlo = [Cc(f"wlo_{i}", [P, 2 * WN], fp32r) for i in range(2)]
        b1 = [Cc(f"b1_{i}", [P, M]) for i in range(2)]
        b2 = [Cc(f"b2_{i}", [P, D]) for i in range(2)]
        xt = [Cc(f"xt_{i}", [P, TJ, D]) for i in range(2)]
        xT = Cc("xT", [P, KD, T])
        xhi = [Cc(f"xhi_{i}", [P, KD, T], fp32r) for i in range(2)]
        xlo = [Cc(f"xlo_{i}", [P, KD, T], fp32r) for i in range(2)]
        NHB = 4
        LAG = 2
        hraw = Cc("hraw", [P, NHB, T])
        hhi = Cc("hhi", [P, NHB, T], fp32r)
        hlo = Cc("hlo", [P, NHB, T], fp32r)
        yt = [Cc(f"yt_{i}", [P, TJ, D]) for i in range(2)]
        s_gr = sem("s_gr")
        t_x = [sem(f"t_x{i}") for i in range(2)]
        t_w1 = [sem(f"t_w1{i}") for i in range(2)]
        t_w2 = [sem(f"t_w2{i}") for i in range(2)]
        t_b1 = [sem(f"t_b1{i}") for i in range(2)]
        t_b2 = [sem(f"t_b2{i}") for i in range(2)]
        t_whi, t_wpool, t_wlo = sem("t_whi"), sem("t_wpool"), sem("t_wlo")
        t_tr, t_xraw, t_xhi, t_xlo = sem("t_tr"), sem("t_xraw"), sem("t_xhi"), sem("t_xlo")
        t_up, t_gelu, t_hhi, t_hlo, t_step = (sem(n) for n in ("t_up", "t_gelu", "t_hhi", "t_hlo", "t_step"))
        t_y = sem("t_y")
        t_out = [sem(f"t_out{i}") for i in range(2)]
        w1_v = W1_r.rearrange("e (k p) h -> e p k h", p=P)
        w2_v = W2_r.rearrange("e (m p) d -> e p m d", p=P)
        b1_v = b1_r.rearrange("e (m p) -> e p m", p=P)
        YB = TJ * D // 512
        NU = 4 // YB
        y_bank = [psum[NU + i * YB:NU + (i + 1) * YB] for i in range(2)]
        x_bank = psum[6:8]
        BY_POOL = (3, 7)

        def piece_of(m):
            return (m - LAG) % M, m >= LAG

        PAIRS = (NT - 1) // 2
        XSTEP = 3

        def tiles(body):
            for i in range(2):
                body(i, i, 0)
            yield
            for n in range(2 * PAIRS, NT):
                body(n, n % 2, n // 2)

        def run_tiles(engine, body):
            peeled = tiles(body)
            next(peeled)
            with engine.Fori(1, PAIRS) as r:
                for i in range(2):
                    body(2 * r + i, i, r)
            next(peeled, None)

        def is_(n, *values):
            return isinstance(n, int) and n in values

        with nc.Block() as block:
            @block.sync
            def _(sp):
                with nc.allow_non_contiguous_dma(reason="a column per half"):
                    sp.dma_start(gr_col[:, :], g_r.rearrange("(k p) -> p k", p=P)).then_inc(s_gr, 16)

                def store(n, i):
                    sp.dma_start(ys_v[bass.ds(n, 1)].rearrange("n p j d -> (n p) j d"), yt[i][:, :, :]).then_inc(t_out[i], 16)

                def body(n, i, r):
                    e = sp.value_load(tile_expert[0:1, bass.ds(n, 1)], min_val=0, max_val=NE - 1)
                    if not is_(n, 0, 1):
                        sp.wait_ge(t_wlo, M * (n - 1))
                        wait_apart(sp, t_tr, n - 1)
                    sp.dma_start(xt[i][:, :, :], xs_v[bass.ds(n, 1)].rearrange("n p j d -> (n p) j d")).then_inc(t_x[i], 16)
                    sp.dma_start(raw[i][:, 0:WN].rearrange("p (k h) -> p k h", k=KD),
                                 w1_v[bass.ds(e, 1)].rearrange("e p k h -> (e p) k h")).then_inc(t_w1[i], 16)
                    sp.dma_start(raw[i][:, WN:2 * WN].rearrange("p (m d) -> p m d", m=M),
                                 w2_v[bass.ds(e, 1)].rearrange("e p m d -> (e p) m d")).then_inc(t_w2[i], 16)
                    if not is_(n, 0, 1):
                        wait_apart(sp, t_y, n - 1)
                        store(n - 2, i)
                    with nc.allow_non_contiguous_dma(reason="a bias column per hidden chunk"):
                        sp.dma_start(b1[i][:, :], b1_v[bass.ds(e, 1)].rearrange("e p m -> (e p) m")).then_inc(t_b1[i], 16)
                    sp.dma_start(b2[i][:, :], b2_r[bass.ds(e, 1), :].to_broadcast([P, D])).then_inc(t_b2[i], 16)
                run_tiles(sp, body)
                for n in (NT - 2, NT - 1):
                    sp.wait_ge(t_y, n + 1)
                    store(n, n % 2)
                sp.wait_ge(t_out[0], 16 * ((NT + 1) // 2))
                sp.wait_ge(t_out[1], 16 * (NT // 2))

            @block.tensor
            def _(pe):
                def transposes(n, i, r):
                    pe.wait_ge(t_x[i], 16 * r + 16)
                    if not is_(n, 0):
                        pe.wait_ge(t_xraw, n)
                    for k in range(KD):
                        for j in range(TJ):
                            last = nc.tensor.transpose(x_bank[k][:, j * P:(j + 1) * P], xt[i][:, j, k * P:(k + 1) * P],
                                                       ident[:, :])
                    last.then_inc(t_tr, 1)

                def second(n, i, m):
                    pe.wait_ge(t_hhi, M * n + m + 1)
                    pe.wait_ge(t_hlo, M * n + m + 1)
                    if m % 2 == 0:
                        pe.wait_ge(t_wlo, M * n + NP1 + m // 2 + 1)
                    if m == 0 and not is_(n, 0, 1):
                        pe.wait_ge(t_y, n - 1)
                    h = m % NHB
                    wsl = slice(WN + m * D, WN + (m + 1) * D)
                    for j in range(TJ):
                        for t, (l, w) in enumerate(((hhi, whi), (hhi, wlo), (hlo, whi))):
                            last = nc.tensor.matmul(
                                y_bank[i][j * D // 512][:, (j * D) % 512:(j * D) % 512 + D], l[:, h, j * P:(j + 1) * P],
                                w[i][:, wsl], start=m == 0 and t == 0 and (j * D) % 512 == 0,
                                stop=m == M - 1 and t == 2, skip_group_check=True)
                    last.then_inc(t_step, 1)

                def body(n, i, r):
                    if is_(n, 0):
                        transposes(0, 0, 0)
                    pe.wait_ge(t_xhi, n + 1)
                    pe.wait_ge(t_xlo, n + 1)
                    pe.wait_ge(t_wlo, M * n + NP1)
                    for m in range(M):
                        if not (is_(n, 0) and m < NU):
                            pe.wait_ge(t_gelu, M * n + m - NU + 1)
                        ub = psum[m % NU]
                        for k in range(KD):
                            wsl = slice(k * HID + m * P, k * HID + (m + 1) * P)
                            for t, (w, x_) in enumerate(((whi, xhi), (whi, xlo), (wlo, xhi))):
                                last = nc.tensor.matmul(ub[:, 0:T], w[i][:, wsl], x_[i][:, k, :],
                                                        start=k == 0 and t == 0, stop=k == KD - 1 and t == 2)
                        last.then_inc(t_up, 1)
                        if m == XSTEP and not is_(n, NT - 1):
                            transposes(n + 1, 1 - i, r + i)
                        if m >= LAG:
                            second(n, i, m - LAG)
                        elif not is_(n, 0):
                            second(n - 1, 1 - i, M - LAG + m)
                    if is_(n, NT - 1):
                        for m in range(M - LAG, M):
                            second(n, i, m)
                run_tiles(pe, body)

            @block.scalar
            def _(sc):
                def weights(n, i, r, m):
                    if m == 0:
                        sc.wait_ge(t_w1[i], 16 * r + 16)
                    if m == NP1:
                        sc.wait_ge(t_w2[i], 16 * r + 16)
                    if not is_(n, 0, 1) and m == 0:
                        sc.wait_ge(t_step, M * (n - 1))
                    if m in BY_POOL:
                        return
                    psl = slice(m * PIECE, (m + 1) * PIECE)
                    nc.scalar.copy(whi[i][:, psl], raw[i][:, psl]).then_inc(t_whi, 1)

                def body(n, i, r):
                    if is_(n, 0):
                        for m in range(M - LAG):
                            weights(0, 0, 0, m)
                    sc.wait_ge(t_b1[i], 16 * r + 16)
                    for m in range(M):
                        sc.wait_ge(t_up, M * n + m + 1)
                        if not (is_(n, 0) and m < NHB):
                            sc.wait_ge(t_step, M * n + m - NHB + 1)
                        nc.scalar.activation(hraw[:, m % NHB, :], psum[m % NU][:, 0:T], ACT.Gelu,
                                             bias=b1[i][:, m:m + 1]).then_inc(t_gelu, 1)
                        sc.wait_ge(t_gelu, M * n + m + 1)
                        nc.scalar.copy(hhi[:, m % NHB, :], hraw[:, m % NHB, :]).then_inc(t_hhi, 1)
                        piece, ahead = piece_of(m)
                        if not ahead:
                            weights(n, i, r, piece)
                        elif not is_(n, NT - 1):
                            weights(n + 1, 1 - i, r + i, piece)
                run_tiles(sc, body)

            @block.vector
            def _(dve):
                dve.wait_ge(s_gr, 16)

                def weights(n, i, m):
                    if m in BY_POOL:
                        dve.wait_ge(t_wpool, len(BY_POOL) * n + BY_POOL.index(m) + 1)
                    else:
                        dve.wait_ge(t_whi, (M - len(BY_POOL)) * n + m + 1 - sum(q < m for q in BY_POOL))
                    psl = slice(m * PIECE, (m + 1) * PIECE)
                    nc.vector.tensor_tensor(wlo[i][:, psl], raw[i][:, psl], whi[i][:, psl].bitcast(fp32),
                                            ALU.subtract).then_inc(t_wlo, 1)

                def tokens(n, i):
                    dve.wait_ge(t_tr, n + 1)
                    if not is_(n, 0):
                        dve.wait_ge(t_xlo, n)
                    for k in range(KD):
                        last = nc.vector.tensor_scalar(xT[:, k, :], x_bank[k][:, 0:T], gr_col[:, k:k + 1], None, ALU.mult)
                    last.then_inc(t_xraw, 1)

                def tokens_low(n, i):
                    dve.wait_ge(t_xhi, n + 1)
                    nc.vector.tensor_tensor(xlo[i][:, :, :], xT[:, :, :], xhi[i][:, :, :].bitcast(fp32),
                                            ALU.subtract).then_inc(t_xlo, 1)

                def output(n, i, r):
                    dve.wait_ge(t_step, M * n + M)
                    dve.wait_ge(t_b2[i], 16 * r + 16)
                    if not is_(n, 0, 1):
                        dve.wait_ge(t_out[i], 16 * r)
                    for h in range(YB):
                        jj = TJ // YB
                        last = nc.vector.tensor_tensor(
                            yt[i][:, jj * h:jj * (h + 1), :], y_bank[i][h][:, :].rearrange("p (j d) -> p j d", d=D),
                            b2[i][:, :].unsqueeze(1).to_broadcast([P, jj, D]), ALU.add)
                    last.then_inc(t_y, 1)

                def body(n, i, r):
                    if is_(n, 0):
                        tokens(0, 0)
                        tokens_low(0, 0)
                        for m in range(M - LAG):
                            weights(0, 0, m)
                    for m in range(M):
                        dve.wait_ge(t_hhi, M * n + m + 1)
                        nc.vector.tensor_tensor(hlo[:, m % NHB, :], hraw[:, m % NHB, :],
                                                hhi[:, m % NHB, :].bitcast(fp32), ALU.subtract).then_inc(t_hlo, 1)
                        if m == LAG and not is_(n, 0):
                            output(n - 1, 1 - i, r - 1 + i)
                        piece, ahead = piece_of(m)
                        if not ahead:
                            weights(n, i, piece)
                        elif not is_(n, NT - 1):
                            if m == XSTEP:
                                tokens(n + 1, 1 - i)
                            if m == M - 2:
                                tokens_low(n + 1, 1 - i)
                            weights(n + 1, 1 - i, piece)
                    if is_(n, NT - 1):
                        output(n, i, r)
                run_tiles(dve, body)

            @block.gpsimd
            def _(pool):
                def weights(n, i, r, m):
                    pool.wait_ge(t_w1[i] if m < NP1 else t_w2[i], 16 * r + 16)
                    if not is_(n, 0, 1):
                        wait_apart(pool, t_step, M * (n - 1))
                    psl = slice(m * PIECE, (m + 1) * PIECE)
                    nc.gpsimd.tensor_copy(whi[i][:, psl], raw[i][:, psl]).then_inc(t_wpool, 1)

                def tokens(n, i):
                    if not is_(n, 0, 1):
                        pool.wait_ge(t_up, M * (n - 1))
                    wait_apart(pool, t_xraw, n + 1)
                    nc.gpsimd.tensor_copy(xhi[i][:, :, :], xT[:, :, :]).then_inc(t_xhi, 1)

                def body(n, i, r):
                    if is_(n, 0):
                        tokens(0, 0)
                        weights(0, 0, 0, BY_POOL[0])
                        weights(0, 0, 0, BY_POOL[1])
                    if not is_(n, NT - 1):
                        weights(n + 1, 1 - i, r + i, BY_POOL[0])
                        tokens(n + 1, 1 - i)
                        weights(n + 1, 1 - i, r + i, BY_POOL[1])
                run_tiles(pool, body)

        stage_c.close()

        stage_d = ExitStack()
        NB = 4
        bs = sb(stage_d, "bs", [P, NB, D])
        ya = sb(stage_d, "ya", [P, TOPK, NB, D])
        yo = sb(stage_d, "yo", [P, NB, D])
        d_base = [sem(f"d_base{i}") for i in range(NB)]
        d_y = [sem(f"d_y{i}") for i in range(NB)]
        d_sum, d_res = sem("d_sum"), sem("d_res")
        d_out = [sem(f"d_out{i}") for i in range(NB)]
        with nc.Block() as block:
            @block.sync
            def _(sp):
                for c in range(C):
                    if c >= NB:
                        sp.wait_ge(d_res, c - NB + 1)
                    sp.dma_start(bs[:, c % NB, :], base_c[c]).then_inc(d_base[c % NB], 16)

            @block.gpsimd
            def _(pool):
                for c in range(C):
                    if c >= NB:
                        pool.wait_ge(d_res, c - NB + 1)
                    for k in range(TOPK):
                        nc.gpsimd.indirect_dma_start(
                            out=ya[:, k, c % NB, :], out_offset=None, in_=ys_dram,
                            in_offset=bass.IndirectOffsetOnAxis(ap=slots[:, k, c:c + 1], axis=0)).then_inc(d_y[c % NB], 16)

            @block.vector
            def _(dve):
                for c in range(C):
                    i = c % NB
                    dve.wait_ge(d_base[i], 16 * (c // NB + 1))
                    dve.wait_ge(d_y[i], 32 * (c // NB + 1))
                    nc.vector.scalar_tensor_tensor(bs[:, i, :], ya[:, 0, i, :], gates[:, 0, c:c + 1], bs[:, i, :],
                                                   ALU.mult, ALU.add).then_inc(d_sum, 1)
                    dve.wait_ge(d_sum, c + 1)
                    if c >= NB:
                        dve.wait_ge(d_out[i], 16 * (c // NB))
                    nc.vector.scalar_tensor_tensor(yo[:, i, :], ya[:, 1, i, :], gates[:, 1, c:c + 1], bs[:, i, :],
                                                   ALU.mult, ALU.add).then_inc(d_res, 1)

            @block.scalar
            def _(sc):
                for c in range(C):
                    sc.wait_ge(d_res, c + 1)
                    sc.dma_start(out_c[c], yo[:, c % NB, :]).then_inc(d_out[c % NB], 16)
                for i in range(NB):
                    sc.wait_ge(d_out[i], 16 * (C // NB))
        stage_d.close()


_INS = ['x', 'ctx_1024', 'L0_xattn_igate_w', 'L0_xattn_igate_b', 'L0_xattn_fgate_w', 'L0_xattn_fgate_b',
        'L0_xattn_ln_scale', 'L0_ffn_g_shared', 'L0_ffn_W1_s', 'L0_ffn_b1_s', 'L0_ffn_W2_s', 'L0_ffn_b2_s',
        'L0_ffn_g_routed', 'L0_ffn_W1_r', 'L0_ffn_b1_r', 'L0_ffn_W2_r', 'L0_ffn_b2_r', 'L0_ffn_centroids']


def kernel(**inputs):
    import numpy as _np
    import concourse.bacc as _bacc
    from concourse import mybir as _mybir
    from concourse.bass_utils import run_bass_kernel_spmd as _run

    nc = _bacc.Bacc("TRN2", target_bir_lowering=False, num_devices=1)
    arrays, args = {}, []
    for name in _INS:
        a = _np.ascontiguousarray(inputs[name])
        arrays[f"in_{name}_dram"] = a
        args.append(nc.dram_tensor(f"in_{name}_dram", a.shape, _mybir.dt.from_np(a.dtype), kind="ExternalInput").ap())
    o = nc.dram_tensor("out_0_dram", inputs['x'].shape, _mybir.dt.float32, kind="ExternalOutput").ap()
    xattn_moe_kernel(nc, *args, o)
    r = _run(nc, [arrays], core_ids=[0])
    return r.results[0]["out_0_dram"]
```

```python
import concourse.bass as bass
from concourse import mybir
from contextlib import ExitStack

fp32 = mybir.dt.float32
fp32r = mybir.dt.float32r
bf16 = mybir.dt.bfloat16
i32 = mybir.dt.int32
ALU = mybir.AluOpType
ACT = mybir.ActivationFunctionType
AX = mybir.AxisListType

P = 128
LN_EPS = 1e-5
RMS_EPS = 1.1920928955078125e-07
NORM_EPS = 1e-6
MASKED = -1.0e30


def xattn_moe_kernel(nc, x, ctxt, ig_w, ig_b, fg_w, fg_b, ln_scale, g_s, W1_s, b1_s, W2_s, b2_s,
                     g_r, W1_r, b1_r, W2_r, b2_r, centroids, out):
    B, S, D = x.shape
    NH = ig_w.shape[0]
    DH = D // NH
    J = S // P
    KD = D // P
    HG = NH // KD
    NS, _, HID = W1_s.shape
    NE = W1_r.shape[0]
    M = HID // P
    VW = DH + 1
    HW = HG * VW
    PW = 3 * VW
    VPAD = 2
    C = B * J
    T = 256
    TJ = T // P
    TOPK = 2
    NT = (B * S * TOPK + NE * (T - 1)) // T
    NL = B * S // T
    SCALE = float(DH) ** -0.5
    IG, FG, TR = 0, 32, 64

    xs_dram = nc.dram_tensor("sorted_tokens", [NT * T, D], fp32).ap()
    ys_dram = nc.dram_tensor("sorted_outputs", [NT * T, D], fp32).ap()
    un_dram = nc.dram_tensor("normed_tokens", [B * S, D], fp32).ap()
    base_dram = nc.dram_tensor("residual_and_shared", [B * S, D], fp32).ap()

    x_v = x.rearrange("b (j p) d -> b p j d", p=P)
    c_v = ctxt.rearrange("b (j p) d -> b p j d", p=P)
    un_v = un_dram.rearrange("(b j p) d -> b p j d", p=P, j=J)
    base_v = base_dram.rearrange("(b j p) d -> b p j d", p=P, j=J)
    un_c = un_dram.rearrange("(c p) d -> c p d", p=P)
    base_c = base_dram.rearrange("(c p) d -> c p d", p=P)
    out_c = out.rearrange("b (j p) d -> (b j) p d", p=P)
    xs_v = xs_dram.rearrange("(n j p) d -> n p j d", p=P, j=TJ)
    ys_v = ys_dram.rearrange("(n j p) d -> n p j d", p=P, j=TJ)

    whole = ExitStack()
    with whole:
        def sb(stack, name, shape, dt=fp32):
            return stack.enter_context(nc.sbuf_tensor(name, shape, dt))

        def sem(name):
            return whole.enter_context(nc.semaphore(name))

        psum = [whole.enter_context(nc.psum_tensor(f"bank{i}", [P, 512], fp32)) for i in range(8)]

        ident = sb(whole, "ident", [P, P])
        logits = sb(whole, "logits", [P, C, NE])
        slots = sb(whole, "slots", [P, TOPK, C], i32)
        gates = sb(whole, "gates", [P, TOPK, C])
        tile_expert = sb(whole, "tile_expert", [P, NT], i32)
        zeros = sb(whole, "zeros", [P, D])

        stage_a = ExitStack()
        A = lambda name, shape, dt=fp32: sb(stage_a, name, shape, dt)
        identb = A("identb", [P, P], bf16)
        causal = A("causal", [P, P], bf16)
        gate_w = A("gate_w", [P, 2 * KD, 40])
        ig_bias = A("ig_bias", [NH, 1])
        fg_bias = A("fg_bias", [40, 1])
        negsel = A("negsel", [NH, NH])
        headmask = A("headmask", [P, HG])
        blockmask = A("blockmask", [P, HG, VW])
        lnsc = A("lnsc", [P, D])
        gs_col = A("gs_col", [P, KD])
        cent = A("cent", [P, KD, NE])
        WN = KD * HID
        whs = A("whs", [P, NS, 2 * WN], fp32r)
        wls = A("wls", [P, NS, 2 * WN], fp32r)
        b1s = A("b1s", [P, NS, M])
        b2s = A("b2s", [P, D])
        eps = A("eps", [P, 2])
        big = [A("big_0", [P, 2 * WN]), A("big_1", [P, 2 * WN])]
        exp_rhs = big[1][0:40, :].rearrange("p (j h s) -> p j h s", j=J, h=NH)
        ends_rhs = A("ends_rhs", [NH, J - 1, NH])
        exp_lhs = A("exp_lhs", [40, S])
        rows = A("rows", [72, S])
        frow = A("frow", [40, 3, S])
        cs = frow[0:NH, 0, :]
        zcol = A("zcol", [40, 1])
        vaug = A("vaug", [P, J, NH + VPAD, VW])
        xb = A("xb", [P, J, D])
        cb = A("cb", [P, J, D])
        qn = A("qn", [P, J, D])
        qcT = A("qcT", [P, 2 * KD, S])
        qmask = big[0][:, :].rearrange("p (g r s) -> p g r s", g=KD, r=HG)
        norm_x, norm_u = ((A(f"bn6_{n}", [P, J, 6]), A(f"mv_{n}", [P, J, 2]), A(f"nw_{n}", [P, 5, J])) for n in "xu")
        cols = A("cols", [P, 3 * P])
        earg = A("earg", [P, P])
        eexp = A("eexp", [P, P])
        NPAIR = J * (J - 1) // 2
        state = A("state", [P, KD, J - 1, HW])
        chunk = A("chunk", [P, 2 * NH * P])
        wv = chunk[:, 0:NPAIR * NH * VW].rearrange("p (n h e) -> p n h e", n=NPAIR, h=NH)
        decay = chunk[:, 0:NH * P].rearrange("p (h s) -> p h s", h=NH)
        ct = chunk[:, NH * P:2 * NH * P].rearrange("p (h s) -> p h s", h=NH)
        hn = A("hn", [P, J, NH, VW])
        rnorm = A("rnorm", [P, 3, J * NH])
        hh = A("hh", [P, J, D])
        x1 = A("x1", [P, J, D])
        un = A("un", [P, J, D])
        base = A("base", [P, J, D])
        xr = A("xr", [P, J, D])
        unT = A("unT", [P, KD, S])
        xhs = A("xhs", [P, KD, S], fp32r)
        xls = A("xls", [P, KD, S], fp32r)
        NHB = 3
        LAG = 2
        hraw = A("shared_hraw", [P, NHB, S])
        b2s2 = hraw[:, 0:NS * D // S, :].rearrange("p a s -> p (a s)").rearrange("p (e d) -> p e d", e=NS)
        hhi = A("shared_hhi", [P, NHB, S], fp32r)
        hlo = A("shared_hlo", [P, NHB, S], fp32r)

        gw_nat = qcT[0:40, 0:2, :].rearrange("p a s -> p (a s)")[:, 0:3 * D]

        s_load = sem("s_load")
        LOADS = 8 + 3 * NS
        s_whs, s_wls = sem("s_whs"), sem("s_wls")
        s_const = sem("s_const")
        s_cpre = sem("s_cpre")
        s_gwT = sem("s_gwT")

        with nc.Block() as block:
            @block.sync
            def _(sp):
                sp.wait_ge(s_cpre, 1)
                loads = [
                    (gw_nat[IG:IG + NH, :], ig_w), (gw_nat[FG:FG + NH, :], fg_w),
                    (ig_bias[:, :], ig_b.rearrange("(h o) -> h o", o=1)),
                    (fg_bias[FG:FG + NH, :], fg_b.rearrange("(h o) -> h o", o=1)),
                    (lnsc[:, :], ln_scale.rearrange("(o d) -> o d", o=1).to_broadcast([P, D])),
                    (cent[:, :, :], centroids.rearrange("(k p) e -> p k e", p=P)),
                    *[(big[e][:, 0:WN].rearrange("p (k h) -> p k h", k=KD),
                       W1_s[e].rearrange("(k p) h -> p k h", p=P)) for e in range(NS)],
                    *[(big[e][:, WN:2 * WN].rearrange("p (m d) -> p m d", m=M),
                       W2_s[e].rearrange("(m p) d -> p m d", p=P)) for e in range(NS)],
                    (b2s2[:, :, :], b2_s.rearrange("(o e) d -> o e d", o=1).to_broadcast([P, NS, D])),
                ]
                with nc.allow_non_contiguous_dma(reason="small transposed vectors"):
                    for n, (dst, src) in enumerate(loads):
                        sp.dma_start(dst, src).then_inc(s_load, 16)
                    sp.dma_start(gs_col[:, :], g_s.rearrange("(k p) -> p k", p=P)).then_inc(s_load, 16)
                    for e in range(NS):
                        sp.dma_start(b1s[:, e, :], b1_s[e, :].rearrange("(m p) -> p m", p=P)).then_inc(s_load, 16)
                assert len(loads) + 1 + NS == LOADS
                sp.wait_ge(s_load, 16 * (len(loads) + 1 + NS))

            @block.gpsimd
            def _(pool):
                nc.gpsimd.memset(ident[:, :], 0.0)
                nc.gpsimd.memset(negsel[:, :], 0.0)
                nc.gpsimd.memset(causal[:, :], 0.0)
                nc.gpsimd.memset(headmask[:, :], 1.0)
                nc.gpsimd.memset(exp_lhs[:, :], 0.0)
                nc.gpsimd.memset(rows[:, :], 0.0)
                nc.gpsimd.memset(blockmask[:, :, :], SCALE)
                nc.gpsimd.memset(vaug[:, :, :, :], 1.0)
                nc.gpsimd.memset(zcol[:, :], 0.0)
                nc.gpsimd.memset(eps[:, 0:1], LN_EPS)
                nc.gpsimd.memset(eps[:, 1:2], RMS_EPS).then_inc(s_const, 1)
                pool.wait_ge(s_const, 1)
                nc.gpsimd.affine_select(out=ident[:, :], in_=ident[:, :], compare_op=ALU.not_equal, fill=1.0,
                                        base=0, pattern=[[-1, P]], channel_multiplier=1)
                nc.gpsimd.affine_select(out=negsel[:, :], in_=negsel[:, :], compare_op=ALU.not_equal, fill=-1.0,
                                        base=0, pattern=[[-1, NH]], channel_multiplier=1)
                nc.gpsimd.affine_select(out=causal[:, :], in_=causal[:, :], compare_op=ALU.is_ge, fill=MASKED,
                                        base=0, pattern=[[1, P]], channel_multiplier=-1)
                nc.gpsimd.affine_select(out=headmask[:, :], in_=headmask[:, :], compare_op=ALU.is_ge, fill=0.0,
                                        base=0, pattern=[[-DH, HG]], channel_multiplier=1)
                nc.gpsimd.affine_select(out=blockmask[:, :, :], in_=blockmask[:, :, :], compare_op=ALU.is_ge,
                                        fill=0.0, base=0, pattern=[[-DH, HG], [0, VW]], channel_multiplier=1)
                nc.gpsimd.memset(exp_lhs[0:NH, :], 1.0).then_inc(s_const, 1)
                pool.wait_ge(s_const, 2)
                nc.gpsimd.affine_select(out=headmask[:, :], in_=headmask[:, :], compare_op=ALU.is_ge, fill=0.0,
                                        base=DH - 1, pattern=[[DH, HG]], channel_multiplier=-1)
                nc.gpsimd.affine_select(out=blockmask[:, :, :], in_=blockmask[:, :, :], compare_op=ALU.is_ge,
                                        fill=0.0, base=DH - 1, pattern=[[DH, HG], [0, VW]], channel_multiplier=-1)
                nc.gpsimd.tensor_copy(identb[:, :], ident[:, :])
                pool.wait_ge(s_wls, NS)
                nc.gpsimd.memset(exp_rhs, 0.0).then_inc(s_const, 1)
                pool.wait_ge(s_const, 3)
                for j in range(J):
                    last = nc.gpsimd.affine_select(out=exp_rhs[:, j, :, :], in_=exp_rhs[:, j, :, :],
                                                   compare_op=ALU.not_equal, fill=1.0, base=FG,
                                                   pattern=[[1, NH], [0, P]], channel_multiplier=-1)
                last.then_inc(s_const, 1)

            @block.vector
            def _(dve):
                nc.vector.memset(gw_nat, 0.0).then_inc(s_cpre, 1)
                nc.vector.memset(zeros[:, :], 0.0)
                dve.wait_ge(s_load, 16 * LOADS)
                nc.vector.tensor_tensor(b2s[:, :], b2s2[:, 0, :], b2s2[:, 1, :], ALU.add)
                dve.wait_ge(s_gwT, 1)
                pv = psum[0][:, 0:6 * 40].rearrange("p (n g) -> p n g", g=40)
                nc.vector.tensor_copy(gate_w[:, :, :], pv[:, 0:2 * KD, :]).then_inc(s_cpre, 1)
                dve.wait_ge(s_cpre, 2)
                nc.vector.tensor_tensor(gate_w[:, KD:2 * KD, :], gate_w[:, KD:2 * KD, :], pv[:, 2 * KD:3 * KD, :],
                                        ALU.add).then_inc(s_cpre, 1)
                for e in range(NS):
                    dve.wait_ge(s_whs, e + 1)
                    nc.vector.tensor_tensor(wls[:, e, :], big[e][:, :], whs[:, e, :].bitcast(fp32), ALU.subtract
                                            ).then_inc(s_wls, 1)

            @block.scalar
            def _(sc):
                sc.wait_ge(s_load, 16 * LOADS)
                for e in range(NS):
                    nc.scalar.copy(whs[:, e, :], big[e][:, :]).then_inc(s_whs, 1)

            @block.tensor
            def _(pe):
                pe.wait_ge(s_load, 16 * LOADS)
                pe.wait_ge(s_const, 2)
                for n in range(3 * KD):
                    last = nc.tensor.transpose(psum[0][:, n * 40:(n + 1) * 40], gw_nat[:, n * P:(n + 1) * P],
                                               ident[0:40, 0:40])
                last.then_inc(s_gwT, 1)

        s_x, s_c, s_xr = sem("s_x"), sem("s_c"), sem("s_xr")
        s_un_out, s_base_out = sem("s_un_out"), sem("s_base_out")
        chain_f, chain_t = sem("chain_f"), sem("chain_t")
        own_act = sem("own_act")
        moments_1, q_ready, tr_done, qcT_ready = (sem(n) for n in ("moments_1", "q_ready", "tr_done", "qcT_ready"))
        qmask_pool, qmask_dve = sem("qmask_pool"), sem("qmask_dve")
        gates_done, logsig_ready, rows_ready, lhs_ready = (sem(n) for n in ("gates_done", "logsig_ready", "rows_ready", "lhs_ready"))
        ends_ready, rhs_ready, cols_done, earg_ready, eexp_ready = (
            sem(n) for n in ("ends_ready", "rhs_ready", "cols_done", "earg_ready", "eexp_ready"))
        vaug_ready, wv_ready, state_done, state_ready = (sem(n) for n in ("vaug_ready", "wv_ready", "state_done", "state_ready"))
        exp_done, score_done, decay_ready, ct_ready = (sem(n) for n in ("exp_done", "score_done", "decay_ready", "ct_ready"))
        pv_done, hn_ready, x1_ready, un_ready = (sem(n) for n in ("pv_done", "hn_ready", "x1_ready", "un_ready"))
        unT_done, unT_ready, logit_done, logit_read = (sem(n) for n in ("unT_done", "unT_ready", "logit_done", "logit_read"))
        xraw_ready, xhs_ready, xls_ready = (sem(n) for n in ("xraw_ready", "xhs_ready", "xls_ready"))
        up_done, gelu_done, hhi_ready, hlo_ready, unit_done, fin_ready = (
            sem(n) for n in ("up_done", "gelu_done", "hhi_ready", "hlo_ready", "unit_done", "fin_ready"))
        passed = sem("passed")

        base_ready = sem("base_ready")

        OWN_FRONT, OWN_BACK = 20, 51
        U = NS * M
        NW = (J - 1) * (J - 1) * NH
        ORDER = "S 0 H 0 U 1 U F 1 U 2 U F 2 U P 3 U 3 U G T U R T U U T U R V U U C V U V U W U".split()
        assert ORDER.count("U") == U
        att_bank, up_bank, down_bank = psum[0:4], psum[4:6], psum[6:8]

        def wait_apart(engine, semaphore, value):
            engine.wait_ge(semaphore, value)
            engine.sem_inc(passed, 1)

        def side_by_side(parts, b, units=True, back=True, front=True):
            k, running = 0, {}
            running["back"] = parts["back"](b + 1) if back else None
            running["front"] = parts["front"](b + 2) if front else None
            for step in ORDER:
                if step == "U":
                    if units:
                        parts["unit"](b, k)
                        k += 1
                elif step == "H":
                    if units:
                        parts["hand_over"](b)
                elif step == "P":
                    if units:
                        parts["base"](b)
                elif step in "FGRC":
                    if front:
                        next(running["front"])
                elif back:
                    next(running["back"])
            if units:
                parts["finish"](b)

        def passes(engine, parts):
            for _ in parts["front"](0):
                pass
            side_by_side(parts, -1, units=False)
            with engine.Fori(0, B - 2) as b:
                side_by_side(parts, b)
            side_by_side(parts, B - 2, front=False)
            side_by_side(parts, B - 1, back=False, front=False)

        class Steps:
            def __init__(self, engine, semaphore, i, n):
                self.engine, self.semaphore, self.first, self.n, self.k = engine, semaphore, i * n, n, 0

            def done(self, instruction, alone=False):
                self.k += 1
                instruction.then_inc(self.semaphore, 1)
                (wait_apart if alone else type(self.engine).wait_ge)(self.engine, self.semaphore, self.first + self.k)

            def end(self):
                assert self.k == self.n, self.k

        with nc.Block() as block:
            @block.sync
            def _(sp):
                def load(dst, src, b, signal):
                    sp.dma_start(dst[:, :, :], src[bass.ds(b, 1)].rearrange("b p j d -> (b p) j d")).then_inc(signal, 16)

                def store_normed(b):
                    wait_apart(sp, un_ready, b + 1)
                    sp.dma_start(un_v[bass.ds(b, 1)].rearrange("b p j d -> (b p) j d"), un[:, :, :]).then_inc(s_un_out, 16)

                load(xb, x_v, 0, s_x)
                load(cb, c_v, 0, s_c)
                load(xr, x_v, 0, s_xr)
                with sp.Fori(1, B) as b:
                    wait_apart(sp, q_ready, b)
                    load(xb, x_v, b, s_x)
                    wait_apart(sp, state_done, b)
                    load(cb, c_v, b, s_c)
                    wait_apart(sp, x1_ready, b)
                    load(xr, x_v, b, s_xr)
                    store_normed(b - 1)
                store_normed(B - 1)
                sp.wait_ge(s_un_out, 16 * B)

            @block.gpsimd
            def _(pool):
                def rhs(j):
                    nc.gpsimd.tensor_tensor(
                        exp_rhs[0:NH, j, :, :], negsel[:, :].unsqueeze(2).to_broadcast([NH, NH, P]),
                        rows[0:NH, j * P:(j + 1) * P].unsqueeze(1).to_broadcast([NH, NH, P]), ALU.mult
                    ).then_inc(rhs_ready, 1)

                def batch(b):
                    pool.wait_ge(s_c, 16 * b + 16)
                    wait_apart(pool, qcT_ready, J * b + J)
                    nc.gpsimd.tensor_copy(vaug[:, :, 0:NH, 0:DH], cb[:, :, :].rearrange("p j (h e) -> p j h e", e=DH)
                                          ).then_inc(vaug_ready, 1)
                    for r in range(HG):
                        last = nc.gpsimd.tensor_scalar(qmask[:, 1, r, :], qcT[:, 1, :], headmask[:, r:r + 1], None,
                                                       ALU.mult)
                    last.then_inc(qmask_pool, 1)
                    pool.wait_ge(rows_ready, b + 1)
                    rhs(0)
                    pool.wait_ge(eexp_ready, b + 1)
                    pool.wait_ge(vaug_ready, b + 1)
                    n = 0
                    for j in range(J - 1):
                        for i in range(j + 1):
                            w = eexp[:, (i * (J - 1) + j) * NH:(i * (J - 1) + j + 1) * NH]
                            last = nc.gpsimd.tensor_tensor(wv[:, n, :, :], vaug[:, i, 0:NH, :],
                                                           w.unsqueeze(2).to_broadcast([P, NH, VW]), ALU.mult)
                            n += 1
                    last.then_inc(wv_ready, 1)
                    for j in range(1, J):
                        rhs(j)

                batch(0)
                with pool.Fori(1, B) as b:
                    batch(b)

            @block.scalar
            def _(sc):
                def front(b):
                    own = Steps(sc, own_act, b, 2)
                    yield
                    yield
                    for j in range(J):
                        sc.wait_ge(tr_done, J * b + j + 1)
                        nc.scalar.copy(qcT[:, :, j * P:(j + 1) * P],
                                       att_bank[j][:, :].rearrange("p (k s) -> p k s", s=P)).then_inc(qcT_ready, 1)
                    yield
                    sc.wait_ge(gates_done, b + 1)
                    f = frow[FG:FG + NH]
                    own.done(nc.scalar.activation(f[:, 0, :], att_bank[3][FG:FG + NH, :], ACT.Abs,
                                                  bias=fg_bias[FG:FG + NH, :]))
                    own.done(nc.scalar.activation(f[:, 1, :], f[:, 0, :], ACT.Exp, scale=-1.0))
                    nc.scalar.activation(f[:, 0, :], f[:, 1, :], ACT.Ln, bias=1.0).then_inc(logsig_ready, 1)
                    own.end()
                    yield
                    sc.wait_ge(rows_ready, b + 1)
                    nc.scalar.copy(exp_lhs[FG:FG + NH, :], rows[FG:FG + NH, :]).then_inc(lhs_ready, 1)
                    yield
                    sc.wait_ge(earg_ready, b + 1)
                    nc.scalar.activation(eexp[:, :], earg[:, :], ACT.Exp).then_inc(eexp_ready, 1)
                    yield

                def back(b):
                    yield
                    for j in range(J):
                        sc.wait_ge(exp_done, J * b + j + 1)
                        if j > 0:
                            sc.wait_ge(ct_ready, J * b + j)
                        for g in range(KD):
                            last = nc.scalar.activation(
                                decay[:, g * HG:(g + 1) * HG, :], att_bank[g][:, :].rearrange("p (h s) -> p h s", s=P),
                                ACT.Exp)
                        last.then_inc(decay_ready, 1)
                        yield
                        yield
                    for _ in range(6):
                        yield
                    sc.wait_ge(unT_done, b + 1)
                    for k in range(KD):
                        last = nc.scalar.copy(unT[:, k, :], att_bank[k][:, :])
                    last.then_inc(unT_ready, 1)
                    yield

                def unit(b, k):
                    sc.wait_ge(up_done, U * b + k + 1)
                    if k >= NHB:
                        sc.wait_ge(unit_done, U * b + k - NHB + 1)
                    nc.scalar.activation(hraw[:, k % NHB, :], up_bank[k % 2][:, :], ACT.Gelu,
                                         bias=b1s[:, k // M, k % M:k % M + 1]).then_inc(gelu_done, 1)
                    sc.wait_ge(gelu_done, U * b + k + 1)
                    nc.scalar.copy(hhi[:, k % NHB, :], hraw[:, k % NHB, :]).then_inc(hhi_ready, 1)

                def finish(b):
                    sc.wait_ge(fin_ready, b + 1)
                    sc.dma_start(base_v[bass.ds(b, 1)].rearrange("b p j d -> (b p) j d"), base[:, :, :]).then_inc(s_base_out, 16)

                def hand_over(b):
                    sc.wait_ge(xraw_ready, b + 1)
                    nc.scalar.copy(xhs[:, :, :], unT[:, :, :]).then_inc(xhs_ready, 1)

                passes(sc, {"front": front, "back": back, "unit": unit, "hand_over": hand_over,
                            "base": lambda b: None, "finish": finish})
                sc.wait_ge(s_base_out, 16 * B)

            @block.vector
            def _(dve):
                ts, tt, stt = nc.vector.tensor_scalar, nc.vector.tensor_tensor, nc.vector.scalar_tensor_tensor

                def moments(own, src, bn6, mv):
                    for j in range(J):
                        last = nc.vector.bn_stats(bn6[:, j, :], src[:, j, :])
                    own.done(last, alone=True)
                    for j in range(J):
                        last = nc.vector.bn_aggr(mv[:, j, :], bn6[:, j, :])
                    own.done(last)

                def rsqrt(own, v, e, nw):
                    own.done(ts(nw[:, 2, :], v, e, None, ALU.add))
                    own.done(ts(nw[:, 3, :].bitcast(i32), nw[:, 2, :].bitcast(i32), -0.5, float(0x5F3759DF),
                                ALU.mult, ALU.add))
                    for _ in range(3):
                        own.done(tt(nw[:, 0, :], nw[:, 3, :], nw[:, 3, :], ALU.mult))
                        own.done(stt(nw[:, 1, :], nw[:, 0, :], -0.5, nw[:, 2, :], ALU.mult, ALU.mult))
                        own.done(stt(nw[:, 3, :], nw[:, 1, :], 1.5, nw[:, 3, :], ALU.add, ALU.mult))

                def normed(dst, src, mv, nw):
                    for j in range(J):
                        last = ts(dst[:, j, :], src[:, j, :], mv[:, j, 0:1], nw[:, 3, j:j + 1],
                                  ALU.subtract, ALU.mult)
                    return last

                def front(b):
                    own = Steps(dve, chain_f, b, OWN_FRONT)
                    bn6, mv, nw = norm_x
                    dve.wait_ge(s_x, 16 * b + 16)
                    moments(own, xb, bn6, mv)
                    yield
                    rsqrt(own, mv[:, :, 1], LN_EPS, nw)
                    normed(qn, xb, mv, nw).then_inc(q_ready, 1)
                    yield
                    dve.wait_ge(qcT_ready, J * b + J)
                    for r in range(HG):
                        last = ts(qmask[:, 0, r, :], qcT[:, 0, :], headmask[:, r:r + 1], None, ALU.mult)
                    last.then_inc(qmask_dve, 1)
                    yield
                    dve.wait_ge(own_act, 2 * b + 1)
                    f = frow[FG:FG + NH]
                    own.done(ts(f[:, 2, :], att_bank[3][FG:FG + NH, :], fg_bias[FG:FG + NH, :], 0.0, ALU.add, ALU.min))
                    dve.wait_ge(logsig_ready, b + 1)
                    yield
                    own.done(tt(f[:, 2, :], f[:, 2, :], f[:, 0, :], ALU.subtract))
                    own.done(nc.vector.tensor_tensor_scan(cs[:, :], zcol[FG:FG + NH, :].to_broadcast([NH, S]),
                                                          f[:, 2, :], 0.0, ALU.add, ALU.add))
                    own.done(stt(rows[FG:FG + NH, :], att_bank[3][IG:IG + NH, :], ig_bias[:, :], cs[:, :],
                                 ALU.add, ALU.subtract))
                    own.done(nc.vector.tensor_tensor_scan(rows[0:NH, :], rows[FG:FG + NH, :], rows[FG:FG + NH, :],
                                                          -3.0e38, ALU.max, ALU.max))
                    tt(rows[TR:TR + NH, :], cs[:, :], rows[0:NH, :], ALU.add).then_inc(rows_ready, 1)
                    ends = rows[0:NH, :].rearrange("p (j s) -> p j s", s=P)[:, 0:J - 1, P - 1:P]
                    tt(ends_rhs[:, :, :], negsel[:, :].unsqueeze(1).to_broadcast([NH, J - 1, NH]),
                       ends.to_broadcast([NH, J - 1, NH]), ALU.mult).then_inc(ends_ready, 1)
                    yield
                    dve.wait_ge(cols_done, b + 1)
                    own.done(nc.vector.tensor_copy(cols[:, 0:J * 72 + (J - 1) * NH],
                                                   att_bank[3][:, 0:J * 72 + (J - 1) * NH]))
                    cv = cols[:, 0:J * 72].rearrange("p (j r) -> p j r", r=72)
                    nm = cols[:, J * 72:J * 72 + (J - 1) * NH].rearrange("p (j h) -> p j h", h=NH)
                    for i in range(J - 1):
                        ev = earg[:, i * (J - 1) * NH:(i + 1) * (J - 1) * NH].rearrange("p (j h) -> p j h", h=NH)
                        tt(ev, nm, cv[:, i:i + 1, FG:FG + NH].to_broadcast([P, J - 1, NH]), ALU.add)
                    rv = earg[:, NW:NW + (J - 1) * NH].rearrange("p (j h) -> p j h", h=NH)
                    stt(rv, cv[:, 1:J, 0:NH], -1.0, nm, ALU.mult, ALU.subtract)
                    mvw = earg[:, NW + (J - 1) * NH:NW + (2 * J - 1) * NH].rearrange("p (j h) -> p j h", h=NH)
                    own.done(ts(mvw, cv[:, :, TR:TR + NH], -1.0, None, ALU.mult))
                    ts(earg[:, 0:NW], earg[:, 0:NW], 0.0, None, ALU.min).then_inc(earg_ready, 1)
                    own.end()
                    yield

                def back(b):
                    own = Steps(dve, chain_t, b, OWN_BACK)
                    bn6, mv, nw = norm_u
                    dve.wait_ge(state_done, b + 1)
                    bm = blockmask[:, :, :].rearrange("p h e -> p (h e)").unsqueeze(1).to_broadcast([P, J - 1, HW])
                    for g in range(KD):
                        last = tt(state[:, g, :, :], att_bank[2 + g][:, 0:(J - 1) * HW].rearrange("p (j c) -> p j c", c=HW),
                                  bm, ALU.mult)
                    last.then_inc(state_ready, 1)
                    yield
                    for j in range(J):
                        dve.wait_ge(score_done, J * b + j + 1)
                        dve.wait_ge(decay_ready, J * b + j + 1)
                        for g in range(KD):
                            last = stt(ct[:, g * HG:(g + 1) * HG, :],
                                       att_bank[2 + g][:, :].rearrange("p (h s) -> p h s", s=P), SCALE,
                                       decay[:, g * HG:(g + 1) * HG, :], ALU.mult, ALU.mult)
                        last.then_inc(ct_ready, 1)
                        yield
                        dve.wait_ge(pv_done, J * b + j + 1)
                        if j > 0:
                            rr = eexp[:, NW + (j - 1) * NH:NW + j * NH].unsqueeze(2).to_broadcast([P, NH, VW])
                            own.done(tt(hn[:, j, :, :], att_bank[0][:, 0:NH * VW].rearrange("p (h e) -> p h e", e=VW),
                                        rr, ALU.mult))
                        for g in range(KD):
                            pvv = att_bank[2 + g][:, 0:HG * PW].rearrange("p (h e) -> p h e", e=PW)[:, :, 0:VW]
                            dst = hn[:, j, g * HG:(g + 1) * HG, :]
                            if j > 0:
                                last = tt(dst, dst, pvv, ALU.add)
                            else:
                                last = nc.vector.tensor_copy(dst, pvv)
                        last.then_inc(hn_ready, 1)
                        yield
                    dve.wait_ge(hn_ready, J * b + J)
                    hv = hn[:, :, :, :].rearrange("p j h e -> p (j h) e")
                    own.done(stt(rnorm[:, 0, :], hv[:, :, DH], -1.0, hv[:, :, DH], ALU.mult, ALU.max))
                    own.done(tt(rnorm[:, 1, :], rnorm[:, 0, :], eexp[:, NW + (J - 1) * NH:NW + (2 * J - 1) * NH], ALU.max))
                    own.done(ts(rnorm[:, 0, :], rnorm[:, 1, :], NORM_EPS, None, ALU.add))
                    own.done(nc.vector.reciprocal(rnorm[:, 2, :], rnorm[:, 0, :]))
                    own.done(tt(hh[:, :, :].rearrange("p j (h e) -> p (j h) e", e=DH), hv[:, :, 0:DH],
                                rnorm[:, 2, :].unsqueeze(2).to_broadcast([P, J * NH, DH]), ALU.mult))
                    yield
                    moments(own, hh, bn6, mv)
                    rsqrt(own, mv[:, :, 1], LN_EPS, nw)
                    yield
                    own.done(normed(x1, hh, mv, nw))
                    own.done(tt(x1[:, :, :], x1[:, :, :], lnsc[:, :].unsqueeze(1).to_broadcast([P, J, D]), ALU.mult))
                    dve.wait_ge(s_xr, 16 * b + 16)
                    tt(x1[:, :, :], x1[:, :, :], xr[:, :, :], ALU.add).then_inc(x1_ready, 1)
                    dve.wait_ge(x1_ready, b + 1)
                    yield
                    moments(own, x1, bn6, mv)
                    rsqrt(own, mv[:, :, 1], LN_EPS, nw)
                    yield
                    own.done(normed(hh, x1, mv, nw))
                    own.done(tt(nw[:, 0, :], nw[:, 3, :], nw[:, 3, :], ALU.mult))
                    own.done(tt(nw[:, 4, :], nw[:, 0, :], mv[:, :, 1], ALU.mult))
                    rsqrt(own, nw[:, 4, :], RMS_EPS, nw)
                    yield
                    if not (isinstance(b, int) and b == 0):
                        dve.wait_ge(s_un_out, 16 * b)
                    for j in range(J):
                        last = ts(un[:, j, :], hh[:, j, :], nw[:, 3, j:j + 1], None, ALU.mult)
                    last.then_inc(un_ready, 1)
                    own.done(nc.vector.reciprocal(nw[:, 4, :], nw[:, 3, :]))
                    yield
                    dve.wait_ge(logit_done, b + 1)
                    tt(logits[:, bass.ds(b * J, J), :], att_bank[2][:, 0:J * NE].rearrange("p (j e) -> p j e", e=NE),
                       nw[:, 4, :].unsqueeze(2).to_broadcast([P, J, NE]), ALU.mult).then_inc(logit_read, 1)
                    own.end()
                    yield

                def unit(b, k):
                    dve.wait_ge(hhi_ready, U * b + k + 1)
                    tt(hlo[:, k % NHB, :], hraw[:, k % NHB, :], hhi[:, k % NHB, :].bitcast(fp32), ALU.subtract
                       ).then_inc(hlo_ready, 1)

                def finish(b):
                    dve.wait_ge(unit_done, U * b + U)
                    for h in range(2):
                        last = tt(base[:, 2 * h:2 * h + 2, :], base[:, 2 * h:2 * h + 2, :],
                                  down_bank[h][:, :].rearrange("p (j d) -> p j d", d=D), ALU.add)
                    last.then_inc(fin_ready, 1)

                def hand_over(b):
                    dve.wait_ge(unT_ready, b + 1)
                    dve.wait_ge(logit_done, b + 1)
                    for k in range(KD):
                        last = ts(unT[:, k, :], unT[:, k, :], gs_col[:, k:k + 1], None, ALU.mult)
                    last.then_inc(xraw_ready, 1)
                    dve.wait_ge(xhs_ready, b + 1)
                    tt(xls[:, :, :], unT[:, :, :], xhs[:, :, :].bitcast(fp32), ALU.subtract).then_inc(xls_ready, 1)

                def to_add(b):
                    own = Steps(dve, base_ready, b, 2)
                    if not (isinstance(b, int) and b == 0):
                        dve.wait_ge(s_base_out, 16 * b)
                    own.done(tt(base[:, :, :], x1[:, :, :], hh[:, :, :], ALU.add))
                    own.done(tt(base[:, :, :], base[:, :, :], b2s[:, :].unsqueeze(1).to_broadcast([P, J, D]), ALU.add))

                passes(dve, {"front": front, "back": back, "unit": unit, "hand_over": hand_over,
                             "base": to_add, "finish": finish})

            @block.tensor
            def _(pe):
                mm, tr = nc.tensor.matmul, nc.tensor.transpose

                def front(b):
                    yield
                    yield
                    pe.wait_ge(q_ready, b + 1)
                    pe.wait_ge(s_c, 16 * b + 16)
                    if not (isinstance(b, int) and b == 0):
                        pe.wait_ge(hn_ready, J * b)
                    for j in range(J):
                        for k in range(KD):
                            tr(att_bank[j][:, k * P:(k + 1) * P], qn[:, j, k * P:(k + 1) * P], ident[:, :])
                        for k in range(KD):
                            last = tr(att_bank[j][:, (KD + k) * P:(KD + k + 1) * P], cb[:, j, k * P:(k + 1) * P], ident[:, :])
                        last.then_inc(tr_done, 1)
                    yield
                    pe.wait_ge(qcT_ready, J * b + J)
                    for k in range(2 * KD):
                        last = mm(att_bank[3][0:40, :], gate_w[:, k, :], qcT[:, k, :], start=k == 0, stop=k == 2 * KD - 1)
                    last.then_inc(gates_done, 1)
                    yield
                    yield
                    pe.wait_ge(rows_ready, b + 1)
                    for j in range(J):
                        tr(att_bank[3][:, j * 72:(j + 1) * 72], rows[:, j * P:(j + 1) * P], ident[0:72, 0:72])
                    pe.wait_ge(ends_ready, b + 1)
                    mm(att_bank[3][:, J * 72:J * 72 + (J - 1) * NH], exp_lhs[0:NH, 0:P],
                       ends_rhs[:, :, :].rearrange("p j h -> p (j h)"), start=True, stop=True).then_inc(cols_done, 1)
                    yield

                def back(b):
                    pe.wait_ge(wv_ready, b + 1)
                    if not (isinstance(b, int) and b == 0):
                        pe.wait_ge(logit_read, b)
                    for g in range(KD):
                        for j in range(J - 1):
                            for i in range(j + 1):
                                last = mm(att_bank[2 + g][:, j * HW:(j + 1) * HW], cb[:, i, g * P:(g + 1) * P],
                                          wv[:, j * (j + 1) // 2 + i, g * HG:(g + 1) * HG, :].rearrange("p h e -> p (h e)"),
                                          start=i == 0, stop=i == j)
                    last.then_inc(state_done, 1)
                    yield
                    pe.wait_ge(lhs_ready, b + 1)
                    for j in range(J):
                        cj = slice(j * P, (j + 1) * P)
                        pe.wait_ge(rhs_ready, J * b + j + 1)
                        if j > 0:
                            pe.wait_ge(hn_ready, J * b + j)
                        for g in range(KD):
                            mm(att_bank[g][:, :], identb[:, :], causal[:, :].unsqueeze(1).to_broadcast([P, HG, P]),
                               start=True, stop=False)
                            last = mm(att_bank[g][:, :], exp_lhs[:, cj],
                                      exp_rhs[:, j, g * HG:(g + 1) * HG, :].rearrange("p h s -> p (h s)"),
                                      start=False, stop=True)
                        last.then_inc(exp_done, 1)
                        if j == 0:
                            pe.wait_ge(state_ready, b + 1)
                            pe.wait_ge(qmask_dve, b + 1)
                            pe.wait_ge(qmask_pool, b + 1)
                        for g in range(KD):
                            last = mm(att_bank[2 + g][:, :], qcT[:, KD + g, cj], qmask[:, g, :, cj], start=True, stop=True)
                        last.then_inc(score_done, 1)
                        yield
                        pe.wait_ge(decay_ready, J * b + j + 1)
                        if j > 0:
                            for g in range(KD):
                                mm(att_bank[0][:, g * HW:(g + 1) * HW], qcT[:, g, cj], state[:, g, j - 1, :],
                                   start=True, stop=True)
                        pe.wait_ge(ct_ready, J * b + j + 1)
                        vflat = vaug[:, j, :, :].rearrange("p h e -> p (h e)")
                        for h in range(NH):
                            last = mm(att_bank[2 + h // HG][:, (h % HG) * PW:(h % HG + 1) * PW], ct[:, h, :],
                                      vflat[:, h * VW:h * VW + PW], start=True, stop=True)
                        last.then_inc(pv_done, 1)
                        yield
                    for _ in range(6):
                        yield
                    pe.wait_ge(un_ready, b + 1)
                    for k in range(KD):
                        for j in range(J):
                            last = tr(att_bank[k][:, j * P:(j + 1) * P], un[:, j, k * P:(k + 1) * P], ident[:, :])
                    last.then_inc(unT_done, 1)
                    pe.wait_ge(unT_ready, b + 1)
                    for j in range(J):
                        for k in range(KD):
                            last = mm(att_bank[2][:, j * NE:(j + 1) * NE], unT[:, k, j * P:(j + 1) * P], cent[:, k, :],
                                      start=k == 0, stop=k == KD - 1)
                    last.then_inc(logit_done, 1)
                    yield

                def second(b, k):
                    pe.wait_ge(hlo_ready, U * b + k + 1)
                    e, m = k // M, k % M
                    wsl = slice(WN + m * D, WN + (m + 1) * D)
                    for j in range(J):
                        for t, (h, w) in enumerate(((hhi, whs), (hhi, wls), (hlo, whs))):
                            last = mm(down_bank[j // 2][:, (j % 2) * D:(j % 2 + 1) * D],
                                      h[:, k % NHB, j * P:(j + 1) * P], w[:, e, wsl],
                                      start=k == 0 and t == 0 and j % 2 == 0, stop=k == U - 1 and t == 2,
                                      skip_group_check=True)
                    last.then_inc(unit_done, 1)

                def unit(b, k):
                    if k == 0:
                        pe.wait_ge(xls_ready, b + 1)
                    if k >= 2:
                        pe.wait_ge(gelu_done, U * b + k - 1)
                    e, m = k // M, k % M
                    for c in range(KD):
                        wsl = slice(c * HID + m * P, c * HID + (m + 1) * P)
                        for t, (w, x_) in enumerate(((whs, xhs), (whs, xls), (wls, xhs))):
                            last = mm(up_bank[k % 2][:, :], w[:, e, wsl], x_[:, c, :],
                                      start=c == 0 and t == 0, stop=c == KD - 1 and t == 2)
                    last.then_inc(up_done, 1)
                    if k >= LAG:
                        second(b, k - LAG)
                    if k == U - 1:
                        for late in range(U - LAG, U):
                            second(b, late)

                passes(pe, {"front": front, "back": back, "unit": unit, "hand_over": lambda b: None,
                            "base": lambda b: None, "finish": lambda b: None})

        stage_a.close()

        stage_r = ExitStack()
        R = lambda name, shape, dt=fp32: sb(stage_r, name, shape, dt)
        prob = R("prob", [P, C, NE])
        cmp_a = R("cmp_a", [P, C * NE, NE])
        cmp_b = R("cmp_b", [P, C * NE, NE])
        earlier = R("earlier", [P, NE, NE])
        rank = R("rank", [P, C, NE])
        pick = R("pick", [P, TOPK, C, NE])
        sel = R("sel", [P, NE, C])
        total = R("total", [P, NE * C])
        upto = R("upto", [P, NE * C])
        pos = R("pos", [P, NE, C])
        tri = R("tri", [P, P])
        ones = R("ones", [P, P])
        tmp = R("tmp", [P, C, NE])
        tmp2 = R("tmp2", [P, C])
        count = R("count", [P, NE])
        first = R("first", [P, NE])
        ntile = R("ntile", [P, NE])
        ends = R("ends", [P, NE])
        delta = R("delta", [P, NE])
        limits = R("limits", [P, NL])
        numbers = R("numbers", [P, NT])
        over = R("over", [P, NE, NL])
        owner = R("owner", [P, NT, NE])
        ownerf = R("ownerf", [P, NT])
        zc = R("zc", [P, NE * C])
        slotf = R("slotf", [P, TOPK, C])
        NX = 4
        xrow = R("xrow", [P, NX, D])

        s_fill = sem("s_fill")
        r_const = sem("r_const")
        r_exp = sem("r_exp")
        r_chain = sem("r_chain")
        r_sel = sem("r_sel")
        r_cnt = sem("r_cnt")
        r_slots = sem("r_slots")
        s_row = [sem(f"s_row{i}") for i in range(NX)]
        s_scat = [sem(f"s_scat{i}") for i in range(NX)]
        ROWS_FILL = NT * T // P

        with nc.Block() as block:
            @block.sync
            def _(sp):
                sp.dma_start(xs_dram.rearrange("(p n) d -> p n d", p=P),
                             zeros[:, :].unsqueeze(1).to_broadcast([P, ROWS_FILL, D])).then_inc(s_fill, 16)
                for c in range(C):
                    if c >= NX:
                        sp.wait_ge(s_scat[c % NX], 32 * (c // NX))
                    sp.dma_start(xrow[:, c % NX, :], un_c[c]).then_inc(s_row[c % NX], 16)

            @block.gpsimd
            def _(pool):
                nc.gpsimd.memset(ones[:, :], 1.0)
                nc.gpsimd.memset(tri[:, :], 1.0)
                nc.gpsimd.memset(zc[:, :], 0.0)
                nc.gpsimd.memset(earlier[:, :, :], 1.0)
                nc.gpsimd.iota(limits[:, :], pattern=[[T, NL]], base=0, channel_multiplier=0,
                               allow_small_or_imprecise_dtypes=True)
                nc.gpsimd.iota(numbers[:, :], pattern=[[1, NT]], base=0, channel_multiplier=0,
                               allow_small_or_imprecise_dtypes=True).then_inc(r_const, 1)
                pool.wait_ge(r_const, 1)
                nc.gpsimd.affine_select(out=tri[:, :], in_=tri[:, :], compare_op=ALU.is_gt, fill=0.0, base=0,
                                        pattern=[[1, P]], channel_multiplier=-1)
                nc.gpsimd.affine_select(out=earlier[:, :, :], in_=earlier[:, :, :], compare_op=ALU.is_gt, fill=0.0,
                                        base=0, pattern=[[1, NE], [-1, NE]], channel_multiplier=0).then_inc(r_const, 1)
                pool.wait_ge(r_slots, 1)
                pool.wait_ge(s_fill, 16)
                for c in range(C):
                    pool.wait_ge(s_row[c % NX], 16 * (c // NX + 1))
                    for k in range(TOPK):
                        nc.gpsimd.indirect_dma_start(
                            out=xs_dram, out_offset=bass.IndirectOffsetOnAxis(ap=slots[:, k, c:c + 1], axis=0),
                            in_=xrow[:, c % NX, :], in_offset=None).then_inc(s_scat[c % NX], 16)
                for i in range(NX):
                    pool.wait_ge(s_scat[i], 32 * (C // NX))

            @block.scalar
            def _(sc):
                nc.scalar.activation(tmp[:, :, :], logits[:, :, :], ACT.Exp, scale=-1.0).then_inc(r_exp, 1)

            @block.tensor
            def _(pe):
                pe.wait_ge(r_const, 2)
                pe.wait_ge(r_sel, 1)
                nc.tensor.matmul(psum[0][:, 0:NE * C], tri[:, :], sel[:, :, :].rearrange("p e c -> p (e c)"),
                                 start=True, stop=True)
                nc.tensor.matmul(psum[1][:, 0:NE * C], ones[:, :], sel[:, :, :].rearrange("p e c -> p (e c)"),
                                 start=True, stop=True).then_inc(r_cnt, 1)

            @block.vector
            def _(dve):
                own = Steps(dve, r_chain, 0, 37)
                ts, tt, stt = nc.vector.tensor_scalar, nc.vector.tensor_tensor, nc.vector.scalar_tensor_tensor
                dve.wait_ge(r_exp, 1)
                own.done(ts(tmp[:, :, :], tmp[:, :, :], 1.0, None, ALU.add))
                own.done(nc.vector.reciprocal(prob[:, :, :], tmp[:, :, :]))
                dve.wait_ge(r_const, 2)
                pf = prob[:, :, :].unsqueeze(2).to_broadcast([P, C, NE, NE])
                pe_ = prob[:, :, :].unsqueeze(3).to_broadcast([P, C, NE, NE])
                ca = cmp_a[:, :, :].rearrange("p (c e) f -> p c e f", e=NE)
                cbv = cmp_b[:, :, :].rearrange("p (c e) f -> p c e f", e=NE)
                own.done(tt(ca, pf, pe_, ALU.is_gt))
                own.done(tt(cbv, pf, pe_, ALU.is_equal))
                own.done(tt(cbv, cbv, earlier[:, :, :].unsqueeze(1).to_broadcast([P, C, NE, NE]), ALU.mult))
                own.done(tt(cmp_a[:, :, :], cmp_a[:, :, :], cmp_b[:, :, :], ALU.add))
                own.done(nc.vector.tensor_reduce(rank[:, :, :].rearrange("p c e -> p (c e)"), cmp_a[:, :, :], AX.X, ALU.add))
                for k in range(TOPK):
                    own.done(ts(pick[:, k, :, :], rank[:, :, :], float(k), None, ALU.is_equal))
                tt(sel[:, :, :].rearrange("p e c -> p c e"), pick[:, 0, :, :], pick[:, 1, :, :], ALU.add).then_inc(r_sel, 1)
                own.done(nc.vector.tensor_reduce(tmp2[:, :], prob[:, :, :], AX.X, ALU.add))
                own.done(nc.vector.reciprocal(tmp2[:, :], tmp2[:, :]))
                for k in range(TOPK):
                    own.done(tt(tmp[:, :, :], pick[:, k, :, :], prob[:, :, :], ALU.mult))
                    own.done(nc.vector.tensor_reduce(gates[:, k, :], tmp[:, :, :], AX.X, ALU.add))
                    own.done(tt(gates[:, k, :], gates[:, k, :], tmp2[:, :], ALU.mult))
                dve.wait_ge(r_cnt, 1)
                own.done(nc.vector.tensor_copy(total[:, :], psum[1][:, 0:NE * C]))
                own.done(nc.vector.tensor_tensor_scan(upto[:, :], zc[:, :], total[:, :], 0.0, ALU.add, ALU.add))
                own.done(tt(total[:, :], upto[:, :], total[:, :], ALU.subtract))
                own.done(tt(pos[:, :, :].rearrange("p e c -> p (e c)"), total[:, :], psum[0][:, 0:NE * C], ALU.add))
                tv = total[:, :].rearrange("p (e c) -> p e c", c=C)
                uv = upto[:, :].rearrange("p (e c) -> p e c", c=C)
                own.done(nc.vector.tensor_copy(first[:, :], tv[:, :, 0]))
                own.done(tt(count[:, :], uv[:, :, C - 1], first[:, :], ALU.subtract))
                own.done(tt(over[:, :, :], count[:, :].unsqueeze(2).to_broadcast([P, NE, NL]),
                            limits[:, :].unsqueeze(1).to_broadcast([P, NE, NL]), ALU.is_gt))
                own.done(nc.vector.tensor_reduce(ntile[:, :], over[:, :, :], AX.X, ALU.add))
                own.done(nc.vector.tensor_tensor_scan(ends[:, :], zc[:, 0:NE], ntile[:, :], 0.0, ALU.add, ALU.add))
                own.done(tt(delta[:, :], ends[:, :], ntile[:, :], ALU.subtract))
                own.done(stt(delta[:, :], delta[:, :], float(T), first[:, :], ALU.mult, ALU.subtract))
                own.done(tt(pos[:, :, :], pos[:, :, :], delta[:, :].unsqueeze(2).to_broadcast([P, NE, C]), ALU.add))
                for k in range(TOPK):
                    own.done(tt(tmp[:, :, :], pick[:, k, :, :], pos[:, :, :].rearrange("p e c -> p c e"), ALU.mult))
                    own.done(nc.vector.tensor_reduce(slotf[:, k, :], tmp[:, :, :], AX.X, ALU.add))
                own.done(tt(owner[:, :, :], numbers[:, :].unsqueeze(2).to_broadcast([P, NT, NE]),
                            ends[:, :].unsqueeze(1).to_broadcast([P, NT, NE]), ALU.is_ge))
                own.done(nc.vector.tensor_reduce(ownerf[:, :], owner[:, :, :], AX.X, ALU.add))
                own.done(ts(ownerf[:, :], ownerf[:, :], float(NE - 1), None, ALU.min))
                own.done(nc.vector.tensor_copy(tile_expert[:, :], ownerf[:, :]))
                nc.vector.tensor_copy(slots[:, :, :], slotf[:, :, :]).then_inc(r_slots, 1)
                own.end()

        stage_r.close()

        stage_c = ExitStack()
        NHB = 4
        Cc = lambda name, shape, dt=fp32: sb(stage_c, name, shape, dt)
        PIECE = 2 * WN // M
        NP1 = WN // PIECE
        gr_col = Cc("gr_col", [P, KD])
        raw = [Cc(f"raw_{i}", [P, 2 * WN]) for i in range(2)]
        whi = [Cc(f"whi_{i}", [P, 2 * WN], fp32r) for i in range(2)]
        wlo = [Cc(f"wlo_{i}", [P, 2 * WN], fp32r) for i in range(2)]
        b1 = [Cc(f"b1_{i}", [P, M]) for i in range(2)]
        b2 = [Cc(f"b2_{i}", [P, D]) for i in range(2)]
        xt = [Cc(f"xt_{i}", [P, TJ, D]) for i in range(2)]
        xT = Cc("xT", [P, KD, T])
        xhi = [Cc(f"xhi_{i}", [P, KD, T], fp32r) for i in range(2)]
        xlo = [Cc(f"xlo_{i}", [P, KD, T], fp32r) for i in range(2)]
        hraw = Cc("hraw", [P, NHB, T])
        hhi = Cc("hhi", [P, NHB, T], fp32r)
        hlo = Cc("hlo", [P, NHB, T], fp32r)
        yt = [Cc(f"yt_{i}", [P, TJ, D]) for i in range(2)]
        s_gr = sem("s_gr")
        t_x = [sem(f"t_x{i}") for i in range(2)]
        t_w1 = [sem(f"t_w1{i}") for i in range(2)]
        t_w2 = [sem(f"t_w2{i}") for i in range(2)]
        t_b1 = [sem(f"t_b1{i}") for i in range(2)]
        t_b2 = [sem(f"t_b2{i}") for i in range(2)]
        t_whi, t_wpool, t_wlo = sem("t_whi"), sem("t_wpool"), sem("t_wlo")
        t_tr, t_xraw, t_xhi, t_xlo = sem("t_tr"), sem("t_xraw"), sem("t_xhi"), sem("t_xlo")
        t_up, t_gelu, t_hhi, t_hlo, t_step = (sem(n) for n in ("t_up", "t_gelu", "t_hhi", "t_hlo", "t_step"))
        t_y = sem("t_y")
        t_out = [sem(f"t_out{i}") for i in range(2)]
        w1_v = W1_r.rearrange("e (k p) h -> e p k h", p=P)
        w2_v = W2_r.rearrange("e (m p) d -> e p m d", p=P)
        b1_v = b1_r.rearrange("e (m p) -> e p m", p=P)
        YB = TJ * D // 512
        NU = 4 // YB
        y_bank = [psum[NU + i * YB:NU + (i + 1) * YB] for i in range(2)]
        x_bank = psum[6:8]
        BY_POOL = (3, 7)

        def piece_of(m):
            return (m - LAG) % M, m >= LAG

        PAIRS = (NT - 1) // 2
        XSTEP = 3

        def tiles(body):
            for i in range(2):
                body(i, i, 0)
            yield
            for n in range(2 * PAIRS, NT):
                body(n, n % 2, n // 2)

        def run_tiles(engine, body):
            peeled = tiles(body)
            next(peeled)
            with engine.Fori(1, PAIRS) as r:
                for i in range(2):
                    body(2 * r + i, i, r)
            next(peeled, None)

        def is_(n, *values):
            return isinstance(n, int) and n in values

        with nc.Block() as block:
            @block.sync
            def _(sp):
                with nc.allow_non_contiguous_dma(reason="a column per half"):
                    sp.dma_start(gr_col[:, :], g_r.rearrange("(k p) -> p k", p=P)).then_inc(s_gr, 16)

                def store(n, i):
                    sp.dma_start(ys_v[bass.ds(n, 1)].rearrange("n p j d -> (n p) j d"), yt[i][:, :, :]).then_inc(t_out[i], 16)

                def body(n, i, r):
                    e = sp.value_load(tile_expert[0:1, bass.ds(n, 1)], min_val=0, max_val=NE - 1)
                    if not is_(n, 0, 1):
                        sp.wait_ge(t_wlo, M * (n - 1))
                        wait_apart(sp, t_tr, n - 1)
                    sp.dma_start(xt[i][:, :, :], xs_v[bass.ds(n, 1)].rearrange("n p j d -> (n p) j d")).then_inc(t_x[i], 16)
                    sp.dma_start(raw[i][:, 0:WN].rearrange("p (k h) -> p k h", k=KD),
                                 w1_v[bass.ds(e, 1)].rearrange("e p k h -> (e p) k h")).then_inc(t_w1[i], 16)
                    sp.dma_start(raw[i][:, WN:2 * WN].rearrange("p (m d) -> p m d", m=M),
                                 w2_v[bass.ds(e, 1)].rearrange("e p m d -> (e p) m d")).then_inc(t_w2[i], 16)
                    if not is_(n, 0, 1):
                        wait_apart(sp, t_y, n - 1)
                        store(n - 2, i)
                    with nc.allow_non_contiguous_dma(reason="a bias column per hidden chunk"):
                        sp.dma_start(b1[i][:, :], b1_v[bass.ds(e, 1)].rearrange("e p m -> (e p) m")).then_inc(t_b1[i], 16)
                    sp.dma_start(b2[i][:, :], b2_r[bass.ds(e, 1), :].to_broadcast([P, D])).then_inc(t_b2[i], 16)
                run_tiles(sp, body)
                for n in (NT - 2, NT - 1):
                    sp.wait_ge(t_y, n + 1)
                    store(n, n % 2)
                sp.wait_ge(t_out[0], 16 * ((NT + 1) // 2))
                sp.wait_ge(t_out[1], 16 * (NT // 2))

            @block.tensor
            def _(pe):
                def transposes(n, i, r):
                    pe.wait_ge(t_x[i], 16 * r + 16)
                    if not is_(n, 0):
                        pe.wait_ge(t_xraw, n)
                    for k in range(KD):
                        for j in range(TJ):
                            last = nc.tensor.transpose(x_bank[k][:, j * P:(j + 1) * P], xt[i][:, j, k * P:(k + 1) * P],
                                                       ident[:, :])
                    last.then_inc(t_tr, 1)

                def second(n, i, m):
                    pe.wait_ge(t_hhi, M * n + m + 1)
                    pe.wait_ge(t_hlo, M * n + m + 1)
                    if m % 2 == 0:
                        pe.wait_ge(t_wlo, M * n + NP1 + m // 2 + 1)
                    if m == 0 and not is_(n, 0, 1):
                        pe.wait_ge(t_y, n - 1)
                    h = m % NHB
                    wsl = slice(WN + m * D, WN + (m + 1) * D)
                    for j in range(TJ):
                        for t, (l, w) in enumerate(((hhi, whi), (hhi, wlo), (hlo, whi))):
                            last = nc.tensor.matmul(
                                y_bank[i][j * D // 512][:, (j * D) % 512:(j * D) % 512 + D], l[:, h, j * P:(j + 1) * P],
                                w[i][:, wsl], start=m == 0 and t == 0 and (j * D) % 512 == 0,
                                stop=m == M - 1 and t == 2, skip_group_check=True)
                    last.then_inc(t_step, 1)

                def body(n, i, r):
                    if is_(n, 0):
                        transposes(0, 0, 0)
                    pe.wait_ge(t_xhi, n + 1)
                    pe.wait_ge(t_xlo, n + 1)
                    pe.wait_ge(t_wlo, M * n + NP1)
                    for m in range(M):
                        if not (is_(n, 0) and m < NU):
                            pe.wait_ge(t_gelu, M * n + m - NU + 1)
                        ub = psum[m % NU]
                        for k in range(KD):
                            wsl = slice(k * HID + m * P, k * HID + (m + 1) * P)
                            for t, (w, x_) in enumerate(((whi, xhi), (whi, xlo), (wlo, xhi))):
                                last = nc.tensor.matmul(ub[:, 0:T], w[i][:, wsl], x_[i][:, k, :],
                                                        start=k == 0 and t == 0, stop=k == KD - 1 and t == 2)
                        last.then_inc(t_up, 1)
                        if m == XSTEP and not is_(n, NT - 1):
                            transposes(n + 1, 1 - i, r + i)
                        if m >= LAG:
                            second(n, i, m - LAG)
                        elif not is_(n, 0):
                            second(n - 1, 1 - i, M - LAG + m)
                    if is_(n, NT - 1):
                        for m in range(M - LAG, M):
                            second(n, i, m)
                run_tiles(pe, body)

            @block.scalar
            def _(sc):
                def weights(n, i, r, m):
                    if m == 0:
                        sc.wait_ge(t_w1[i], 16 * r + 16)
                    if m == NP1:
                        sc.wait_ge(t_w2[i], 16 * r + 16)
                    if not is_(n, 0, 1) and m == 0:
                        sc.wait_ge(t_step, M * (n - 1))
                    if m in BY_POOL:
                        return
                    psl = slice(m * PIECE, (m + 1) * PIECE)
                    nc.scalar.copy(whi[i][:, psl], raw[i][:, psl]).then_inc(t_whi, 1)

                def body(n, i, r):
                    if is_(n, 0):
                        for m in range(M - LAG):
                            weights(0, 0, 0, m)
                    sc.wait_ge(t_b1[i], 16 * r + 16)
                    for m in range(M):
                        sc.wait_ge(t_up, M * n + m + 1)
                        if not (is_(n, 0) and m < NHB):
                            sc.wait_ge(t_step, M * n + m - NHB + 1)
                        nc.scalar.activation(hraw[:, m % NHB, :], psum[m % NU][:, 0:T], ACT.Gelu,
                                             bias=b1[i][:, m:m + 1]).then_inc(t_gelu, 1)
                        sc.wait_ge(t_gelu, M * n + m + 1)
                        nc.scalar.copy(hhi[:, m % NHB, :], hraw[:, m % NHB, :]).then_inc(t_hhi, 1)
                        piece, ahead = piece_of(m)
                        if not ahead:
                            weights(n, i, r, piece)
                        elif not is_(n, NT - 1):
                            weights(n + 1, 1 - i, r + i, piece)
                run_tiles(sc, body)

            @block.vector
            def _(dve):
                dve.wait_ge(s_gr, 16)

                def weights(n, i, m):
                    if m in BY_POOL:
                        dve.wait_ge(t_wpool, len(BY_POOL) * n + BY_POOL.index(m) + 1)
                    else:
                        dve.wait_ge(t_whi, (M - len(BY_POOL)) * n + m + 1 - sum(q < m for q in BY_POOL))
                    psl = slice(m * PIECE, (m + 1) * PIECE)
                    nc.vector.tensor_tensor(wlo[i][:, psl], raw[i][:, psl], whi[i][:, psl].bitcast(fp32),
                                            ALU.subtract).then_inc(t_wlo, 1)

                def tokens(n, i):
                    dve.wait_ge(t_tr, n + 1)
                    if not is_(n, 0):
                        dve.wait_ge(t_xlo, n)
                    for k in range(KD):
                        last = nc.vector.tensor_scalar(xT[:, k, :], x_bank[k][:, 0:T], gr_col[:, k:k + 1], None, ALU.mult)
                    last.then_inc(t_xraw, 1)

                def tokens_low(n, i):
                    dve.wait_ge(t_xhi, n + 1)
                    nc.vector.tensor_tensor(xlo[i][:, :, :], xT[:, :, :], xhi[i][:, :, :].bitcast(fp32),
                                            ALU.subtract).then_inc(t_xlo, 1)

                def output(n, i, r):
                    dve.wait_ge(t_step, M * n + M)
                    dve.wait_ge(t_b2[i], 16 * r + 16)
                    if not is_(n, 0, 1):
                        dve.wait_ge(t_out[i], 16 * r)
                    for h in range(YB):
                        jj = TJ // YB
                        last = nc.vector.tensor_tensor(
                            yt[i][:, jj * h:jj * (h + 1), :], y_bank[i][h][:, :].rearrange("p (j d) -> p j d", d=D),
                            b2[i][:, :].unsqueeze(1).to_broadcast([P, jj, D]), ALU.add)
                    last.then_inc(t_y, 1)

                def body(n, i, r):
                    if is_(n, 0):
                        tokens(0, 0)
                        tokens_low(0, 0)
                        for m in range(M - LAG):
                            weights(0, 0, m)
                    for m in range(M):
                        dve.wait_ge(t_hhi, M * n + m + 1)
                        nc.vector.tensor_tensor(hlo[:, m % NHB, :], hraw[:, m % NHB, :],
                                                hhi[:, m % NHB, :].bitcast(fp32), ALU.subtract).then_inc(t_hlo, 1)
                        if m == LAG and not is_(n, 0):
                            output(n - 1, 1 - i, r - 1 + i)
                        piece, ahead = piece_of(m)
                        if not ahead:
                            weights(n, i, piece)
                        elif not is_(n, NT - 1):
                            if m == XSTEP:
                                tokens(n + 1, 1 - i)
                            if m == M - 2:
                                tokens_low(n + 1, 1 - i)
                            weights(n + 1, 1 - i, piece)
                    if is_(n, NT - 1):
                        output(n, i, r)
                run_tiles(dve, body)

            @block.gpsimd
            def _(pool):
                def weights(n, i, r, m):
                    pool.wait_ge(t_w1[i] if m < NP1 else t_w2[i], 16 * r + 16)
                    if not is_(n, 0, 1):
                        wait_apart(pool, t_step, M * (n - 1))
                    psl = slice(m * PIECE, (m + 1) * PIECE)
                    nc.gpsimd.tensor_copy(whi[i][:, psl], raw[i][:, psl]).then_inc(t_wpool, 1)

                def tokens(n, i):
                    if not is_(n, 0, 1):
                        pool.wait_ge(t_up, M * (n - 1))
                    wait_apart(pool, t_xraw, n + 1)
                    nc.gpsimd.tensor_copy(xhi[i][:, :, :], xT[:, :, :]).then_inc(t_xhi, 1)

                def body(n, i, r):
                    if is_(n, 0):
                        tokens(0, 0)
                        weights(0, 0, 0, BY_POOL[0])
                        weights(0, 0, 0, BY_POOL[1])
                    if not is_(n, NT - 1):
                        weights(n + 1, 1 - i, r + i, BY_POOL[0])
                        tokens(n + 1, 1 - i)
                        weights(n + 1, 1 - i, r + i, BY_POOL[1])
                run_tiles(pool, body)

        stage_c.close()

        stage_d = ExitStack()
        NB = 4
        bs = sb(stage_d, "bs", [P, NB, D])
        ya = sb(stage_d, "ya", [P, TOPK, NB, D])
        yo = sb(stage_d, "yo", [P, NB, D])
        d_base = [sem(f"d_base{i}") for i in range(NB)]
        d_y = [sem(f"d_y{i}") for i in range(NB)]
        d_sum, d_res = sem("d_sum"), sem("d_res")
        d_out = [sem(f"d_out{i}") for i in range(NB)]
        with nc.Block() as block:
            @block.sync
            def _(sp):
                for c in range(C):
                    if c >= NB:
                        sp.wait_ge(d_res, c - NB + 1)
                    sp.dma_start(bs[:, c % NB, :], base_c[c]).then_inc(d_base[c % NB], 16)

            @block.gpsimd
            def _(pool):
                for c in range(C):
                    if c >= NB:
                        pool.wait_ge(d_res, c - NB + 1)
                    for k in range(TOPK):
                        nc.gpsimd.indirect_dma_start(
                            out=ya[:, k, c % NB, :], out_offset=None, in_=ys_dram,
                            in_offset=bass.IndirectOffsetOnAxis(ap=slots[:, k, c:c + 1], axis=0)).then_inc(d_y[c % NB], 16)

            @block.vector
            def _(dve):
                for c in range(C):
                    i = c % NB
                    dve.wait_ge(d_base[i], 16 * (c // NB + 1))
                    dve.wait_ge(d_y[i], 32 * (c // NB + 1))
                    nc.vector.scalar_tensor_tensor(bs[:, i, :], ya[:, 0, i, :], gates[:, 0, c:c + 1], bs[:, i, :],
                                                   ALU.mult, ALU.add).then_inc(d_sum, 1)
                    dve.wait_ge(d_sum, c + 1)
                    if c >= NB:
                        dve.wait_ge(d_out[i], 16 * (c // NB))
                    nc.vector.scalar_tensor_tensor(yo[:, i, :], ya[:, 1, i, :], gates[:, 1, c:c + 1], bs[:, i, :],
                                                   ALU.mult, ALU.add).then_inc(d_res, 1)

            @block.scalar
            def _(sc):
                for c in range(C):
                    sc.wait_ge(d_res, c + 1)
                    sc.dma_start(out_c[c], yo[:, c % NB, :]).then_inc(d_out[c % NB], 16)
                for i in range(NB):
                    sc.wait_ge(d_out[i], 16 * (C // NB))
        stage_d.close()


_INS = ['x', 'ctx_1024', 'L0_xattn_igate_w', 'L0_xattn_igate_b', 'L0_xattn_fgate_w', 'L0_xattn_fgate_b',
        'L0_xattn_ln_scale', 'L0_ffn_g_shared', 'L0_ffn_W1_s', 'L0_ffn_b1_s', 'L0_ffn_W2_s', 'L0_ffn_b2_s',
        'L0_ffn_g_routed', 'L0_ffn_W1_r', 'L0_ffn_b1_r', 'L0_ffn_W2_r', 'L0_ffn_b2_r', 'L0_ffn_centroids']


def kernel(**inputs):
    import numpy as _np
    import concourse.bacc as _bacc
    from concourse import mybir as _mybir
    from concourse.bass_utils import run_bass_kernel_spmd as _run

    nc = _bacc.Bacc("TRN2", target_bir_lowering=False, num_devices=1)
    arrays, args = {}, []
    for name in _INS:
        a = _np.ascontiguousarray(inputs[name])
        arrays[f"in_{name}_dram"] = a
        args.append(nc.dram_tensor(f"in_{name}_dram", a.shape, _mybir.dt.from_np(a.dtype), kind="ExternalInput").ap())
    o = nc.dram_tensor("out_0_dram", inputs['x'].shape, _mybir.dt.float32, kind="ExternalOutput").ap()
    xattn_moe_kernel(nc, *args, o)
    r = _run(nc, [arrays], core_ids=[0])
    return r.results[0]["out_0_dram"]
```
